# Optimizing a Trainium2 kernel written in Bass

```python
import numpy as np
import jax
import jax.numpy as jnp

def _softmax(x, axis=-1):
    return jax.nn.softmax(x, axis=axis)

def _gelu(x):
    return jax.nn.gelu(x, approximate=True)

def _silu(x):
    return jax.nn.silu(x)

def _sigmoid(x):
    return jax.nn.sigmoid(x)

def _layernorm(x, axis=-1, eps=1e-05):
    m = jnp.mean(x, axis=axis, keepdims=True)
    v = jnp.var(x, axis=axis, keepdims=True)
    return (x - m) / jnp.sqrt(v + eps)

def _scatter_add(tgt, idx, src, axis=0):
    return tgt.at[idx].add(src)

def _segment_sum(src, seg, n):
    return jax.ops.segment_sum(src, seg, n)
kernel_name = 'mk_gps_d2_gnn_r32_8f9775'

def setup_inputs(seed: int=0):
    np.random.seed(seed)
    _w = jnp.asarray

    def _rec_inputs():
        import jax
        import jax.numpy as jnp
        _gk = jax.random.key(seed)
        x = -0.0003019 + 1 * jax.random.normal(jax.random.fold_in(_gk, 1), (1250, 512), jnp.float32)
        _s = jax.random.randint(jax.random.fold_in(_gk, 2), (10000,), 0, 1250, jnp.int32)
        _d = jax.random.randint(jax.random.fold_in(_gk, 3), (10000,), 0, 1250, jnp.int32)
        _loop = jnp.arange(1250, dtype=jnp.int32)
        src = jnp.concatenate([_s, _d, _loop])
        dst = jnp.concatenate([_d, _s, _loop])
        _o = jnp.argsort(dst, stable=True)
        src = src[_o]
        dst = dst[_o]
        edge_attr_128 = -0.00010739 + 0.99994 * jax.random.normal(jax.random.fold_in(_gk, 11), (21250, 128), jnp.float32)
        return (x, src, dst, edge_attr_128)
    x, src, dst, edge_attr_128 = _rec_inputs()

    def _L0_gnn_setup():
        import jax, jax.numpy as jnp
        import numpy as np
        N = 1250
        IN_DIM = 512
        OUT_DIM = 512
        E_RAND = 20000
        SLOPE = 0.1
        key = jax.random.key(seed)
        k1, k2, k3, k4, k5 = jax.random.split(key, 5)
        features = jax.random.normal(k1, (N, IN_DIM), dtype=jnp.float32)
        src = jax.random.randint(k2, (E_RAND,), 0, N)
        dst = jax.random.randint(k3, (E_RAND,), 0, N)
        loops = jnp.arange(N)
        edges = jnp.stack([jnp.concatenate([src, loops]), jnp.concatenate([dst, loops])], axis=1).astype(jnp.int32)
        W = jax.random.normal(k4, (IN_DIM, OUT_DIM), dtype=jnp.float32) / np.sqrt(IN_DIM)
        b = jnp.zeros((OUT_DIM,), dtype=jnp.float32)
        a = jax.random.normal(k5, (2 * OUT_DIM, 1), dtype=jnp.float32) * np.sqrt(2.0 / (2 * OUT_DIM))
        return {'features': features, 'edges': edges, 'W': W, 'b': b, 'a': a}
    _L0_gnn_all = _L0_gnn_setup()
    _L0_gnn_in = {k: v for k, v in _L0_gnn_all.items() if k in ('W', 'b', 'a')}
    del _L0_gnn_all

    def _L0_mix_setup():
        import jax, jax.numpy as jnp
        import numpy as np
        DIM = 512
        HEADS = 8
        DIM_HEAD = 64
        INNER = HEADS * DIM_HEAD
        key = jax.random.key(seed)
        k1, k2, k3, k4 = jax.random.split(key, 4)
        x = jax.random.normal(k1, (4, 256, DIM), dtype=jnp.float32)
        w_qkv = jax.random.normal(k2, (DIM, 3 * INNER), dtype=jnp.float32) / np.sqrt(DIM)
        w_out = jax.random.normal(k3, (INNER, DIM), dtype=jnp.float32) / np.sqrt(INNER)
        b_out = jax.random.normal(k4, (DIM,), dtype=jnp.float32) * 0.01
        return {'x': x, 'w_qkv': w_qkv, 'w_out': w_out, 'b_out': b_out}
    _L0_mix_all = _L0_mix_setup()
    _L0_mix_in = {k: v for k, v in _L0_mix_all.items() if k in ('w_qkv', 'w_out', 'b_out')}
    del _L0_mix_all

    def _L0_ffn_setup():
        import jax, jax.numpy as jnp
        import numpy as np
        B, S, D, F, E, K = (4, 64, 512, 64, 8, 2)
        key = jax.random.key(seed)
        kx, kg, kw, kv, k2 = jax.random.split(key, 5)
        scale = 0.02
        return {'x': jax.random.normal(kx, (B, S, D), dtype=jnp.float32), 'Wg': jax.random.normal(kg, (D, E), dtype=jnp.float32) * scale, 'W': jax.random.normal(kw, (E, D, F), dtype=jnp.float32) * scale, 'V': jax.random.normal(kv, (E, D, F), dtype=jnp.float32) * scale, 'W2': jax.random.normal(k2, (E, F, D), dtype=jnp.float32) * scale}
    _L0_ffn_all = _L0_ffn_setup()
    _L0_ffn_in = {k: v for k, v in _L0_ffn_all.items() if k in ('Wg', 'W', 'V', 'W2')}
    del _L0_ffn_all

    def _L1_gnn_setup():
        import jax, jax.numpy as jnp
        import numpy as np
        N_NODES = 625
        N_EDGES = 3125
        IN = 512
        HID = 512
        OUT = 512
        EF = 128
        NH = 16
        HEAD = OUT // NH

        def _ln(x):
            mu = jnp.mean(x, axis=-1, keepdims=True)
            var = jnp.var(x, axis=-1, keepdims=True)
            return (x - mu) / jnp.sqrt(var + 1e-05)

        def _mlp(x, W1, b1, g, be, W2, b2):
            hdn = x @ W1 + b1
            hdn = _ln(hdn) * g + be
            hdn = jax.nn.relu(hdn)
            return hdn @ W2 + b2
        key = jax.random.key(seed)
        ks = jax.random.split(key, 16)

        def w(k, i, o):
            return jax.random.normal(k, (i, o), jnp.float32) / np.float32(np.sqrt(i))
        inp = {'h': jax.random.normal(ks[0], (N_NODES, IN), jnp.float32), 'edge_feat': jax.random.normal(ks[1], (N_EDGES, EF), jnp.float32), 'edge_index': jax.random.randint(ks[2], (2, N_EDGES), 0, N_NODES, jnp.int32)}
        inp['hk_W1'] = w(ks[3], IN + EF, HID)
        inp['hk_b1'] = jnp.zeros((HID,), jnp.float32)
        inp['hk_g'] = jnp.ones((HID,), jnp.float32)
        inp['hk_be'] = jnp.zeros((HID,), jnp.float32)
        inp['hk_W2'] = w(ks[4], HID, OUT)
        inp['hk_b2'] = jnp.zeros((OUT,), jnp.float32)
        inp['hv_W1'] = w(ks[5], IN + EF, HID)
        inp['hv_b1'] = jnp.zeros((HID,), jnp.float32)
        inp['hv_g'] = jnp.ones((HID,), jnp.float32)
        inp['hv_be'] = jnp.zeros((HID,), jnp.float32)
        inp['hv_W2'] = w(ks[6], HID, OUT)
        inp['hv_b2'] = jnp.zeros((OUT,), jnp.float32)
        inp['hq_W1'] = w(ks[7], IN, HID)
        inp['hq_b1'] = jnp.zeros((HID,), jnp.float32)
        inp['hq_g'] = jnp.ones((HID,), jnp.float32)
        inp['hq_be'] = jnp.zeros((HID,), jnp.float32)
        inp['hq_W2'] = w(ks[8], HID, OUT)
        inp['hq_b2'] = jnp.zeros((OUT,), jnp.float32)
        inp['no_W1'] = w(ks[9], 2 * HID, HID)
        inp['no_b1'] = jnp.zeros((HID,), jnp.float32)
        inp['no_g'] = jnp.ones((HID,), jnp.float32)
        inp['no_be'] = jnp.zeros((HID,), jnp.float32)
        inp['no_W2'] = w(ks[10], HID, HID)
        inp['no_b2'] = jnp.zeros((HID,), jnp.float32)
        return inp
    _L1_gnn_all = _L1_gnn_setup()
    _L1_gnn_in = {k: v for k, v in _L1_gnn_all.items() if k in ('hk_W1', 'hk_b1', 'hk_g', 'hk_be', 'hk_W2', 'hk_b2', 'hv_W1', 'hv_b1', 'hv_g', 'hv_be', 'hv_W2', 'hv_b2', 'hq_W1', 'hq_b1', 'hq_g', 'hq_be', 'hq_W2', 'hq_b2', 'no_W1', 'no_b1', 'no_g', 'no_be', 'no_W2', 'no_b2')}
    del _L1_gnn_all

    def _L1_mix_setup():
        import jax, jax.numpy as jnp
        import numpy as np
        NUM_HEADS = 8
        EPS = 1e-06
        key = jax.random.key(seed)
        k1, k2, k3, k4 = jax.random.split(key, 4)
        B, N, C = (16, 128, 512)
        x = jax.random.normal(k1, (B, N, C), dtype=jnp.float32)
        W_qkv = jax.random.normal(k2, (3 * C, C), dtype=jnp.float32) * C ** (-0.5)
        W_proj = jax.random.normal(k3, (C, C), dtype=jnp.float32) * C ** (-0.5)
        b_proj = jax.random.normal(k4, (C,), dtype=jnp.float32) * 0.02
        return {'x': x, 'W_qkv': W_qkv, 'W_proj': W_proj, 'b_proj': b_proj}
    _L1_mix_all = _L1_mix_setup()
    _L1_mix_in = {k: v for k, v in _L1_mix_all.items() if k in ('W_qkv', 'W_proj', 'b_proj')}
    del _L1_mix_all

    def _L1_ffn_setup():
        import jax, jax.numpy as jnp
        import numpy as np
        B, T, D = (4, 256, 512)
        E, F, CAP = (8, 64, 128)
        key = jax.random.key(seed)
        ks = jax.random.split(key, 6)
        s = 0.02
        return {'x': jax.random.normal(ks[0], (B, T, D), dtype=jnp.float32), 'Wr': jax.random.normal(ks[1], (D, E), dtype=jnp.float32) * s, 'W1': jax.random.normal(ks[2], (E, D, F), dtype=jnp.float32) * s, 'b1': jax.random.normal(ks[3], (E, F), dtype=jnp.float32) * s, 'W2': jax.random.normal(ks[4], (E, F, D), dtype=jnp.float32) * s, 'b2': jax.random.normal(ks[5], (E, D), dtype=jnp.float32) * s}
    _L1_ffn_all = _L1_ffn_setup()
    _L1_ffn_in = {k: v for k, v in _L1_ffn_all.items() if k in ('Wr', 'W1', 'b1', 'W2', 'b2')}
    del _L1_ffn_all
    return {'x': x, 'src': src, 'dst': dst, 'edge_attr_128': edge_attr_128, 'L0_gnn_W': _L0_gnn_in['W'], 'L0_gnn_b': _L0_gnn_in['b'], 'L0_gnn_a': _L0_gnn_in['a'], 'L0_mix_w_qkv': _L0_mix_in['w_qkv'], 'L0_mix_w_out': _L0_mix_in['w_out'], 'L0_mix_b_out': _L0_mix_in['b_out'], 'L0_ffn_Wg': _L0_ffn_in['Wg'], 'L0_ffn_W': _L0_ffn_in['W'], 'L0_ffn_V': _L0_ffn_in['V'], 'L0_ffn_W2': _L0_ffn_in['W2'], 'L1_gnn_hk_W1': _L1_gnn_in['hk_W1'], 'L1_gnn_hk_b1': _L1_gnn_in['hk_b1'], 'L1_gnn_hk_g': _L1_gnn_in['hk_g'], 'L1_gnn_hk_be': _L1_gnn_in['hk_be'], 'L1_gnn_hk_W2': _L1_gnn_in['hk_W2'], 'L1_gnn_hk_b2': _L1_gnn_in['hk_b2'], 'L1_gnn_hv_W1': _L1_gnn_in['hv_W1'], 'L1_gnn_hv_b1': _L1_gnn_in['hv_b1'], 'L1_gnn_hv_g': _L1_gnn_in['hv_g'], 'L1_gnn_hv_be': _L1_gnn_in['hv_be'], 'L1_gnn_hv_W2': _L1_gnn_in['hv_W2'], 'L1_gnn_hv_b2': _L1_gnn_in['hv_b2'], 'L1_gnn_hq_W1': _L1_gnn_in['hq_W1'], 'L1_gnn_hq_b1': _L1_gnn_in['hq_b1'], 'L1_gnn_hq_g': _L1_gnn_in['hq_g'], 'L1_gnn_hq_be': _L1_gnn_in['hq_be'], 'L1_gnn_hq_W2': _L1_gnn_in['hq_W2'], 'L1_gnn_hq_b2': _L1_gnn_in['hq_b2'], 'L1_gnn_no_W1': _L1_gnn_in['no_W1'], 'L1_gnn_no_b1': _L1_gnn_in['no_b1'], 'L1_gnn_no_g': _L1_gnn_in['no_g'], 'L1_gnn_no_be': _L1_gnn_in['no_be'], 'L1_gnn_no_W2': _L1_gnn_in['no_W2'], 'L1_gnn_no_b2': _L1_gnn_in['no_b2'], 'L1_mix_W_qkv': _L1_mix_in['W_qkv'], 'L1_mix_W_proj': _L1_mix_in['W_proj'], 'L1_mix_b_proj': _L1_mix_in['b_proj'], 'L1_ffn_Wr': _L1_ffn_in['Wr'], 'L1_ffn_W1': _L1_ffn_in['W1'], 'L1_ffn_b1': _L1_ffn_in['b1'], 'L1_ffn_W2': _L1_ffn_in['W2'], 'L1_ffn_b2': _L1_ffn_in['b2']}

def reference(x, src, dst, edge_attr_128, L0_gnn_W, L0_gnn_b, L0_gnn_a, L0_mix_w_qkv, L0_mix_w_out, L0_mix_b_out, L0_ffn_Wg, L0_ffn_W, L0_ffn_V, L0_ffn_W2, L1_gnn_hk_W1, L1_gnn_hk_b1, L1_gnn_hk_g, L1_gnn_hk_be, L1_gnn_hk_W2, L1_gnn_hk_b2, L1_gnn_hv_W1, L1_gnn_hv_b1, L1_gnn_hv_g, L1_gnn_hv_be, L1_gnn_hv_W2, L1_gnn_hv_b2, L1_gnn_hq_W1, L1_gnn_hq_b1, L1_gnn_hq_g, L1_gnn_hq_be, L1_gnn_hq_W2, L1_gnn_hq_b2, L1_gnn_no_W1, L1_gnn_no_b1, L1_gnn_no_g, L1_gnn_no_be, L1_gnn_no_W2, L1_gnn_no_b2, L1_mix_W_qkv, L1_mix_W_proj, L1_mix_b_proj, L1_ffn_Wr, L1_ffn_W1, L1_ffn_b1, L1_ffn_W2, L1_ffn_b2):
    import jax
    import jax.numpy as jnp

    def _L0_gnn_ref(features, edges, W, b, a):
        import jax, jax.numpy as jnp
        import numpy as np
        N = 1250
        IN_DIM = 512
        OUT_DIM = 512
        E_RAND = 20000
        SLOPE = 0.1
        emb = features @ W + b
        a_src = a[:OUT_DIM, 0]
        a_dst = a[OUT_DIM:, 0]
        s_node = emb @ a_src
        t_node = emb @ a_dst
        src = edges[:, 0]
        dst = edges[:, 1]
        e = jnp.exp(jax.nn.leaky_relu(s_node[src] + t_node[dst], negative_slope=SLOPE))
        row_sum = jax.ops.segment_sum(e, src, num_segments=N)
        results = jax.ops.segment_sum(e[:, None] * emb[dst], src, num_segments=N)
        return results / row_sum[:, None]

    def _L0_mix_ref(x, w_qkv, w_out, b_out):
        import jax, jax.numpy as jnp
        import numpy as np
        DIM = 512
        HEADS = 8
        DIM_HEAD = 64
        INNER = HEADS * DIM_HEAD
        b, n, d = x.shape
        qkv = x @ w_qkv
        q, k, v = jnp.split(qkv, 3, axis=-1)

        def to_heads(t):
            return t.reshape(b, n, HEADS, DIM_HEAD).transpose(0, 2, 1, 3)
        q, k, v = map(to_heads, (q, k, v))
        q = jax.nn.elu(q) + 1.0
        k = jax.nn.elu(k) + 1.0
        kv = jnp.einsum('bhnd,bhnm->bhdm', k, v)
        z = 1.0 / (jnp.einsum('bhnd,bhd->bhn', q, k.sum(axis=2)) + 1e-06)
        out = jnp.einsum('bhnd,bhdm->bhnm', q, kv) * z[..., None]
        out = out.transpose(0, 2, 1, 3).reshape(b, n, INNER)
        return out @ w_out + b_out

    def _L0_ffn_ref(x, Wg, W, V, W2):
        import jax, jax.numpy as jnp
        import numpy as np
        B, S, D, F, E, K = (4, 64, 512, 64, 8, 2)
        gate_logits = jnp.einsum('bsd,de->bse', x, Wg)
        topv, topi = jax.lax.top_k(gate_logits, K)
        w = jax.nn.softmax(topv, axis=-1)
        gw = jnp.sum(w[..., None] * jax.nn.one_hot(topi, E, dtype=x.dtype), axis=-2)
        y = jnp.zeros_like(x)
        n_experts = W.shape[0]
        for e in range(n_experts):
            h = jax.nn.silu(jnp.einsum('bsd,df->bsf', x, W[e])) * jnp.einsum('bsd,df->bsf', x, V[e])
            y = y + gw[..., e:e + 1] * jnp.einsum('bsf,fd->bsd', h, W2[e])
        return y

    def _L1_gnn_ref(h, edge_feat, edge_index, hk_W1, hk_b1, hk_g, hk_be, hk_W2, hk_b2, hv_W1, hv_b1, hv_g, hv_be, hv_W2, hv_b2, hq_W1, hq_b1, hq_g, hq_be, hq_W2, hq_b2, no_W1, no_b1, no_g, no_be, no_W2, no_b2):
        import jax, jax.numpy as jnp
        import numpy as np
        N_NODES = 625
        N_EDGES = 3125
        IN = 512
        HID = 512
        OUT = 512
        EF = 128
        NH = 16
        HEAD = OUT // NH

        def _ln(x):
            mu = jnp.mean(x, axis=-1, keepdims=True)
            var = jnp.var(x, axis=-1, keepdims=True)
            return (x - mu) / jnp.sqrt(var + 1e-05)

        def _mlp(x, W1, b1, g, be, W2, b2):
            hdn = x @ W1 + b1
            hdn = _ln(hdn) * g + be
            hdn = jax.nn.relu(hdn)
            return hdn @ W2 + b2
        N = h.shape[0]
        src, dst = (edge_index[0], edge_index[1])
        kv_in = jnp.concatenate([h[src], edge_feat], axis=-1)
        k = _mlp(kv_in, hk_W1, hk_b1, hk_g, hk_be, hk_W2, hk_b2).reshape(-1, NH, HEAD)
        v = _mlp(kv_in, hv_W1, hv_b1, hv_g, hv_be, hv_W2, hv_b2).reshape(-1, NH, HEAD)
        q = _mlp(h, hq_W1, hq_b1, hq_g, hq_be, hq_W2, hq_b2).reshape(-1, NH, HEAD)
        logits = jnp.sum(q[dst] * k, axis=-1) / np.float32(np.sqrt(HEAD))
        mx = jax.ops.segment_max(logits, dst, num_segments=N)
        ex = jnp.exp(logits - mx[dst])
        den = jax.ops.segment_sum(ex, dst, num_segments=N)
        alpha = ex / den[dst]
        m = alpha[..., None] * v
        out = jax.ops.segment_sum(m, dst, num_segments=N).reshape(N, OUT)
        out = _mlp(jnp.concatenate([out, h], axis=-1), no_W1, no_b1, no_g, no_be, no_W2, no_b2)
        return out + h

    def _L1_mix_ref(x, W_qkv, W_proj, b_proj):
        import jax, jax.numpy as jnp
        import numpy as np
        NUM_HEADS = 8
        EPS = 1e-06
        B, N, C = x.shape
        H = NUM_HEADS
        E = C // H
        scale = E ** (-0.5)
        qkv = (x @ W_qkv.T).reshape(B, N, 3, H, E)
        q, k, v = (qkv[:, :, 0], qkv[:, :, 1], qkv[:, :, 2])
        q_ = jax.nn.relu(q) + scale
        k_ = jax.nn.relu(k) + scale
        kv = jnp.einsum('bnhe,bnhf->bhef', k_, v)
        k_sum = jnp.sum(k_, axis=1)
        z = 1.0 / (jnp.einsum('bnhe,bhe->bnh', q_, k_sum) + EPS)
        out = jnp.einsum('bnhe,bhef->bnhf', q_, kv) * z[..., None]
        out = out.reshape(B, N, C)
        return out @ W_proj.T + b_proj

    def _L1_ffn_ref(x, Wr, W1, b1, W2, b2):
        import jax, jax.numpy as jnp
        import numpy as np
        B, T, D = (4, 256, 512)
        E, F, CAP = (8, 64, 128)
        Bb, Tt, Dd = x.shape
        N = Bb * Tt
        C = min(CAP, N)
        x_flat = x.reshape(N, Dd)
        logits = x_flat @ Wr
        probs = jax.nn.softmax(logits, axis=0)
        vals, idx = jax.lax.top_k(probs.T, C)
        selected = x_flat[idx]
        h = jax.nn.gelu(jnp.einsum('ecd,edf->ecf', selected, W1) + b1[:, None, :], approximate=False)
        out_e = jnp.einsum('ecf,efd->ecd', h, W2) + b2[:, None, :]
        weighted = vals[..., None] * out_e
        output = jnp.zeros_like(x_flat).at[idx.reshape(-1)].add(weighted.reshape(-1, Dd))
        return output.reshape(Bb, Tt, Dd)
    edge_index = jnp.stack([src, dst])
    edge_index_t = jnp.stack([src, dst], axis=1)
    xn = _layernorm(x, axis=-1)
    x = x + _L0_gnn_ref(xn, edge_index_t, L0_gnn_W, L0_gnn_b, L0_gnn_a) + _L0_mix_ref(xn[None], L0_mix_w_qkv, L0_mix_w_out, L0_mix_b_out)[0]
    x = x + _L0_ffn_ref(_layernorm(x, axis=-1)[None], L0_ffn_Wg, L0_ffn_W, L0_ffn_V, L0_ffn_W2)[0]
    xn = _layernorm(x, axis=-1)
    x = x + _L1_gnn_ref(xn, edge_attr_128, edge_index, L1_gnn_hk_W1, L1_gnn_hk_b1, L1_gnn_hk_g, L1_gnn_hk_be, L1_gnn_hk_W2, L1_gnn_hk_b2, L1_gnn_hv_W1, L1_gnn_hv_b1, L1_gnn_hv_g, L1_gnn_hv_be, L1_gnn_hv_W2, L1_gnn_hv_b2, L1_gnn_hq_W1, L1_gnn_hq_b1, L1_gnn_hq_g, L1_gnn_hq_be, L1_gnn_hq_W2, L1_gnn_hq_b2, L1_gnn_no_W1, L1_gnn_no_b1, L1_gnn_no_g, L1_gnn_no_be, L1_gnn_no_W2, L1_gnn_no_b2) + _L1_mix_ref(xn[None], L1_mix_W_qkv, L1_mix_W_proj, L1_mix_b_proj)[0]
    x = x + _L1_ffn_ref(_layernorm(x, axis=-1)[None], L1_ffn_Wr, L1_ffn_W1, L1_ffn_b1, L1_ffn_W2, L1_ffn_b2)[0]
    return x

_drawn_inputs = setup_inputs


def setup_inputs(seed=0):
    import zlib

    import numpy as np

    out = dict(_drawn_inputs(seed))
    spreads = {'L0_gnn_b': (0.0, 0.1),
     'L1_gnn_hk_b1': (0.0, 0.8),
     'L1_gnn_hk_g': (1.0, 0.6),
     'L1_gnn_hk_be': (0.0, 0.8),
     'L1_gnn_hk_b2': (0.0, 2.0),
     'L1_gnn_hv_b1': (0.0, 0.464),
     'L1_gnn_hv_g': (1.0, 0.537),
     'L1_gnn_hv_be': (0.0, 0.471),
     'L1_gnn_hv_b2': (0.0, 0.295),
     'L1_gnn_hq_b1': (0.0, 0.8),
     'L1_gnn_hq_g': (1.0, 0.6),
     'L1_gnn_hq_be': (0.0, 0.8),
     'L1_gnn_hq_b2': (0.0, 0.8),
     'L1_gnn_no_b1': (0.0, 0.381),
     'L1_gnn_no_g': (1.0, 0.2),
     'L1_gnn_no_be': (0.0, 0.375),
     'L1_gnn_no_b2': (0.0, 0.275)}
    factors = {'L0_mix_b_out': 5.793,
     'L0_ffn_Wg': 5.745,
     'L0_ffn_W': 5.028,
     'L0_ffn_V': 4.872,
     'L0_ffn_W2': 4.915,
     'L1_gnn_hk_W1': 2.764,
     'L1_gnn_hk_W2': 2.779,
     'L1_gnn_hq_W1': 3.414,
     'L1_gnn_hq_W2': 2.808,
     'L1_mix_b_proj': 6.612,
     'L1_ffn_Wr': 8.0,
     'L1_ffn_W1': 22.553,
     'L1_ffn_b1': 200.0,
     'L1_ffn_W2': 8.0,
     'L1_ffn_b2': 200.0,
     'L1_mix_W_proj': 2.704}
    for name, (base, spread) in spreads.items():
        noise = np.random.default_rng([zlib.crc32(name.encode()), seed]).standard_normal(out[name].shape)
        drawn = base * np.exp(spread * noise) if base else spread * noise
        out[name] = jnp.asarray(drawn.astype(out[name].dtype))
    for name, factor in factors.items():
        out[name] = (out[name] * factor).astype(out[name].dtype)
    return out
```

```python
from contextlib import ExitStack

import concourse.bass as bass
import concourse.mybir as mybir
from concourse.alu_op_type import AluOpType as ALU

ACT = mybir.ActivationFunctionType
AX = mybir.AxisListType
F32 = mybir.dt.float32
I32 = mybir.dt.int32

P = 125
N = 1250
T = N // P
D = 512
KC = D // 128
NB = 250
NN = N // NB
E = 21250
CH = E // P
EF = 128
NE = 8
CAP = 128
NH = 16
HD = D // NH
QW = D + NH
EPS = 1e-5
BIG = 1e30
TABLES = 2
GR = 10
SB_ = 5
BC = CH // SB_
BE = BC * P


def sl(t, n=P):
    return slice(t * n, (t + 1) * n)


class Env:

    def __init__(self, nc, ctx):
        self.nc, self.ctx, self.sems, self.stage = nc, ctx, {}, 0

    def sem(self, name):
        if name not in self.sems:
            self.sems[name] = self.nc.alloc_semaphore(name=name)
        return self.sems[name]

    def retire(self, *prefixes):
        old = [n for n in self.sems if n.startswith(prefixes)]
        self.nc.clear_and_free_semaphores([self.sems.pop(n) for n in old])
        self.nc.all_engine_barrier()

    def sb(self, ctx, name, shape, dt=F32):
        return ctx.enter_context(self.nc.sbuf_tensor(f"{name}_{self.stage}", shape, dt))

    def banks(self, ctx, name, n):
        return [ctx.enter_context(self.nc.psum_tensor(f"{name}{i}_{self.stage}", [128, 512], F32)) for i in range(n)]


def rows(w, width=None):
    return w.rearrange("(k p) m -> p k m", p=128)


def bcast(row, parts, n):
    return row.rearrange("(o n) -> o n", o=1).to_broadcast([parts, n])


def setup(env, src, dst, cnt, agg, x):
    nc = env.nc
    with ExitStack() as ctx:
        sb = lambda n, s, d=F32: env.sb(ctx, n, s, d)
        zero = sb("zero", [P, N + 1])
        rowi = sb("rowi", [85, 3, 2, P], I32)
        rowf = sb("rowf", [85, 3, 2, P])
        nextf = sb("nextf", [P, CH])
        lastf = sb("lastf", [P, 1])
        junki = sb("junki", [P, 1], I32)
        tmp = sb("tmp", [P, CH])
        ps = env.banks(ctx, "ps", 3)
        s_mem, s_sel, s_zero, s_zd = env.sem("const_cleared"), env.sem("const_ready"), env.sem("zero_ready"), env.sem("tables_cleared")
        s_row, s_rowf, s_tr, s_col, s_pad, s_x = (env.sem("index_rows_loaded"), env.sem("index_rows_float"),
                                             env.sem("index_columns"), env.sem("index_step"), env.sem("index_padded"),
                                             env.sem("x_loaded"))
        with nc.Block() as block:
            @block.sync
            def _(sp):
                sp.wait_ge(s_pad, 1)
                for n, a in enumerate((src, dst)):
                    sp.dma_start(rowi[:, n, :, :], a.rearrange("(p h e) -> p h e", h=2, e=P)).then_inc(s_row, 16)
                m = 84 * 2 * P
                sp.dma_start(rowi[0:84, 2, :, :], dst[1:1 + m].rearrange("(p h e) -> p h e", h=2, e=P)).then_inc(s_row, 16)
                sp.dma_start(rowi[84:85, 2, 0, :], dst[1 + m:1 + m + P].rearrange("(p e) -> p e", e=P)).then_inc(s_row, 16)
                sp.dma_start(rowi[84:85, 2, 1, 0:P - 1], dst[1 + m + P:E].rearrange("(p e) -> p e", e=P - 1)).then_inc(s_row, 16)
                sp.dma_start(env.X[:, :, :], x.rearrange("(t p) d -> p t d", p=P)).then_inc(s_x, 16)
                sp.wait_ge(s_zero, 1)
                n = 0
                for table in cnt:
                    for k in range(T):
                        sp.dma_start(table[k * P * N:(k + 1) * P * N, :].rearrange("(p a) o -> p (a o)", p=P),
                                     zero[:, 0:N]).then_inc(s_zd, 16)
                        n += 16
                    sp.dma_start(table[N * N:N * N + P, :], zero[:, 0:1]).then_inc(s_zd, 16)
                    n += 16
                for k in range(T):
                    sp.dma_start(agg[sl(k), :], zero[:, 0:QW]).then_inc(s_zd, 16)
                    n += 16
                sp.wait_ge(s_zd, n)
                sp.wait_ge(s_x, 16)

            @block.gpsimd
            def _(g):
                for n, (m, v) in enumerate(((env.ident, 0.0), (env.bd, 0.0), (env.later, 1.0), (env.tri, 1.0),
                                            (env.sel, 0.0), (lastf, 0.0))):
                    if n:
                        g.wait_ge(s_mem, n)
                    g.memset(m[:], v).then_inc(s_mem, 1)
                g.wait_ge(s_mem, 6)
                g.affine_select(out=env.ident[:, :], in_=env.ident[:, :], compare_op=ALU.not_equal, fill=1.0,
                                base=0, pattern=[[-1, 128]], channel_multiplier=1).then_inc(s_sel, 1)
                g.wait_ge(s_sel, 1)
                g.memset(env.bd[0:64, 0:64], 1.0).then_inc(s_sel, 1)
                g.wait_ge(s_sel, 2)
                g.memset(env.bd[64:128, 64:128], 1.0).then_inc(s_sel, 1)
                g.wait_ge(s_sel, 3)
                g.affine_select(out=env.later[:, :], in_=env.later[:, :], compare_op=ALU.is_gt, fill=0.0,
                                base=0, pattern=[[1, P]], channel_multiplier=-1).then_inc(s_sel, 1)
                g.wait_ge(s_sel, 4)
                g.affine_select(out=env.tri[:, :, :], in_=env.tri[:, :, :], compare_op=ALU.is_gt, fill=0.0,
                                base=0, pattern=[[1, NE], [-1, NE]], channel_multiplier=0).then_inc(s_sel, 1)
                g.wait_ge(s_sel, 5)
                g.affine_select(out=env.sel[:, :, :].rearrange("e b (h f) -> e (b h) f", h=2),
                                in_=env.sel[:, :, :].rearrange("e b (h f) -> e (b h) f", h=2),
                                compare_op=ALU.not_equal, fill=1.0, base=0, pattern=[[-1, NE], [0, 64]],
                                channel_multiplier=1).then_inc(s_sel, 1)
                g.wait_ge(s_sel, 6)
                g.affine_select(out=lastf[:, :], in_=lastf[:, :], compare_op=ALU.not_equal, fill=1.0,
                                base=-(P - 1), pattern=[[0, 1]], channel_multiplier=1).then_inc(s_sel, 1)
                g.wait_ge(s_sel, 7)
                g.iota(junki[:, :], pattern=[[0, 1]], base=N * N, channel_multiplier=1).then_inc(s_sel, 1)

            @block.vector
            def _(dve):
                dve.memset(rowi[:, :, :, :], -1).then_inc(s_pad, 1)
                dve.memset(zero[:, :], 0.0).then_inc(s_zero, 1)
                dve.memset(env.ones[:, :], 1.0).then_inc(s_zero, 1)
                dve.memset(env.eps[:, :], EPS).then_inc(s_zero, 1)
                dve.wait_ge(s_row, 80)
                dve.tensor_copy(rowf[:, :, :, :], rowi[:, :, :, :]).then_inc(s_rowf, 1)
                dve.wait_ge(s_sel, 8)
                dve.tensor_copy(env.junk[:, :], junki[:, :]).then_inc(s_col, 1)
                dve.wait_ge(s_tr, 1)
                for n, to in enumerate((env.srcf, env.dstf, nextf)):
                    dve.tensor_copy(to[:, :].rearrange("p (c h) -> p h c", h=2),
                                    ps[n][0:P, 0:CH].rearrange("p (h c) -> p h c", h=2)).then_inc(s_col, 1)
                dve.wait_ge(s_col, 4)
                dve.tensor_copy(env.srci[:, :], env.srcf[:, :]).then_inc(s_col, 1)
                dve.tensor_copy(env.dsti[:, :], env.dstf[:, :]).then_inc(s_col, 1)
                dve.scalar_tensor_tensor(env.keyf[:, :], env.dstf[:, :], float(N), env.srcf[:, :], ALU.mult, ALU.add)\
                   .then_inc(s_col, 1)
                dve.tensor_tensor(tmp[:, :], env.dstf[:, :], nextf[:, :], ALU.is_equal).then_inc(s_col, 1)
                dve.wait_ge(s_col, 8)
                dve.scalar_tensor_tensor(env.scati[:, :], tmp[:, :], float(4 * N), env.dstf[:, :], ALU.mult, ALU.add)\
                   .then_inc(s_col, 1)
                dve.memset(env.prevf[:, 0:1], -1.0).then_inc(s_col, 1)
                dve.tensor_scalar(env.prevf[:, 1:CH], env.dstf[:, 0:CH - 1], 1.0, lastf[:, 0:1], ALU.add, ALU.mult)\
                   .then_inc(s_col, 1)
                dve.wait_ge(s_col, 11)
                dve.tensor_scalar(env.prevf[:, 1:CH], env.prevf[:, 1:CH], -1.0, None, ALU.add).then_inc(s_col, 1)

            @block.tensor
            def _(pe):
                pe.wait_ge(s_rowf, 1)
                pe.wait_ge(s_sel, 8)
                for n in range(3):
                    for h in range(2):
                        last = pe.transpose(ps[n][0:P, 85 * h:85 * h + 85], rowf[:, n, h, :], env.ident[0:85, 0:85])
                last.then_inc(s_tr, 1)


def layernorm(env, call):
    env.stage += 1
    nc, X, XN, xnT = env.nc, env.X, env.XN, env.xnT
    stats, aggr, var, std, rstd, xn, tr, out = (env.sem(n) for n in (
        "ln_stats", "ln_moments", "ln_var_eps", "ln_std", "ln_rstd", "xn_ready", "xn_transposed", "xnT_ready"))
    b = T * call
    with ExitStack() as ctx:
        st = env.sb(ctx, "ln_st", [P, T, 6])
        mv = env.sb(ctx, "ln_mv", [P, T, 2])
        sd = env.sb(ctx, "ln_sd", [P, T])
        rs = env.sb(ctx, "ln_rs", [P, T])
        ps = env.banks(ctx, "ln_ps", 2)
        with nc.Block() as block:
            @block.vector
            def _(dve):
                for t in range(T):
                    dve.bn_stats(st[:, t, :], X[:, t, :]).then_inc(stats, 1)
                for t in range(T):
                    dve.wait_ge(stats, b + t + 1)
                    dve.bn_aggr(mv[:, t, :], st[:, t, :]).then_inc(aggr, 1)
                dve.wait_ge(aggr, b + T)
                dve.tensor_scalar(sd[:, :], mv[:, :, 1], EPS, None, ALU.add).then_inc(var, 1)
                dve.wait_ge(std, call + 1)
                dve.reciprocal(rs[:, :], sd[:, :]).then_inc(rstd, 1)
                dve.wait_ge(rstd, call + 1)
                for t in range(T):
                    dve.tensor_scalar(XN[:, t, :], X[:, t, :], mv[:, t, 0:1], rs[:, t:t + 1], ALU.subtract, ALU.mult)\
                       .then_inc(xn, 1)

            @block.scalar
            def _(act):
                act.wait_ge(var, call + 1)
                act.activation(sd[:, :], sd[:, :], ACT.Sqrt).then_inc(std, 1)
                for t in range(T):
                    act.wait_ge(tr, b + t + 1)
                    act.activation(xnT[:, :, sl(t)], ps[t % 2][:, 0:KC * P].rearrange("p (k n) -> p k n", k=KC), ACT.Copy)\
                       .then_inc(out, 1)

            @block.tensor
            def _(pe):
                for t in range(T):
                    pe.wait_ge(xn, b + t + 1)
                    if t >= 2:
                        pe.wait_ge(out, b + t - 1)
                    for k in range(KC):
                        last = pe.transpose(ps[t % 2][:, sl(k)], XN[:, t, sl(k, 128)], env.ident[0:P, 0:P])
                    last.then_inc(tr, 1)


def linear_attention(env, call, wqkv, wout, bout, elu, counts=None):
    env.stage += 1
    nc, X, xnT = env.nc, env.X, env.xnT
    names = ("mix_weights", "mix_k_done", "mix_v_done", "mix_k_neg", "mix_k_exp", "mix_kf", "mix_v", "mix_kv", "mix_kvbd",
             "mix_ksb", "mix_kvT_ps", "mix_kvT", "mix_m_ps", "mix_m", "mix_q_ps", "mix_q_neg", "mix_q_exp", "mix_q",
             "mix_den_ps", "mix_den", "mix_rden", "mix_qs", "mix_y_ps", "mix_yb", "mix_x", "mix_ones")
    s = {n: env.sem(n) for n in names}
    SCALE = 64 ** -0.5
    U = KC * NN
    with ExitStack() as ctx:
        sb = lambda n, sh, d=F32: env.sb(ctx, n, sh, d)
        W = sb("mixW", [128, KC, 3 * D])
        WO = sb("mixWO", [128, KC, D])
        BO = sb("mixBO", [P, D])
        kf = sb("kf", [P, 2, D])
        kn = sb("kn", [P, 2, D])
        v = sb("v", [P, 2, KC, 130])
        qT = sb("qT", [128, KC, N])
        qn = sb("qn", [128, 2, NB])
        kvbd = sb("kvbd", [128, KC, 128])
        ksb = sb("ksb", [128, KC, 128])
        kvT = sb("kvT", [128, KC, 128])
        M = sb("M", [128, KC, D])
        dn = sb("dn", [128, 2, NB])
        yb = sb("yb", [P, 2, D])
        if counts:
            keyrow = sb("keyrow", [P, 2, GR * P])
            dr = sb("dr", [P, 2, GR * P], I32)
            sr = sb("sr", [P, 2, GR * P], I32)
            eq = sb("eq", [P, 2, P])
        ring = env.banks(ctx, "ring", 4)
        kvp = env.banks(ctx, "kvp", 4)
        src, dst, cnt = counts or (None, None, None)
        if counts:
            c_key, c_num, c_idx, c_fin = (env.sem(n) for n in ("count_keys", "count_compared", "count_step", "count_ready"))
            c_put = [env.sem(f"count_scattered{i}") for i in range(TABLES)]
            c_slot = [env.sem(f"count_rows_loaded{i}") for i in range(2)]

        with nc.Block() as block:
            @block.sync
            def _(sp):
                sp.dma_start(W[:, :, :], rows(wqkv)).then_inc(s["mix_weights"], 16)
                sp.dma_start(WO[:, :, :], rows(wout)).then_inc(s["mix_weights"], 16)
                sp.dma_start(BO[:, :], bcast(bout, P, D)).then_inc(s["mix_weights"], 16)
                if counts:
                    for g in range(CH // GR):
                        if g >= 2:
                            sp.wait_ge(c_key, g - 1)
                        for a, to in ((dst, dr), (src, sr)):
                            sp.dma_start(to[:, g % 2, :], bcast(a[g * GR * P:(g + 1) * GR * P], P, GR * P))\
                              .then_inc(c_slot[g % 2], 16)

            if counts:
                @block.gpsimd
                def _(g):
                    for c in range(CH):
                        if c % GR == 0:
                            g.wait_ge(c_fin, c // GR + 1)
                        if c >= TABLES:
                            g.wait_ge(c_put[c % TABLES], 16 * (c // TABLES))
                        g.indirect_dma_start(out=cnt[c % TABLES][:, :],
                                             out_offset=bass.IndirectOffsetOnAxis(ap=env.cidx[:, c:c + 1], axis=0),
                                             in_=env.cnum[:, c:c + 1], in_offset=None, compute_op=ALU.add)\
                         .then_inc(c_put[c % TABLES], 16)
                    for i in range(TABLES):
                        g.wait_ge(c_put[i], 16 * (CH // TABLES))

            @block.vector
            def _(dve):
                def count_group(g):
                    dve.wait_ge(c_slot[g % 2], 32 * (g // 2 + 1))
                    if g >= 2:
                        dve.wait_ge(c_num, 2 * GR * (g - 1))
                    dve.scalar_tensor_tensor(keyrow[:, g % 2, :], dr[:, g % 2, :], float(N), sr[:, g % 2, :], ALU.mult, ALU.add)\
                       .then_inc(c_key, 1)
                    dve.wait_ge(c_key, g + 1)
                    for i in range(GR):
                        c = g * GR + i
                        row = keyrow[:, g % 2, sl(i)]
                        if c:
                            dve.wait_ge(c_num, 2 * c)
                        dve.tensor_scalar(eq[:, 0, :], row, env.keyf[:, c:c + 1], 0.0, ALU.is_equal, ALU.add,
                                          accum_out=env.cnum[:, c:c + 1]).then_inc(c_num, 1)
                        dve.scalar_tensor_tensor(eq[:, 1, :], row, env.keyf[:, c:c + 1], env.later[:, :],
                                                 ALU.is_equal, ALU.mult, accum_out=env.clater[:, c:c + 1]).then_inc(c_num, 1)
                    cs = slice(g * GR, (g + 1) * GR)
                    k = 2 * g
                    dve.wait_ge(c_num, 2 * GR * (g + 1))
                    dve.tensor_scalar(env.clater[:, cs], env.clater[:, cs], 0.0, None, ALU.is_equal).then_inc(c_idx, 1)
                    dve.tensor_scalar(env.cdel[:, cs], env.keyf[:, cs], env.junk[:, 0:1], None, ALU.subtract).then_inc(c_idx, 1)
                    dve.wait_ge(c_idx, 3 * g + 2)
                    dve.tensor_tensor(env.cdel[:, cs], env.cdel[:, cs], env.clater[:, cs], ALU.mult).then_inc(c_idx, 1)
                    dve.wait_ge(c_idx, 3 * g + 3)
                    dve.tensor_scalar(env.cidx[:, cs], env.cdel[:, cs], env.junk[:, 0:1], None, ALU.add).then_inc(c_fin, 1)

                groups = list(range(CH // GR)) if counts else []
                if counts:
                    count_group(groups.pop(0))
                dve.memset(v[:, :, :, :], 1.0).then_inc(s["mix_ones"], 1)
                dve.wait_ge(s["mix_weights"], 48 * (call + 1))
                b = T * call
                for t in range(T):
                    u = t % 2
                    dve.wait_ge(s["mix_k_done"], b + t + 1)
                    if t >= 2:
                        dve.wait_ge(s["mix_kv"], b + t - 1)
                    if elu:
                        dve.tensor_scalar(kn[:, u, :], ring[u][0:P, :], 0.0, None, ALU.min).then_inc(s["mix_k_neg"], 1)
                        dve.wait_ge(s["mix_k_exp"], t + 1)
                        dve.scalar_tensor_tensor(kf[:, u, :], ring[u][0:P, :], 0.0, kn[:, u, :], ALU.max, ALU.add)\
                           .then_inc(s["mix_kf"], 1)
                    else:
                        dve.tensor_scalar(kf[:, u, :], ring[u][0:P, :], 0.0, SCALE, ALU.max, ALU.add).then_inc(s["mix_kf"], 1)
                    if groups:
                        count_group(groups.pop(0))
                dve.wait_ge(s["mix_kv"], b + T)
                for j in range(KC):
                    dve.tensor_tensor(kvbd[:, j, :], kvp[j][:, 0:128], env.bd[:, :], ALU.mult).then_inc(s["mix_kvbd"], 1)
                    dve.tensor_scalar(ksb[:, j, :], env.bd[:, :], kvp[j][:, 128:129], None, ALU.mult).then_inc(s["mix_ksb"], 1)
                for n in range(U):
                    j, m = n // NN, n % NN
                    q = qT[:, j, sl(m, NB)]
                    dve.wait_ge(s["mix_q_ps"], U * call + n + 1)
                    if elu:
                        dve.tensor_scalar(qn[:, n % 2, :], ring[n % 4][:, 0:NB], 0.0, None, ALU.min).then_inc(s["mix_q_neg"], 1)
                        dve.wait_ge(s["mix_q_exp"], n + 1)
                        dve.scalar_tensor_tensor(q, ring[n % 4][:, 0:NB], 0.0, qn[:, n % 2, :], ALU.max, ALU.add)\
                           .then_inc(s["mix_q"], 1)
                    else:
                        dve.tensor_scalar(q, ring[n % 4][:, 0:NB], 0.0, SCALE, ALU.max, ALU.add).then_inc(s["mix_q"], 1)
                    if groups and n % 3 == 2:
                        count_group(groups.pop(0))
                for n in range(U):
                    j, m = n // NN, n % NN
                    k = U * call + n
                    q = qT[:, j, sl(m, NB)]
                    dve.wait_ge(s["mix_den_ps"], k + 1)
                    dve.tensor_scalar(dn[:, n % 2, :], ring[n % 4][:, 0:NB], 1e-6, None, ALU.add).then_inc(s["mix_den"], 1)
                    dve.wait_ge(s["mix_den"], k + 1)
                    dve.reciprocal(dn[:, n % 2, :], dn[:, n % 2, :]).then_inc(s["mix_rden"], 1)
                    dve.wait_ge(s["mix_rden"], k + 1)
                    dve.tensor_tensor(q, q, dn[:, n % 2, :], ALU.mult).then_inc(s["mix_qs"], 1)
                    if groups and n % 2:
                        count_group(groups.pop(0))
                for t in range(T):
                    dve.wait_ge(s["mix_y_ps"], b + t + 1)
                    dve.tensor_tensor(yb[:, t % 2, :], ring[t % 4][0:P, :], BO[:, :], ALU.add).then_inc(s["mix_yb"], 1)
                    dve.wait_ge(s["mix_yb"], b + t + 1)
                    dve.tensor_tensor(X[:, t, :], X[:, t, :], yb[:, t % 2, :], ALU.add).then_inc(s["mix_x"], 1)

            @block.scalar
            def _(act):
                b = T * call
                act.wait_ge(s["mix_ones"], call + 1)
                for t in range(T):
                    u = t % 2
                    if elu:
                        act.wait_ge(s["mix_k_neg"], t + 1)
                        act.activation(kn[:, u, :], kn[:, u, :], ACT.Exp).then_inc(s["mix_k_exp"], 1)
                    act.wait_ge(s["mix_v_done"], b + t + 1)
                    if t >= 2:
                        act.wait_ge(s["mix_kv"], b + t - 1)
                    act.activation(v[:, u, :, 0:128], ring[2 + u][0:P, :].rearrange("p (j m) -> p j m", j=KC), ACT.Copy)\
                       .then_inc(s["mix_v"], 1)
                if elu:
                    for n in range(4):
                        act.wait_ge(s["mix_q_neg"], n + 1)
                        act.activation(qn[:, n % 2, :], qn[:, n % 2, :], ACT.Exp).then_inc(s["mix_q_exp"], 1)
                for j in range(KC):
                    act.wait_ge(s["mix_kvT_ps"], KC * call + j + 1)
                    act.activation(kvT[:, j, :], kvp[j][:, 0:128], ACT.Copy).then_inc(s["mix_kvT"], 1)
                for j in range(KC):
                    act.wait_ge(s["mix_m_ps"], KC * call + j + 1)
                    act.activation(M[:, j, :], kvp[j][:, :], ACT.Copy).then_inc(s["mix_m"], 1)
                if elu:
                    for n in range(4, U):
                        act.wait_ge(s["mix_q_neg"], n + 1)
                        act.activation(qn[:, n % 2, :], qn[:, n % 2, :], ACT.Exp).then_inc(s["mix_q_exp"], 1)

            @block.tensor
            def _(pe):
                b = T * call

                def product(ps, t, w, col):
                    for k in range(KC):
                        last = pe.matmul(ps, xnT[:, k, sl(t)], w[:, k, col:col + D], start=(k == 0), stop=(k == KC - 1))
                    return last

                def kv(t):
                    pe.wait_ge(s["mix_kf"], b + t + 1)
                    pe.wait_ge(s["mix_v"], b + t + 1)
                    for j in range(KC):
                        last = pe.matmul(kvp[j][:, 0:129], kf[:, t % 2, sl(j, 128)], v[:, t % 2, j, 0:129],
                                         start=(t == 0), stop=(t == T - 1))
                    last.then_inc(s["mix_kv"], 1)

                pe.wait_ge(s["mix_weights"], 48 * (call + 1))
                for t in range(T):
                    if t >= 2:
                        pe.wait_ge(s["mix_kf"], b + t - 1)
                        pe.wait_ge(s["mix_v"], b + t - 1)
                    product(ring[t % 2][0:P, :], t, W, D).then_inc(s["mix_k_done"], 1)
                    product(ring[2 + t % 2][0:P, :], t, W, 2 * D).then_inc(s["mix_v_done"], 1)
                    if t:
                        kv(t - 1)
                kv(T - 1)

                def q_product(n):
                    j, m = n // NN, n % NN
                    if n < 4:
                        pe.wait_ge(s["mix_kf"], b + T)
                        pe.wait_ge(s["mix_v"], b + T)
                    else:
                        pe.wait_ge(s["mix_q"], U * call + n - 3)
                    for k in range(KC):
                        last = pe.matmul(ring[n % 4][:, 0:NB], W[:, k, sl(j, 128)], xnT[:, k, sl(m, NB)],
                                         start=(k == 0), stop=(k == KC - 1))
                    last.then_inc(s["mix_q_ps"], 1)

                for n in range(4):
                    q_product(n)
                for j in range(KC):
                    pe.wait_ge(s["mix_kvbd"], KC * call + j + 1)
                    pe.wait_ge(s["mix_ksb"], KC * call + j + 1)
                    pe.transpose(kvp[j][:, 0:128], kvbd[:, j, :], env.ident[:, :]).then_inc(s["mix_kvT_ps"], 1)
                for j in range(KC):
                    pe.wait_ge(s["mix_kvT"], KC * call + j + 1)
                    pe.matmul(kvp[j][:, :], kvT[:, j, :], WO[:, j, :], start=True, stop=True).then_inc(s["mix_m_ps"], 1)
                for n in range(4, U):
                    q_product(n)
                for n in range(U):
                    j, m = n // NN, n % NN
                    pe.wait_ge(s["mix_q"], U * (call + 1))
                    if n >= 4:
                        pe.wait_ge(s["mix_qs"], U * call + n - 3)
                    pe.matmul(ring[n % 4][:, 0:NB], ksb[:, j, :], qT[:, j, sl(m, NB)], start=True, stop=True)\
                      .then_inc(s["mix_den_ps"], 1)
                pe.wait_ge(s["mix_m"], KC * (call + 1))
                pe.wait_ge(s["mix_qs"], U * (call + 1))
                for t in range(T):
                    if t >= 4:
                        pe.wait_ge(s["mix_x"], b + t - 3)
                    for j in range(KC):
                        last = pe.matmul(ring[t % 4][0:P, :], qT[:, j, sl(t)], M[:, j, :], start=(j == 0), stop=(j == KC - 1))
                    last.then_inc(s["mix_y_ps"], 1)


def graph_attention(env, W_, b_, a_, cnt, s_dram):
    env.stage += 1
    nc, X, xnT = env.nc, env.X, env.xnT
    g = {n: env.sem("gat_" + n) for n in ("weights", "emb_ps", "emb", "s", "t", "s_out", "s_row", "cnt0", "cnt1", "leak", "leak2", "leak3",
                                          "exp", "num", "at", "ps", "rec", "x", "num2")}
    with ExitStack() as ctx:
        sb = lambda n, sh, d=F32: env.sb(ctx, n, sh, d)
        W = sb("gatW", [128, KC, D])
        B = sb("gatB", [P, D])
        A = sb("gatA", [P, 2 * D])
        emb = sb("emb", [P, T, D])
        junk = sb("gjunk", [P, 2, D])
        sc = sb("gs", [P, T])
        tc = sb("gt", [P, T])
        srow = sb("srow", [P, N])
        ct = sb("ct", [P, 2, TABLES, N])
        z = sb("gz", [P, 2, N])
        z2 = sb("gz2", [P, 2, N])
        AT = sb("AT", [P, T, N])
        rec = sb("grec", [P, T])
        pe_ps = env.banks(ctx, "gp", 2)
        ysum = env.banks(ctx, "gy", 2)
        rsum = env.banks(ctx, "gr", 2)
        slots = (g["cnt0"], g["cnt1"])
        with nc.Block() as block:
            @block.sync
            def _(sp):
                sp.dma_start(W[:, :, :], rows(W_)).then_inc(g["weights"], 16)
                sp.dma_start(B[:, :], bcast(b_, P, D)).then_inc(g["weights"], 16)
                sp.dma_start(A[:, :], bcast(a_.rearrange("n o -> (n o)"), P, 2 * D)).then_inc(g["weights"], 16)
                for j in range(T):
                    if j >= 2:
                        sp.wait_ge(g["num"], j - 1)
                    if j == 2:
                        sp.wait_ge(g["s"], T)
                        with nc.allow_non_contiguous_dma("1250 values, turned from columns to a row"):
                            sp.dma_start(s_dram.rearrange("(t p) -> p t", p=P), sc[:, :]).then_inc(g["s_out"], 16)
                        sp.wait_ge(g["s_out"], 16)
                        sp.dma_start(srow[:, :], bcast(s_dram, P, N)).then_inc(g["s_row"], 16)
                    for i in range(TABLES):
                        sp.dma_start(ct[:, j % 2, i, :], cnt[i][0:N * N, :].rearrange("(j s) o -> j (s o)", s=N)[sl(j), :])\
                          .then_inc(slots[j % 2], 16)

            @block.vector
            def _(dve):
                dve.wait_ge(g["weights"], 48)
                for t in range(T):
                    dve.wait_ge(g["emb_ps"], t + 1)
                    dve.tensor_tensor(emb[:, t, :], pe_ps[t % 2][0:P, :], B[:, :], ALU.add).then_inc(g["emb"], 1)
                    dve.wait_ge(g["emb"], t + 1)
                    if t:
                        dve.wait_ge(g["s"], t)
                        dve.wait_ge(g["t"], t)
                    dve.scalar_tensor_tensor(junk[:, 0, :], emb[:, t, :], 1.0, A[:, 0:D], ALU.mult, ALU.mult,
                                             accum_out=sc[:, t:t + 1]).then_inc(g["s"], 1)
                    dve.scalar_tensor_tensor(junk[:, 1, :], emb[:, t, :], 1.0, A[:, D:2 * D], ALU.mult, ALU.mult,
                                             accum_out=tc[:, t:t + 1]).then_inc(g["t"], 1)
                for j in range(2):
                    dve.wait_ge(slots[j % 2], 16 * TABLES)
                    dve.tensor_tensor(AT[:, j, :], ct[:, j % 2, 0, :], ct[:, j % 2, 1, :], ALU.add).then_inc(g["num"], 1)
                dve.wait_ge(g["s_row"], 16)
                dve.wait_ge(g["t"], T)
                for j in range(T):
                    u = j % 2
                    if j >= 2:
                        dve.wait_ge(slots[u], 16 * TABLES * (j // 2 + 1))
                        dve.tensor_tensor(AT[:, j, :], ct[:, u, 0, :], ct[:, u, 1, :], ALU.add).then_inc(g["num"], 1)
                        dve.wait_ge(g["at"], j - 1)
                    dve.tensor_scalar(z[:, u, :], srow[:, :], tc[:, j:j + 1], None, ALU.add).then_inc(g["leak"], 1)
                    dve.wait_ge(g["leak"], j + 1)
                    dve.scalar_tensor_tensor(z2[:, u, :], z[:, u, :], 0.1, z[:, u, :], ALU.mult, ALU.max).then_inc(g["leak2"], 1)
                    dve.wait_ge(g["exp"], j + 1)
                    dve.wait_ge(g["num"], j + 1)
                    dve.tensor_tensor(AT[:, j, :], AT[:, j, :], z[:, u, :], ALU.mult).then_inc(g["at"], 1)
                for t in range(T):
                    dve.wait_ge(g["ps"], t + 1)
                    dve.reciprocal(rec[:, t:t + 1], rsum[t % 2][0:P, 0:1]).then_inc(g["rec"], 1)
                    dve.wait_ge(g["rec"], t + 1)
                    dve.scalar_tensor_tensor(X[:, t, :], ysum[t % 2][0:P, :], rec[:, t:t + 1], X[:, t, :], ALU.mult, ALU.add)\
                       .then_inc(g["x"], 1)

            @block.scalar
            def _(act):
                for j in range(T):
                    act.wait_ge(g["leak2"], j + 1)
                    act.activation(z[:, j % 2, :], z2[:, j % 2, :], ACT.Exp).then_inc(g["exp"], 1)

            @block.tensor
            def _(pe):
                pe.wait_ge(g["weights"], 48)
                for t in range(T):
                    if t >= 2:
                        pe.wait_ge(g["emb"], t - 1)
                    for k in range(KC):
                        last = pe.matmul(pe_ps[t % 2][0:P, :], xnT[:, k, sl(t)], W[:, k, :], start=(k == 0), stop=(k == KC - 1))
                    last.then_inc(g["emb_ps"], 1)
                pe.wait_ge(g["emb"], T)
                for t in range(T):
                    if t == 0:
                        pe.wait_ge(g["at"], T)
                    if t >= 2:
                        pe.wait_ge(g["x"], t - 1)
                    for j in range(T):
                        pe.matmul(ysum[t % 2][0:P, :], AT[:, j, sl(t)], emb[:, j, :], start=(j == 0), stop=(j == T - 1))
                    for j in range(T):
                        last = pe.matmul(rsum[t % 2][0:P, 0:2], AT[:, j, sl(t)], env.ones[0:P, 0:2], start=(j == 0), stop=(j == T - 1))
                    last.then_inc(g["ps"], 1)


def experts(env, call, wr, w1, wv, b1, w2, b2, out=None):
    env.stage += 1
    nc, X, xnT = env.nc, env.X, env.xnT
    f = {n: env.sem("ffn_" + n) for n in ("weights", "gate_ps", "gate", "gateT_ps", "gwT", "a_ps", "act", "h", "gb_ps", "hs", "y_ps", "x",
                                          "step", "exp", "out", "gb_free")}
    U = KC * NN
    nw = 4 if call == 0 else 5


    with ExitStack() as ctx:
        sb = lambda n, sh, d=F32: env.sb(ctx, n, sh, d)
        WR = sb("WR", [128, KC, NE])
        W1 = sb("W1", [128, KC, D])
        W2 = sb("W2", [128, KC, D])
        h = sb("h", [128, KC, N])
        gwT = sb("gwT", [NE, N])
        ab = sb("ab", [128, 2, NB])
        if call == 0:
            WV = sb("WV", [128, KC, D])
            L = sb("L", [P, T, NE])
            gt = sb("gt4", [P, T, NE, NE])
            ge = sb("ge4", [P, T, NE, NE])
            mx = sb("mx", [P, T])
            msk = sb("msk", [P, T, NE])
        else:
            B1 = sb("B1", [128, KC])
            B2 = sb("B2", [NE, D])
            LT = sb("LT", [NE, N])
            wk = sb("wk", [NE, N])
            m8 = sb("m8", [NE, 8])
            mx = sb("mx", [NE, 4])
        pa = env.banks(ctx, "pa", 2)
        pg = env.banks(ctx, "pg", 3)
        py = env.banks(ctx, "py", 2)
        with nc.Block() as block:
            @block.sync
            def _(sp):
                sp.dma_start(WR[:, :, :], rows(wr)).then_inc(f["weights"], 16)
                for k in range(KC):
                    sp.dma_start(W1[:, k, :].rearrange("p (e f) -> p e f", e=NE), w1[:, sl(k, 128), :].rearrange("e p f -> p e f"))\
                      .then_inc(f["weights"], 16)
                sp.dma_start(W2[:, :, :], rows(w2.rearrange("e f d -> (e f) d"))).then_inc(f["weights"], 16)
                if call == 0:
                    for k in range(KC):
                        sp.dma_start(WV[:, k, :].rearrange("p (e f) -> p e f", e=NE), wv[:, sl(k, 128), :].rearrange("e p f -> p e f"))\
                          .then_inc(f["weights"], 16)
                else:
                    with nc.allow_non_contiguous_dma("a bias of 512 values as columns"):
                        sp.dma_start(B1[:, :], b1.rearrange("e f -> (e f)").rearrange("(k p) -> p k", p=128)).then_inc(f["weights"], 16)
                    sp.dma_start(B2[:, :], b2).then_inc(f["weights"], 16)
                if out is not None:
                    for t in range(T):
                        sp.wait_ge(f["x"], T * call + t + 1)
                        sp.dma_start(out[sl(t), :], X[:, t, :]).then_inc(f["out"], 16)
                    sp.wait_ge(f["out"], 16 * T)
            W_READY = 16 * 10 if call == 0 else 16 * (10 + 8)

            @block.vector
            def _(dve):
                n0 = 0 if call == 0 else 9
                count = [n0]

                def step(ins):
                    ins.then_inc(f["step"], 1)
                    count[0] += 1
                    dve.wait_ge(f["step"], count[0])

                dve.wait_ge(f["gate_ps"], call + 1)
                if call == 0:
                    step(dve.tensor_copy(L[:, :, :], pg[2][0:P, 0:T * NE].rearrange("p (t e) -> p t e", e=NE)))
                    other = L[:, :, :].unsqueeze(2).to_broadcast([P, T, NE, NE])
                    own = L[:, :, :].unsqueeze(3).to_broadcast([P, T, NE, NE])
                    dve.tensor_tensor(gt[:, :, :, :], other, own, ALU.is_gt)
                    step(dve.tensor_tensor(ge[:, :, :, :], other, own, ALU.is_equal))
                    step(dve.tensor_tensor(ge[:, :, :, :], ge[:, :, :, :],
                                           env.tri[0:P, :, :].unsqueeze(1).to_broadcast([P, T, NE, NE]), ALU.mult))
                    step(dve.tensor_tensor(gt[:, :, :, :], gt[:, :, :, :], ge[:, :, :, :], ALU.add))
                    step(dve.tensor_reduce(msk[:, :, :], gt[:, :, :, :], AX.X, ALU.add))
                    dve.tensor_scalar(msk[:, :, :], msk[:, :, :], 2.0, None, ALU.is_lt)
                    step(dve.tensor_reduce(mx[:, :], L[:, :, :], AX.X, ALU.max))
                    dve.tensor_tensor(L[:, :, :], L[:, :, :], mx[:, :].unsqueeze(2).to_broadcast([P, T, NE]), ALU.subtract)\
                       .then_inc(f["gate"], 1)
                    dve.wait_ge(f["exp"], 1)
                    step(dve.tensor_tensor(L[:, :, :], L[:, :, :], msk[:, :, :], ALU.mult))
                    step(dve.tensor_reduce(mx[:, :], L[:, :, :], AX.X, ALU.add))
                    step(dve.reciprocal(mx[:, :], mx[:, :]))
                    dve.tensor_tensor(L[:, :, :], L[:, :, :], mx[:, :].unsqueeze(2).to_broadcast([P, T, NE]), ALU.mult)\
                       .then_inc(f["gate"], 1)
                else:
                    for m in range(3):
                        w = min(2 * NB, N - m * 2 * NB)
                        last = dve.tensor_copy(LT[:, m * 2 * NB:m * 2 * NB + w], pg[m][0:NE, 0:w])
                        step(last)
                    step(dve.tensor_reduce(mx[:, 0:1], LT[:, :], AX.X, ALU.max))
                    dve.tensor_scalar(mx[:, 1:2], mx[:, 0:1], -1.0, None, ALU.mult).then_inc(f["gate"], 1)
                    dve.wait_ge(f["exp"], 2)
                    step(dve.reciprocal(mx[:, 3:4], mx[:, 2:3]))
                    step(dve.tensor_scalar(LT[:, :], LT[:, :], mx[:, 3:4], None, ALU.mult))
                    for r in range(CAP // 8):
                        cur = LT if r == 0 else wk
                        step(dve.max(m8[:, :], cur[:, :]))
                        step(dve.match_replace(wk[:, :], m8[:, :], cur[:, :], -1.0))
                    step(dve.tensor_tensor(wk[:, :], wk[:, :], LT[:, :], ALU.not_equal))
                    dve.tensor_tensor(gwT[:, :], LT[:, :], wk[:, :], ALU.mult).then_inc(f["gwT"], 1)
                if call == 0:
                    for n in range(U):
                        j, m = n % KC, n // KC
                        dve.wait_ge(f["act"], n + 1)
                        dve.tensor_tensor(h[:, j, sl(m, NB)], pa[n % 2][:, NB:2 * NB], ab[:, n % 2, :], ALU.mult).then_inc(f["h"], 1)
                for n in range(U):
                    j, m = n % KC, n // KC
                    dve.wait_ge(f["gb_ps"], U * call + n + 1)
                    if call == 0:
                        dve.wait_ge(f["h"], n + 1)
                    else:
                        dve.wait_ge(f["act"], U + n + 1)
                    dve.tensor_tensor(h[:, j, sl(m, NB)], h[:, j, sl(m, NB)], pg[n % 2][:, 0:NB], ALU.mult).then_inc(f["hs"], 1)
                for t in range(T):
                    dve.wait_ge(f["y_ps"], T * call + t + 1)
                    dve.tensor_tensor(X[:, t, :], X[:, t, :], py[t % 2][0:P, :], ALU.add).then_inc(f["x"], 1)

            @block.scalar
            def _(act):
                act.wait_ge(f["gate"], 1 if call == 0 else 3)
                if call == 0:
                    act.activation(L[:, :, :], L[:, :, :], ACT.Exp).then_inc(f["exp"], 1)
                    for n in range(U):
                        act.wait_ge(f["a_ps"], n + 1)
                        if n >= 2:
                            act.wait_ge(f["h"], n - 1)
                        act.activation(ab[:, n % 2, :], pa[n % 2][:, 0:NB], ACT.Silu).then_inc(f["act"], 1)
                    for m in range(3):
                        w = min(4, T - 4 * m)
                        act.wait_ge(f["gateT_ps"], m + 1)
                        act.activation(gwT[:, m * 4 * P:(m * 4 + w) * P], pg[m][0:NE, 0:w * P], ACT.Copy).then_inc(f["gwT"], 1)
                else:
                    act.activation(LT[:, :], LT[:, :], ACT.Exp, bias=mx[:, 1:2], accum_out=mx[:, 2:3]).then_inc(f["exp"], 1)
                    act.wait_ge(f["weights"], W_READY)
                    for n in range(U):
                        j, m = n % KC, n // KC
                        act.wait_ge(f["a_ps"], U + n + 1)
                        act.activation(h[:, j, sl(m, NB)], pa[n % 2][:, 0:NB], ACT.Gelu, bias=B1[:, j:j + 1]).then_inc(f["act"], 1)

            @block.tensor
            def _(pe):
                pe.wait_ge(f["weights"], W_READY)
                if call == 0:
                    for t in range(T):
                        for k in range(KC):
                            last = pe.matmul(pg[2][0:P, t * NE:(t + 1) * NE], xnT[:, k, sl(t)], WR[:, k, :],
                                             start=(k == 0), stop=(k == KC - 1))
                    last.then_inc(f["gate_ps"], 1)
                else:
                    for m in range(NN):
                        for k in range(KC):
                            last = pe.matmul(pg[m // 2][0:NE, (m % 2) * NB:(m % 2 + 1) * NB], WR[:, k, :], xnT[:, k, sl(m, NB)],
                                             start=(k == 0), stop=(k == KC - 1))
                    last.then_inc(f["gate_ps"], 1)
                for n in range(U):
                    j, m = n % KC, n // KC
                    if n >= 2:
                        pe.wait_ge(f["act"], U * call + n - 1)
                        if call == 0:
                            pe.wait_ge(f["h"], n - 1)
                    for i, w in enumerate((W1, WV) if call == 0 else (W1,)):
                        for k in range(KC):
                            last = pe.matmul(pa[n % 2][:, sl(i, NB)], w[:, k, sl(j, 128)], xnT[:, k, sl(m, NB)],
                                             start=(k == 0), stop=(k == KC - 1))
                    last.then_inc(f["a_ps"], 1)
                if call == 0:
                    pe.wait_ge(f["gate"], 2)
                    for m in range(3):
                        for i in range(min(4, T - 4 * m)):
                            last = pe.transpose(pg[m][0:NE, sl(i)], L[:, 4 * m + i, :], env.ident[0:P, 0:P])
                        last.then_inc(f["gateT_ps"], 1)
                pe.wait_ge(f["gwT"], 3 if call == 0 else 4)
                for n in range(U):
                    j, m = n % KC, n // KC
                    if n >= 2:
                        pe.wait_ge(f["hs"], U * call + n - 1)
                    pe.matmul(pg[n % 2][:, 0:NB], env.sel[:, j, :], gwT[:, sl(m, NB)], start=True, stop=True).then_inc(f["gb_ps"], 1)
                pe.wait_ge(f["hs"], U * (call + 1))
                for t in range(T):
                    if t >= 2:
                        pe.wait_ge(f["x"], T * call + t - 1)
                    for j in range(KC):
                        last = pe.matmul(py[t % 2][0:P, :], h[:, j, sl(t)], W2[:, j, :], start=(j == 0),
                                         stop=(j == KC - 1 and call == 0))
                    if call == 1:
                        last = pe.matmul(py[t % 2][0:P, :], gwT[:, sl(t)], B2[:, :], start=False, stop=True)
                    last.then_inc(f["y_ps"], 1)



class NodeMlp:

    def __init__(self, env, ctx, call, tag, hs=None):
        self.env, self.call = env, call
        sb = lambda n, sh: env.sb(ctx, tag + n, sh)
        self.hs, self.hT = hs or sb("hs", [P, T, D]), sb("hT", [128, KC, N])
        self.ssq, self.sd, self.rs, self.junk = sb("ssq", [P, T]), sb("sd", [P, T]), sb("rs", [P, T]), sb("sq", [P, 2, D])
        self.G, self.BE, self.W2 = sb("G", [128, KC]), sb("BE", [128, KC]), sb("W2", [128, KC, D])
        self.pt, self.py = env.banks(ctx, tag + "pt", 2), env.banks(ctx, tag + "py", 2)
        self.s = {n: env.sem("mlp_" + n) for n in ("hs", "sq", "var", "std", "rstd", "xh", "tr", "relu", "y", "used")}
        self.b = T * call

    def act(self, act):
        s, b = self.s, self.b
        for t in range(T):
            act.wait_ge(s["hs"], b + t + 1)
            if t >= 2:
                act.wait_ge(s["sq"], b + t - 1)
            act.activation(self.junk[:, t % 2, :], self.hs[:, t, :], ACT.Square, accum_out=self.ssq[:, t:t + 1]).then_inc(s["sq"], 1)
        act.wait_ge(s["sq"], b + T)
        act.activation(self.sd[:, :], self.ssq[:, :], ACT.Sqrt, scale=1.0 / D, bias=self.env.eps[0:P, 0:1]).then_inc(s["std"], 1)
        for t in range(T):
            act.wait_ge(s["tr"], b + t + 1)
            for k in range(KC):
                last = act.activation(self.hT[:, k, sl(t)], self.pt[t % 2][:, sl(k)], ACT.Relu,
                                      scale=self.G[:, k:k + 1], bias=self.BE[:, k:k + 1])
            last.then_inc(s["relu"], 1)

    def dve(self, dve):
        s, b = self.s, self.b
        dve.wait_ge(s["std"], self.call + 1)
        dve.reciprocal(self.rs[:, :], self.sd[:, :]).then_inc(s["rstd"], 1)
        dve.wait_ge(s["rstd"], self.call + 1)
        for t in range(T):
            dve.tensor_scalar(self.hs[:, t, :], self.hs[:, t, :], self.rs[:, t:t + 1], None, ALU.mult).then_inc(s["xh"], 1)

    def pe(self, pe):
        s, b = self.s, self.b
        for t in range(T):
            pe.wait_ge(s["xh"], b + t + 1)
            if t >= 2:
                pe.wait_ge(s["relu"], b + t - 1)
            for k in range(KC):
                last = pe.transpose(self.pt[t % 2][:, sl(k)], self.hs[:, t, sl(k, 128)], self.env.ident[0:P, 0:P])
            last.then_inc(s["tr"], 1)
        for t in range(T):
            pe.wait_ge(s["relu"], b + t + 1)
            if t >= 2:
                pe.wait_ge(s["used"], b + t - 1)
            for k in range(KC):
                last = pe.matmul(self.py[t % 2][0:P, :], self.hT[:, k, sl(t)], self.W2[:, k, :], start=(k == 0), stop=(k == KC - 1))
            last.then_inc(s["y"], 1)


def centre(dve, step, w, nk, m, parts):
    step(dve.tensor_reduce(m[0:parts, 0:nk], w, AX.X, ALU.add))
    step(dve.tensor_scalar(m[0:parts, 0:nk], m[0:parts, 0:nk], 1.0 / D, None, ALU.mult))
    for k in range(nk):
        last = dve.tensor_scalar(w[:, k, :], w[:, k, :], m[0:parts, k:k + 1], None, ALU.subtract)
    step(last)


def node_tables(env, w, tab):
    env.stage += 1
    nc, X, XN, xnT = env.nc, env.X, env.XN, env.xnT
    f = {n: env.sem("tab_" + n) for n in ("weights", "step", "xres", "ps", "row", "qrow", "qprod", "qb", "q")}
    slot = [env.sem(f"tab_stored{i}") for i in range(4)]
    with ExitStack() as ctx:
        sb = lambda n, sh, d=F32: env.sb(ctx, n, sh, d)
        WK, WV, WQ = sb("tWK", [128, 5, D]), sb("tWV", [128, 5, D]), sb("tWQ", [128, KC, D])
        BK, BV, BQ = sb("tBK", [P, 1, D]), sb("tBV", [P, 1, D]), sb("tBQ", [P, 1, D])
        B2Q, B2K = sb("tB2Q", [P, D]), sb("tB2K", [P, D])
        m = sb("tm", [128, 8])
        row = sb("trow", [P, 4, QW])
        prod = sb("tprod", [P, D])
        pp = env.banks(ctx, "pp", 4)
        mlp = NodeMlp(env, ctx, 0, "q")
        with nc.Block() as block:
            @block.sync
            def _(sp):
                loads = [(WK[:, :, :], rows(w["hk_W1"])), (WV[:, :, :], rows(w["hv_W1"])), (WQ[:, :, :], rows(w["hq_W1"])),
                         (BK[:, 0, :], bcast(w["hk_b1"], P, D)), (BV[:, 0, :], bcast(w["hv_b1"], P, D)),
                         (BQ[:, 0, :], bcast(w["hq_b1"], P, D)), (B2Q[:, :], bcast(w["hq_b2"], P, D)),
                         (B2K[:, :], bcast(w["hk_b2"], P, D)), (mlp.W2[:, :, :], rows(w["hq_W2"]))]
                for to, a in loads:
                    sp.dma_start(to, a).then_inc(f["weights"], 16)
                with nc.allow_non_contiguous_dma("512 values as columns"):
                    for to, a in ((mlp.G, "hq_g"), (mlp.BE, "hq_be")):
                        sp.dma_start(to[:, :], w[a].rearrange("(k p) -> p k", p=128)).then_inc(f["weights"], 16)
                for n in range(3 * T):
                    t = n % T
                    if n < 2 * T:
                        sp.wait_ge(f["row"], n + 1)
                        sp.dma_start(tab["k" if n < T else "v"][sl(t), :], row[:, n % 4, 0:D]).then_inc(slot[n % 4], 16)
                    else:
                        sp.wait_ge(f["q"], t + 1)
                        sp.dma_start(tab["q"][sl(t), :], row[:, n % 4, :]).then_inc(slot[n % 4], 16)
                for i in range(4):
                    sp.wait_ge(slot[i], 16 * len(range(i, 3 * T, 4)))

            @block.vector
            def _(dve):
                n_step = [0]

                def step(ins):
                    ins.then_inc(f["step"], 1)
                    n_step[0] += 1
                    dve.wait_ge(f["step"], n_step[0])

                for t in range(T):
                    dve.tensor_tensor(X[:, t, :], X[:, t, :], XN[:, t, :], ALU.add).then_inc(f["xres"], 1)
                dve.wait_ge(f["weights"], 16 * 11)
                centre(dve, step, WK[:, :, :], 5, m, 128)
                centre(dve, step, WV[:, :, :], 5, m, 128)
                centre(dve, step, WQ[:, :, :], KC, m, 128)
                for b in (BK, BV, BQ):
                    centre(dve, step, b[:, :, :], 1, m, P)
                dve.tensor_copy(env.W1E["k"][:, :], WK[:, KC, :])
                step(dve.tensor_copy(env.W1E["v"][:, :], WV[:, KC, :]))
                for n in range(3 * T):
                    dve.wait_ge(f["ps"], n + 1)
                    if n < 2 * T:
                        if n >= 4:
                            dve.wait_ge(slot[n % 4], 16 * (n // 4))
                        dve.tensor_tensor(row[:, n % 4, 0:D], pp[n % 4][0:P, :], (BK if n < T else BV)[:, 0, :], ALU.add)\
                           .then_inc(f["row"], 1)
                    else:
                        dve.tensor_tensor(mlp.hs[:, n - 2 * T, :], pp[n % 4][0:P, :], BQ[:, 0, :], ALU.add).then_inc(mlp.s["hs"], 1)
                mlp.dve(dve)
                for t in range(T):
                    n = 2 * T + t
                    r = row[:, n % 4, :]
                    dve.wait_ge(mlp.s["y"], t + 1)
                    dve.wait_ge(slot[n % 4], 16 * (n // 4))
                    dve.tensor_tensor(r[:, 0:D], mlp.py[t % 2][0:P, :], B2Q[:, :], ALU.add).then_inc(mlp.s["used"], 1)
                    dve.wait_ge(mlp.s["used"], t + 1)
                    dve.tensor_tensor(prod[:, :], r[:, 0:D], B2K[:, :], ALU.mult).then_inc(f["qprod"], 1)
                    dve.wait_ge(f["qprod"], t + 1)
                    dve.tensor_reduce(r[:, D:QW], prod[:, :].rearrange("p (h d) -> p h d", h=NH), AX.X, ALU.add).then_inc(f["qb"], 1)
                    dve.wait_ge(f["qb"], t + 1)
                    dve.tensor_scalar(r, r, float(HD) ** -0.5, None, ALU.mult).then_inc(f["q"], 1)

            @block.scalar
            def _(act):
                mlp.act(act)

            @block.tensor
            def _(pe):
                pe.wait_ge(f["step"], 3 * 3 + 3 * 3 + 1)
                for n in range(3 * T):
                    t, wt = n % T, (WK, WV, WQ)[n // T]
                    if n >= 4:
                        if n - 4 < 2 * T:
                            pe.wait_ge(f["row"], n - 3)
                        else:
                            pe.wait_ge(mlp.s["hs"], n - 3 - 2 * T)
                    for k in range(KC):
                        last = pe.matmul(pp[n % 4][0:P, :], xnT[:, k, sl(t)], wt[:, k, :], start=(k == 0), stop=(k == KC - 1))
                    last.then_inc(f["ps"], 1)
                mlp.pe(pe)


UN = 4
J0, J1 = 1, 41


def at(j, u, d):
    q, r = divmod(u + d, UN)
    return j + q, r


def chunks(eng, step, last):
    for c in range(UN * J0):
        step(*divmod(c, UN))
    with eng.Fori(J0, J1) as j:
        for u in range(UN):
            step(j, u)
    for c in range(UN * J1, last + 1):
        step(*divmod(c, UN))


def edge_pass(env, mode, edge_attr, tab, w, dst, agg):
    env.stage += 1
    nc = env.nc
    V = mode == "v"
    ci = 1 if V else 0
    b = CH * ci
    names = ("efT_ps", "efT", "h_ps", "hs", "sq", "std", "rstd", "xh", "tr", "relu", "y", "prod", "red", "logit",
             "wv", "sz", "tot_ps", "tot", "weights")
    f = {n: env.sem("edge_" + n) for n in names}
    ring = lambda n: [env.sem(f"edge_{n}{i}") for i in range(UN)]
    ef_in, g_in, q_in, d_in, sc_out = ring("attr_loaded"), ring("hidden_gathered"), ring("q_gathered"), ring("dst_loaded"), ring("scattered")
    uses = [len(range(u, CH, UN)) for u in range(UN)]

    def loaded(j, u, both=True):
        return 16 * (j + 1 + (uses[u] * ci if both else 0))

    with ExitStack() as ctx:
        sb = lambda n, sh, d=F32: env.sb(ctx, n, sh, d)
        W2 = sb("eW2", [128, KC, D])
        G, BE = sb("eG", [128, KC]), sb("eBE", [128, KC])
        ef = sb("ef", [P, UN, EF])
        efT = sb("efT", [128, 2, P])
        hg = sb("hg", [P, UN, D])
        hs = sb("ehs", [P, 2, D])
        sq = sb("esq", [P, D])
        ssq, sd, rs = sb("essq", [P, UN]), sb("esd", [P, UN]), sb("ers", [P, UN])
        xh = sb("exh", [P, 2, D])
        rT = sb("erT", [128, 2, KC, P])
        if V:
            wv = sb("ewv", [P, 2, D])
            dr = sb("edr", [P, UN, P], I32)
            S, Z = sb("eS", [P, 2, P]), sb("eZ", [P, 2, P])
            tot = sb("etot", [P, UN, QW])
        else:
            qg = sb("eqg", [P, UN, QW])
            prod, red = sb("eprod", [P, D]), sb("ered", [P, NH])
        pe_ef, pe_h = env.banks(ctx, "pef", 1)[0], env.banks(ctx, "peh", 1)[0]
        pt, py = env.banks(ctx, "pet", 2), env.banks(ctx, "pey", 2)
        if V:
            po, pd = env.banks(ctx, "peo", 1)[0], env.banks(ctx, "ped", 1)[0]
        W1E = env.W1E[mode]
        with nc.Block() as block:
            @block.sync
            def _(sp):
                sp.dma_start(W2[:, :, :], rows(w[f"h{mode}_W2"])).then_inc(f["weights"], 16)
                with nc.allow_non_contiguous_dma("512 values as columns"):
                    sp.dma_start(G[:, :], w[f"h{mode}_g"].rearrange("(k p) -> p k", p=128)).then_inc(f["weights"], 16)
                    sp.dma_start(BE[:, :], w[f"h{mode}_be"].rearrange("(k p) -> p k", p=128)).then_inc(f["weights"], 16)

                for c in range(CH):
                    u = c % UN
                    if c >= UN:
                        sp.wait_ge(f["efT_ps"], b + c - UN + 1)
                    sp.dma_start(ef[:, u, :], edge_attr[sl(c), :]).then_inc(ef_in[u], 16)
                    if V:
                        if c >= UN:
                            sp.wait_ge(f["sz"], c - UN + 1)
                        sp.dma_start(dr[:, u, :], bcast(dst[sl(c)], P, P)).then_inc(d_in[u], 16)

            @block.gpsimd
            def _(g):
                for c in range(CH + 7):
                    if c < CH:
                        u = c % UN
                        if c >= UN:
                            g.wait_ge(f["hs"], b + c - UN + 1)
                        g.indirect_dma_start(out=hg[:, u, :], out_offset=None, in_=tab[mode][:, :],
                                             in_offset=bass.IndirectOffsetOnAxis(ap=env.srci[:, c:c + 1], axis=0))\
                         .then_inc(g_in[u], 16)
                        if not V:
                            if c >= UN:
                                g.wait_ge(f["logit"], c - UN + 1)
                            g.indirect_dma_start(out=qg[:, u, :], out_offset=None, in_=tab["q"][:, :],
                                                 in_offset=bass.IndirectOffsetOnAxis(ap=env.dsti[:, c:c + 1], axis=0))\
                             .then_inc(q_in[u], 16)
                    if V and c >= 7:
                        x = c - 7
                        g.wait_ge(f["tot"], x + 1)
                        g.indirect_dma_start(out=agg[:, :], out_offset=bass.IndirectOffsetOnAxis(ap=env.scati[:, x:x + 1], axis=0),
                                             in_=tot[:, x % UN, :], in_offset=None, bounds_check=N - 1, oob_is_err=False)\
                         .then_inc(sc_out[x % UN], 16)
                if V:
                    for u in range(UN):
                        g.wait_ge(sc_out[u], 16 * uses[u])

            @block.vector
            def _(dve):
                def add(j, u):
                    c = UN * j + u
                    dve.wait_ge(f["h_ps"], b + c + 1)
                    dve.wait_ge(g_in[u], loaded(j, u))
                    if not (isinstance(c, int) and c < 2):
                        dve.wait_ge(f["sq"], b + c - 1)
                        dve.wait_ge(f["xh"], b + c - 1)
                    dve.tensor_tensor(hs[:, u % 2, :], pe_h[0:P, :], hg[:, u, :], ALU.add).then_inc(f["hs"], 1)

                def normalise(j, u):
                    c = UN * j + u
                    dve.wait_ge(f["std"], b + c + 1)
                    dve.reciprocal(rs[:, u:u + 1], sd[:, u:u + 1]).then_inc(f["rstd"], 1)
                    if not (isinstance(c, int) and c < 2):
                        dve.wait_ge(f["tr"], b + c - 1)
                    dve.wait_ge(f["rstd"], b + c + 1)
                    dve.tensor_scalar(xh[:, u % 2, :], hs[:, u % 2, :], rs[:, u:u + 1], None, ALU.mult).then_inc(f["xh"], 1)

                def logits(j, u):
                    c = UN * j + u
                    dve.wait_ge(f["y"], c + 1)
                    dve.wait_ge(q_in[u], loaded(j, u, False))
                    if not (isinstance(c, int) and c < 1):
                        dve.wait_ge(f["red"], c)
                    dve.tensor_tensor(prod[:, :], py[u % 2][0:P, :], qg[:, u, 0:D], ALU.mult).then_inc(f["prod"], 1)
                    dve.wait_ge(f["prod"], c + 1)
                    if not (isinstance(c, int) and c < 1):
                        dve.wait_ge(f["logit"], c)
                    dve.tensor_reduce(red[:, :], prod[:, :].rearrange("p (h d) -> p h d", h=NH), AX.X, ALU.add).then_inc(f["red"], 1)
                    dve.wait_ge(f["red"], c + 1)
                    dve.tensor_tensor(env.L[:, bass.ds(c * NH, NH)], red[:, :], qg[:, u, D:QW], ALU.add).then_inc(f["logit"], 1)

                def weigh(j, u):
                    c = UN * j + u
                    dve.wait_ge(f["y"], b + c + 1)
                    if not (isinstance(c, int) and c < 2):
                        dve.wait_ge(f["tot_ps"], c - 1)
                    dve.tensor_tensor(wv[:, u % 2, :].rearrange("p (h d) -> p h d", h=NH),
                                      py[u % 2][0:P, :].rearrange("p (h d) -> p h d", h=NH),
                                      env.L[:, bass.ds(c * NH, NH)].unsqueeze(2).to_broadcast([P, NH, HD]), ALU.mult)\
                       .then_inc(f["wv"], 1)
                    dve.wait_ge(d_in[u], loaded(j, u, False))
                    dve.tensor_scalar(S[:, u % 2, :], dr[:, u, :], env.dstf[:, bass.ds(c, 1)], None, ALU.is_equal)
                    dve.tensor_scalar(Z[:, u % 2, :], dr[:, u, :], env.prevf[:, bass.ds(c, 1)], None, ALU.is_equal).then_inc(f["sz"], 1)

                def step(j, u):
                    c = UN * j + u
                    static = isinstance(c, int)
                    if not static or c < CH:
                        add(j, u)
                    if not static or 0 <= c - 2 < CH:
                        (weigh if V else logits)(*at(j, u, -2))
                    if not static or c < CH:
                        normalise(j, u)
                chunks(dve, step, CH + 1)

            @block.scalar
            def _(act):
                def copy_ef(j, u):
                    c = UN * j + u
                    act.wait_ge(f["efT_ps"], b + c + 1)
                    if not (isinstance(c, int) and c < 2):
                        act.wait_ge(f["h_ps"], b + c - 1)
                    act.activation(efT[:, u % 2, :], pe_ef[:, 0:P], ACT.Copy).then_inc(f["efT"], 1)

                def deviation(j, u):
                    c = UN * j + u
                    act.wait_ge(f["hs"], b + c + 1)
                    act.activation(sq[:, :], hs[:, u % 2, :], ACT.Square, accum_out=ssq[:, u:u + 1]).then_inc(f["sq"], 1)
                    act.wait_ge(f["sq"], b + c + 1)
                    act.activation(sd[:, u:u + 1], ssq[:, u:u + 1], ACT.Sqrt, scale=1.0 / D, bias=env.eps[0:P, 0:1])\
                       .then_inc(f["std"], 1)

                def relu(j, u):
                    c = UN * j + u
                    act.wait_ge(f["tr"], b + c + 1)
                    if not (isinstance(c, int) and c < 2):
                        act.wait_ge(f["y"], b + c - 1)
                    for k in range(KC):
                        last = act.activation(rT[:, u % 2, k, :], pt[u % 2][:, sl(k)], ACT.Relu, scale=G[:, k:k + 1], bias=BE[:, k:k + 1])
                    last.then_inc(f["relu"], 1)

                def total(j, u):
                    c = UN * j + u
                    act.wait_ge(f["tot_ps"], c + 1)
                    if not (isinstance(j, int) and j == 0):
                        act.wait_ge(sc_out[u], 16 * j)
                    act.activation(tot[:, u, 0:D], po[0:P, :], ACT.Copy)
                    act.activation(tot[:, u, D:QW], pd[0:P, 0:NH], ACT.Copy).then_inc(f["tot"], 1)

                act.wait_ge(f["weights"], 48 * (ci + 1))
                copy_ef(0, 0)

                def step(j, u):
                    c = UN * j + u
                    static = isinstance(c, int)
                    if not static or c + 1 < CH:
                        copy_ef(*at(j, u, 1))
                    if not static or c < CH:
                        deviation(j, u)
                    if V and (not static or 0 <= c - 3 < CH):
                        total(*at(j, u, -3))
                    if not static or 0 <= c - 1 < CH:
                        relu(*at(j, u, -1))
                chunks(act, step, CH + 2)

            @block.tensor
            def _(pe):
                def flip_ef(j, u):
                    c = UN * j + u
                    pe.wait_ge(ef_in[u], loaded(j, u))
                    if not (isinstance(c, int) and c < 1):
                        pe.wait_ge(f["efT"], b + c)
                    pe.transpose(pe_ef[:, 0:P], ef[:, u, :], env.ident[0:P, 0:P]).then_inc(f["efT_ps"], 1)

                def hidden(j, u):
                    c = UN * j + u
                    pe.wait_ge(f["efT"], b + c + 1)
                    if not (isinstance(c, int) and c < 1):
                        pe.wait_ge(f["hs"], b + c)
                    pe.matmul(pe_h[0:P, :], efT[:, u % 2, :], W1E[:, :], start=True, stop=True).then_inc(f["h_ps"], 1)

                def flip_xh(j, u):
                    c = UN * j + u
                    pe.wait_ge(f["xh"], b + c + 1)
                    if not (isinstance(c, int) and c < 2):
                        pe.wait_ge(f["relu"], b + c - 1)
                    for k in range(KC):
                        last = pe.transpose(pt[u % 2][:, sl(k)], xh[:, u % 2, sl(k, 128)], env.ident[0:P, 0:P])
                    last.then_inc(f["tr"], 1)

                def product(j, u):
                    c = UN * j + u
                    pe.wait_ge(f["relu"], b + c + 1)
                    if not (isinstance(c, int) and c < 2):
                        pe.wait_ge(f["wv" if V else "prod"], c - 1)
                    for k in range(KC):
                        last = pe.matmul(py[u % 2][0:P, :], rT[:, u % 2, k, :], W2[:, k, :], start=(k == 0), stop=(k == KC - 1))
                    last.then_inc(f["y"], 1)

                def total(j, u):
                    c = UN * j + u
                    first = isinstance(c, int) and c == 0
                    pe.wait_ge(f["wv"], c + 1)
                    pe.wait_ge(f["sz"], c + 1)
                    if not first:
                        pe.wait_ge(f["tot"], c)
                    pv = (u - 1) % UN
                    pe.matmul(po[0:P, :], S[:, u % 2, :], wv[:, u % 2, :], start=True, stop=first)
                    last = pe.matmul(pd[0:P, 0:NH], S[:, u % 2, :], env.L[:, bass.ds(c * NH, NH)], start=True, stop=first)
                    if not first:
                        pe.matmul(po[0:P, :], Z[:, u % 2, :], tot[:, pv, 0:D], start=False, stop=True)
                        last = pe.matmul(pd[0:P, 0:NH], Z[:, u % 2, :], tot[:, pv, D:QW], start=False, stop=True)
                    last.then_inc(f["tot_ps"], 1)

                pe.wait_ge(f["weights"], 48 * (ci + 1))
                flip_ef(0, 0)

                def step(j, u):
                    c = UN * j + u
                    static = isinstance(c, int)
                    if not static or c + 1 < CH:
                        flip_ef(*at(j, u, 1))
                    if not static or c < CH:
                        hidden(j, u)
                    if not static or 0 <= c - 1 < CH:
                        flip_xh(*at(j, u, -1))
                    if not static or 0 <= c - 2 < CH:
                        product(*at(j, u, -2))
                    if V and (not static or 0 <= c - 3 < CH):
                        total(*at(j, u, -3))
                chunks(pe, step, CH + 2)


def segment_exp(env, dst):
    nc, L = env.nc, env.L
    R = SB_ * NH
    f = {n: env.sem("seg_" + n) for n in ("dst", "pad", "flag", "lt_ps", "lt", "step", "row_ps", "row", "col_ps", "col", "m", "m_ps", "sub", "exp")}
    Lb = L[:, :].rearrange("p (b i h) -> p i b h", b=SB_, h=NH)
    with ExitStack() as ctx:
        sb = lambda n, sh, d=F32: env.sb(ctx, n, sh, d)
        DD = sb("sDD", [R, BE + 2], I32)
        fl = sb("sfl", [R, BE + 1])
        LT = sb("sLT", [R, BE])
        F = sb("sF", [R, BE])
        B = sb("sB", [R, BE])
        Lc = sb("sLc", [P, 2, SB_, NH])
        fn = sb("sfn", [R, 4])
        row = sb("srow4", [1, 4, SB_, NH])
        ini = sb("sini", [1, 2, SB_, NH])
        col = sb("scol", [R, 2])
        tmp = sb("stmp", [1, 2, NH])
        pl = env.banks(ctx, "spl", 2)
        pr = env.banks(ctx, "spr", 2)
        pm = env.banks(ctx, "spm", 2)
        with nc.Block() as block:
            @block.sync
            def _(sp):
                sp.wait_ge(f["pad"], 1)
                for k in range(SB_):
                    lo, hi = max(0, k * BE - 1), min(E, (k + 1) * BE + 1)
                    at0 = 1 if k == 0 else 0
                    sp.dma_start(DD[k * NH:(k + 1) * NH, at0:at0 + hi - lo], bcast(dst[lo:hi], NH, hi - lo)).then_inc(f["dst"], 16)

            @block.tensor
            def _(pe):
                for i in range(BC):
                    q, r = divmod(i, 4)
                    pe.wait_ge(f["step"], i + 1)
                    if r == 0 and q >= 2:
                        pe.wait_ge(f["lt"], q - 1)
                    last = pe.transpose(pl[q % 2][0:R, sl(r)], Lc[:, i % 2, :, :].rearrange("p b h -> p (b h)"), env.ident[0:P, 0:P])
                    last.then_inc(f["lt_ps"], 1)
                pe.wait_ge(f["flag"], 6)
                for n, c in enumerate((F[:, BE - 1:BE], B[:, 0:1], fn[:, 0:1], fn[:, 1:2])):
                    last = pe.transpose(pr[0][0:1, n * R:(n + 1) * R], c, env.ident[0:R, 0:R])
                last.then_inc(f["row_ps"], 1)
                pe.wait_ge(f["row"], 1)
                for n in range(2):
                    last = pe.transpose(pr[1][0:R, n:n + 1], ini[0:1, n, :, :].rearrange("o b h -> o (b h)"), env.ident[0:1, 0:1])
                last.then_inc(f["col_ps"], 1)
                pe.wait_ge(f["m"], 1)
                for i in range(BC):
                    q, r = divmod(i, 6)
                    if r == 0 and q >= 2:
                        pe.wait_ge(f["sub"], q - 1)
                    last = pe.transpose(pm[q % 2][0:P, r * R:(r + 1) * R], F[:, sl(i)], env.ident[0:R, 0:R])
                    if r == 5 or i == BC - 1:
                        last.then_inc(f["m_ps"], 1)

            @block.scalar
            def _(act):
                for i in range(BC):
                    if i >= 2:
                        act.wait_ge(f["lt_ps"], i - 1)
                    act.activation(Lc[:, i % 2, :, :], Lb[:, i, :, :], ACT.Copy).then_inc(f["step"], 1)
                    q, r = divmod(i, 4)
                    if r == 3 or i == BC - 1:
                        act.wait_ge(f["lt_ps"], i + 1)
                        act.activation(LT[:, q * 4 * P:(q * 4 + r + 1) * P], pl[q % 2][0:R, 0:(r + 1) * P], ACT.Copy).then_inc(f["lt"], 1)
                act.wait_ge(f["sub"], (BC + 5) // 6)
                act.activation(L[:, :], L[:, :], ACT.Exp).then_inc(f["exp"], 1)

            @block.vector
            def _(dve):
                n = [0]
                chain = env.sem("seg_chain")

                def step(ins):
                    ins.then_inc(chain, 1)
                    n[0] += 1
                    dve.wait_ge(chain, n[0])

                dve.memset(DD[:, :], -1).then_inc(f["pad"], 1)
                dve.wait_ge(f["dst"], 16 * SB_)
                step(dve.tensor_tensor(fl[:, :], DD[:, 1:BE + 2], DD[:, 0:BE + 1], ALU.not_equal))
                step(dve.tensor_scalar(fl[:, :], fl[:, :], -BIG, None, ALU.mult))
                dve.tensor_reduce(fn[:, 0:1], fl[:, 0:BE], AX.X, ALU.min).then_inc(f["flag"], 1)
                dve.tensor_reduce(fn[:, 1:2], fl[:, 1:BE + 1], AX.X, ALU.min).then_inc(f["flag"], 1)
                dve.wait_ge(f["lt"], (BC + 3) // 4)
                dve.tensor_tensor_scan(F[:, :], fl[:, 0:BE], LT[:, :], -BIG, ALU.add, ALU.max).then_inc(f["flag"], 1)
                dve.tensor_tensor_scan(B[:, ::-1], fl[:, BE:0:-1], LT[:, ::-1], -BIG, ALU.add, ALU.max).then_inc(f["flag"], 1)
                dve.memset(ini[:, :, :, :], -BIG).then_inc(f["flag"], 1)
                dve.memset(tmp[:, :, :], 0.0).then_inc(f["flag"], 1)
                dve.wait_ge(f["row_ps"], 1)
                step(dve.tensor_copy(row[:, :, :, :].rearrange("o n b h -> o (n b h)"), pr[0][0:1, 0:4 * R]))
                for k in range(1, SB_):
                    m = SB_ - 1 - k
                    dve.tensor_tensor(tmp[:, 0, :], row[:, 0, k - 1, :], row[:, 2, k, :], ALU.add)
                    step(dve.tensor_tensor(tmp[:, 1, :], row[:, 1, m + 1, :], row[:, 3, m, :], ALU.add))
                    dve.tensor_tensor(row[:, 0, k, :], row[:, 0, k, :], tmp[:, 0, :], ALU.max)
                    step(dve.tensor_tensor(row[:, 1, m, :], row[:, 1, m, :], tmp[:, 1, :], ALU.max))
                step(dve.tensor_copy(ini[:, 0, 1:SB_, :], row[:, 0, 0:SB_ - 1, :]))
                dve.tensor_copy(ini[:, 1, 0:SB_ - 1, :], row[:, 1, 1:SB_, :]).then_inc(f["row"], 1)
                dve.wait_ge(f["col_ps"], 1)
                step(dve.tensor_copy(col[:, :], pr[1][0:R, 0:2]))
                dve.tensor_tensor_scan(F[:, :], fl[:, 0:BE], LT[:, :], col[:, 0:1], ALU.add, ALU.max)
                step(dve.tensor_tensor_scan(B[:, ::-1], fl[:, BE:0:-1], LT[:, ::-1], col[:, 1:2], ALU.add, ALU.max))
                dve.tensor_tensor(F[:, :], F[:, :], B[:, :], ALU.max).then_inc(f["m"], 1)
                for q in range((BC + 5) // 6):
                    k = min(6, BC - 6 * q)
                    dve.wait_ge(f["m_ps"], q + 1)
                    dve.tensor_tensor(Lb[:, 6 * q:6 * q + k, :, :], Lb[:, 6 * q:6 * q + k, :, :],
                                      pm[q % 2][0:P, 0:k * R].rearrange("p (i b h) -> p i b h", i=k, b=SB_), ALU.subtract)\
                       .then_inc(f["sub"], 1)


def node_output(env, w, agg):
    env.stage += 1
    nc, X, xnT = env.nc, env.X, env.xnT
    f = {n: env.sem("out_" + n) for n in ("weights", "step", "agg", "tr", "aggT", "ps", "yb", "x")}
    with ExitStack() as ctx:
        sb = lambda n, sh, d=F32: env.sb(ctx, n, sh, d)
        W1 = sb("oW1", [128, 2 * KC, D])
        B1, B2, BV = sb("oB1", [P, 1, D]), sb("oB2", [P, D]), sb("oBV", [P, D])
        A = sb("oA", [P, T, QW])
        den, one = sb("oden", [P, T, NH]), sb("oone", [P, T, NH])
        bv = sb("obv", [P, 2, D])
        m = sb("om", [128, 8])
        aT = sb("oaT", [128, KC, N])
        yb = sb("oyb", [P, 2, D])
        pa, pp = env.banks(ctx, "opa", 2), env.banks(ctx, "opp", 2)
        mlp = NodeMlp(env, ctx, 1, "o", env.XN)
        with nc.Block() as block:
            @block.sync
            def _(sp):
                for to, a in ((W1[:, :, :], rows(w["no_W1"])), (B1[:, 0, :], bcast(w["no_b1"], P, D)), (B2[:, :], bcast(w["no_b2"], P, D)),
                              (BV[:, :], bcast(w["hv_b2"], P, D)), (mlp.W2[:, :, :], rows(w["no_W2"])),
                              (A[:, :, :], agg.rearrange("(t p) d -> p t d", p=P))):
                    sp.dma_start(to, a).then_inc(f["weights"], 16)
                with nc.allow_non_contiguous_dma("512 values as columns"):
                    for to, a in ((mlp.G, "no_g"), (mlp.BE, "no_be")):
                        sp.dma_start(to[:, :], w[a].rearrange("(k p) -> p k", p=128)).then_inc(f["weights"], 16)

            @block.vector
            def _(dve):
                n = [0]

                def step(ins):
                    ins.then_inc(f["step"], 1)
                    n[0] += 1
                    dve.wait_ge(f["step"], n[0])

                dve.wait_ge(f["weights"], 16 * 8)
                centre(dve, step, W1[:, :, :], 2 * KC, m, 128)
                centre(dve, step, B1[:, :, :], 1, m, P)
                step(dve.tensor_scalar(one[:, :, :], A[:, :, D:QW], 0.0, None, ALU.is_equal))
                step(dve.tensor_tensor(den[:, :, :], A[:, :, D:QW], one[:, :, :], ALU.add))
                dve.reciprocal(den[:, :, :], den[:, :, :])
                step(dve.tensor_scalar(one[:, :, :], one[:, :, :], -1.0, 1.0, ALU.mult, ALU.add))
                heads = lambda a: a.rearrange("p (h d) -> p h d", h=NH)
                wide = lambda a: a.unsqueeze(2).to_broadcast([P, NH, HD])
                for t in range(T):
                    a = A[:, t, 0:D]
                    dve.tensor_tensor(heads(bv[:, t % 2, :]), heads(BV[:, :]), wide(one[:, t, :]), ALU.mult)
                    step(dve.tensor_tensor(heads(a), heads(a), wide(den[:, t, :]), ALU.mult))
                    dve.tensor_tensor(a, a, bv[:, t % 2, :], ALU.add).then_inc(f["agg"], 1)
                for t in range(T):
                    dve.wait_ge(f["ps"], t + 1)
                    dve.tensor_tensor(mlp.hs[:, t, :], pp[t % 2][0:P, :], B1[:, 0, :], ALU.add).then_inc(mlp.s["hs"], 1)
                mlp.dve(dve)
                for t in range(T):
                    dve.wait_ge(mlp.s["y"], T + t + 1)
                    dve.tensor_tensor(yb[:, t % 2, :], mlp.py[t % 2][0:P, :], B2[:, :], ALU.add).then_inc(mlp.s["used"], 1)
                    dve.wait_ge(mlp.s["used"], T + t + 1)
                    dve.tensor_tensor(X[:, t, :], X[:, t, :], yb[:, t % 2, :], ALU.add).then_inc(f["x"], 1)

            @block.scalar
            def _(act):
                for t in range(T):
                    act.wait_ge(f["tr"], t + 1)
                    act.activation(aT[:, :, sl(t)], pa[t % 2][:, 0:KC * P].rearrange("p (k n) -> p k n", k=KC), ACT.Copy)\
                       .then_inc(f["aggT"], 1)
                mlp.act(act)

            @block.tensor
            def _(pe):
                for t in range(T):
                    pe.wait_ge(f["agg"], t + 1)
                    if t >= 2:
                        pe.wait_ge(f["aggT"], t - 1)
                    for k in range(KC):
                        last = pe.transpose(pa[t % 2][:, sl(k)], A[:, t, sl(k, 128)], env.ident[0:P, 0:P])
                    last.then_inc(f["tr"], 1)
                for t in range(T):
                    pe.wait_ge(f["aggT"], t + 1)
                    if t >= 2:
                        pe.wait_ge(mlp.s["hs"], T + t - 1)
                    for k in range(2 * KC):
                        part = aT[:, k, sl(t)] if k < KC else xnT[:, k - KC, sl(t)]
                        last = pe.matmul(pp[t % 2][0:P, :], part, W1[:, k, :], start=(k == 0), stop=(k == 2 * KC - 1))
                    last.then_inc(f["ps"], 1)
                mlp.pe(pe)


STAGES = 99


def build(nc, a, out):
    with ExitStack() as ctx:
        env = Env(nc, ctx)
        sb = lambda n, s, d=F32: env.sb(ctx, n, s, d)
        env.X, env.XN, env.xnT = sb("X", [P, T, D]), sb("XN", [P, T, D]), sb("xnT", [128, KC, N])
        env.ident, env.bd = sb("ident", [128, 128]), sb("bd", [128, 128])
        env.later, env.tri, env.sel = sb("later", [P, P]), sb("tri", [P, NE, NE]), sb("sel", [NE, KC, 128])
        env.ones, env.eps, env.junk = sb("ones", [128, 2]), sb("eps", [128, 1]), sb("junk", [P, 1])
        env.srcf, env.dstf, env.keyf, env.prevf = (sb(n, [P, CH]) for n in ("srcf", "dstf", "keyf", "prevf"))
        env.cnum, env.clater, env.cdel = (sb(n, [P, CH]) for n in ("cnum", "clater", "cdel"))
        env.srci, env.dsti, env.scati, env.cidx = (sb(n, [P, CH], I32) for n in ("srci", "dsti", "scati", "cidx"))
        dram = lambda n, shape: nc.dram_tensor(n, shape, F32, kind="Internal").ap()
        cnt = [dram(f"counts{i}", (N * N + P, 1)) for i in range(TABLES)]
        tab = {"k": dram("hidden_k", (N, D)), "v": dram("hidden_v", (N, D)), "q": dram("queries", (N, QW))}
        agg = dram("aggregate", (N, QW))
        s_dram = dram("s_row", (N,))
        L1 = {k[7:]: v for k, v in a.items() if k.startswith("L1_gnn_")}
        setup(env, a["src"], a["dst"], cnt, agg, a["x"])
        layernorm(env, 0)
        linear_attention(env, 0, a["L0_mix_w_qkv"], a["L0_mix_w_out"], a["L0_mix_b_out"], True, (a["src"], a["dst"], cnt))
        graph_attention(env, a["L0_gnn_W"], a["L0_gnn_b"], a["L0_gnn_a"], cnt, s_dram)
        env.retire("const", "zero", "tables", "index", "x_loaded", "count", "gat_")
        if STAGES > 1:
            layernorm(env, 1)
            experts(env, 0, a["L0_ffn_Wg"], a["L0_ffn_W"], a["L0_ffn_V"], None, a["L0_ffn_W2"], None)
        if STAGES > 2:
            layernorm(env, 2)
            env.L = sb("L", [P, CH * NH])
            env.W1E = {"k": sb("W1Ek", [128, D]), "v": sb("W1Ev", [128, D])}
            node_tables(env, L1, tab)
            edge_pass(env, "k", a["edge_attr_128"], tab, L1, a["dst"], agg)
            env.retire("tab_")
            segment_exp(env, a["dst"])
            edge_pass(env, "v", a["edge_attr_128"], tab, L1, a["dst"], agg)
            env.retire("edge_", "seg_")
            node_output(env, L1, agg)
            linear_attention(env, 1, a["L1_mix_W_qkv"], a["L1_mix_W_proj"], a["L1_mix_b_proj"], False)
        if STAGES > 3:
            layernorm(env, 3)
            experts(env, 1, a["L1_ffn_Wr"], a["L1_ffn_W1"], None, a["L1_ffn_b1"], a["L1_ffn_W2"], a["L1_ffn_b2"], out)
        else:
            with nc.Block() as block:
                @block.sync
                def _(sp):
                    sp.dma_start(out.rearrange("(t p) d -> p t d", p=P), env.X[:, :, :]).then_inc(env.sem("dbg"), 16)
                    sp.wait_ge(env.sem("dbg"), 16)


def kernel(**inputs):
    import numpy as np
    import concourse.bacc as bacc
    from concourse.bass_utils import run_bass_kernel_spmd

    nc = bacc.Bacc("TRN2", target_bir_lowering=False, num_devices=1)
    arrays, args = {}, {}
    for name, value in inputs.items():
        value = np.asarray(value)
        if name in ("L1_mix_W_qkv", "L1_mix_W_proj"):
            value = value.T
        value = np.ascontiguousarray(value)
        arrays["in_" + name] = value
        args[name] = nc.dram_tensor("in_" + name, value.shape, mybir.dt.from_np(value.dtype), kind="ExternalInput").ap()
    out = nc.dram_tensor("out", (N, D), F32, kind="ExternalOutput").ap()
    build(nc, args, out)
    return run_bass_kernel_spmd(nc, [arrays], core_ids=[0]).results[0]["out"]
```

```python
from contextlib import ExitStack

import concourse.bass as bass
import concourse.mybir as mybir
from concourse.alu_op_type import AluOpType as ALU

ACT = mybir.ActivationFunctionType
AX = mybir.AxisListType
F32 = mybir.dt.float32
I32 = mybir.dt.int32
F16 = mybir.dt.float16

P = 125
N = 1250
T = N // P
D = 512
KC = D // 128
NB = 250
NN = N // NB
E = 21250
CH = E // P
EF = 128
NE = 8
CAP = 128
NH = 16
HD = D // NH
QW = D + NH
EPS = 1e-5
BIG = 1e30
TABLES = 2
GR = 10
SB_ = 5
BC = CH // SB_
BE = BC * P
CR = CH // 2

UP = 64.0
UP2 = UP * UP


def sl(t, n=P):
    return slice(t * n, (t + 1) * n)


class Env:

    def __init__(self, nc, ctx):
        self.nc, self.ctx, self.sems, self.stage = nc, ctx, {}, 0

    def sem(self, name):
        if name not in self.sems:
            self.sems[name] = self.nc.alloc_semaphore(name=name)
        return self.sems[name]

    def retire(self, *prefixes):
        old = [n for n in self.sems if n.startswith(prefixes)]
        self.nc.clear_and_free_semaphores([self.sems.pop(n) for n in old])
        self.nc.all_engine_barrier()

    def sb(self, ctx, name, shape, dt=F32):
        return ctx.enter_context(self.nc.sbuf_tensor(f"{name}_{self.stage}", shape, dt))

    def banks(self, ctx, name, n):
        return [ctx.enter_context(self.nc.psum_tensor(f"{name}{i}_{self.stage}", [128, 512], F32)) for i in range(n)]


def rows(w, width=None):
    return w.rearrange("(k p) m -> p k m", p=128)


def bcast(row, parts, n):
    return row.rearrange("(o n) -> o n", o=1).to_broadcast([parts, n])


def setup(env, src, dst, cnt, agg, x):
    nc = env.nc
    with ExitStack() as ctx:
        sb = lambda n, s, d=F32: env.sb(ctx, n, s, d)
        zero = sb("zero", [P, N + 1])
        rowi = sb("rowi", [CR, 3, 2, P], I32)
        rowf = sb("rowf", [CR, 3, 2, P])
        nextf = sb("nextf", [P, CH])
        lastf = sb("lastf", [P, 1])
        junki = sb("junki", [P, 1], I32)
        tmp, cont, own = sb("tmp", [P, CH]), sb("cont", [P, CH]), sb("own", [P, CH])
        owni = sb("owni", [P, CH], I32)
        endd = sb("endd", [P, CH])
        endr = sb("endr", [CR, 2, P])
        ps = env.banks(ctx, "ps", 4)
        s_mem, s_sel, s_zero, s_zd = env.sem("const_cleared"), env.sem("const_ready"), env.sem("zero_ready"), env.sem("tables_cleared")
        s_row, s_rowf, s_tr, s_col, s_pad, s_x = (env.sem("index_rows_loaded"), env.sem("index_rows_float"),
                                             env.sem("index_columns"), env.sem("index_step"), env.sem("index_padded"),
                                             env.sem("x_loaded"))
        with nc.Block() as block:
            @block.sync
            def _(sp):
                sp.wait_ge(s_pad, 1)
                for n, a in enumerate((src, dst)):
                    sp.dma_start(rowi[:, n, :, :], a.rearrange("(p h e) -> p h e", h=2, e=P)).then_inc(s_row, 16)
                m = 84 * 2 * P
                sp.dma_start(rowi[0:84, 2, :, :], dst[1:1 + m].rearrange("(p h e) -> p h e", h=2, e=P)).then_inc(s_row, 16)
                sp.dma_start(rowi[84:85, 2, 0, :], dst[1 + m:1 + m + P].rearrange("(p e) -> p e", e=P)).then_inc(s_row, 16)
                sp.dma_start(rowi[84:85, 2, 1, 0:P - 1], dst[1 + m + P:E].rearrange("(p e) -> p e", e=P - 1)).then_inc(s_row, 16)
                sp.dma_start(env.X[:, :, :], x.rearrange("(t p) d -> p t d", p=P)).then_inc(s_x, 16)
                sp.wait_ge(s_zero, 1)
                n = 0
                for table in cnt:
                    for k in range(T):
                        sp.dma_start(table[k * P * N:(k + 1) * P * N, :].rearrange("(p a) o -> p (a o)", p=P),
                                     zero[:, 0:N]).then_inc(s_zd, 16)
                        n += 16
                    sp.dma_start(table[N * N:N * N + P, :], zero[:, 0:1]).then_inc(s_zd, 16)
                    n += 16
                for k in range(0, N + CH, P):
                    m = min(P, N + CH - k)
                    sp.dma_start(agg[k:k + m, :], zero[0:m, 0:QW]).then_inc(s_zd, 16)
                    n += 16
                sp.wait_ge(s_zd, n)
                sp.wait_ge(s_x, 16)

            @block.gpsimd
            def _(g):
                for n, (m, v) in enumerate(((env.ident, 0.0), (env.bd, 0.0), (env.later, 1.0), (env.tri, 1.0),
                                            (env.sel, 0.0), (lastf, 0.0))):
                    if n:
                        g.wait_ge(s_mem, n)
                    g.memset(m[:], v).then_inc(s_mem, 1)
                g.wait_ge(s_mem, 6)
                g.affine_select(out=env.ident[:, :], in_=env.ident[:, :], compare_op=ALU.not_equal, fill=1.0,
                                base=0, pattern=[[-1, 128]], channel_multiplier=1).then_inc(s_sel, 1)
                g.wait_ge(s_sel, 1)
                g.memset(env.bd[0:64, 0:64], 1.0).then_inc(s_sel, 1)
                g.wait_ge(s_sel, 2)
                g.memset(env.bd[64:128, 64:128], 1.0).then_inc(s_sel, 1)
                g.wait_ge(s_sel, 3)
                g.affine_select(out=env.later[:, :], in_=env.later[:, :], compare_op=ALU.is_gt, fill=0.0,
                                base=0, pattern=[[1, P]], channel_multiplier=-1).then_inc(s_sel, 1)
                g.wait_ge(s_sel, 4)
                g.affine_select(out=env.tri[:, :, :], in_=env.tri[:, :, :], compare_op=ALU.is_gt, fill=0.0,
                                base=0, pattern=[[1, NE], [-1, NE]], channel_multiplier=0).then_inc(s_sel, 1)
                g.wait_ge(s_sel, 5)
                g.affine_select(out=env.sel[:, :, :].rearrange("e b (h f) -> e (b h) f", h=2),
                                in_=env.sel[:, :, :].rearrange("e b (h f) -> e (b h) f", h=2),
                                compare_op=ALU.not_equal, fill=1.0, base=0, pattern=[[-1, NE], [0, 64]],
                                channel_multiplier=1).then_inc(s_sel, 1)
                g.wait_ge(s_sel, 6)
                g.affine_select(out=lastf[:, :], in_=lastf[:, :], compare_op=ALU.not_equal, fill=1.0,
                                base=-(P - 1), pattern=[[0, 1]], channel_multiplier=1).then_inc(s_sel, 1)
                g.wait_ge(s_sel, 7)
                g.iota(junki[:, :], pattern=[[0, 1]], base=N * N, channel_multiplier=1).then_inc(s_sel, 1)
                g.wait_ge(s_sel, 8)
                g.iota(owni[:, :], pattern=[[1, CH]], base=N, channel_multiplier=0).then_inc(s_sel, 1)

            @block.vector
            def _(dve):
                dve.memset(rowi[:, :, :, :], -1).then_inc(s_pad, 1)
                dve.memset(zero[:, :], 0.0).then_inc(s_zero, 1)
                dve.memset(env.ones[:, :], 1.0).then_inc(s_zero, 1)
                dve.memset(env.eps[:, :], EPS).then_inc(s_zero, 1)
                dve.wait_ge(s_row, 80)
                dve.tensor_copy(rowf[:, :, :, :], rowi[:, :, :, :]).then_inc(s_rowf, 1)
                dve.wait_ge(s_rowf, 1)
                dve.tensor_copy(endr[:, :, :], rowf[:, 1, :, P - 1:P].to_broadcast([CR, 2, P])).then_inc(s_rowf, 1)
                dve.tensor_copy(env.headf[:, :], rowf[:, 1, :, 0]).then_inc(s_rowf, 1)
                dve.wait_ge(s_sel, 9)
                dve.tensor_copy(env.junk[:, :], junki[:, :]).then_inc(s_col, 1)
                dve.tensor_copy(own[:, :], owni[:, :]).then_inc(s_col, 1)
                dve.wait_ge(s_tr, 1)
                for n, to in enumerate((env.srcf, env.dstf, nextf, endd)):
                    dve.tensor_copy(to[:, :].rearrange("p (c h) -> p h c", h=2),
                                    ps[n][0:P, 0:CH].rearrange("p (h c) -> p h c", h=2)).then_inc(s_col, 1)
                dve.wait_ge(s_col, 6)
                dve.tensor_copy(env.srci[:, :], env.srcf[:, :]).then_inc(s_col, 1)
                dve.tensor_copy(env.dsti[:, :], env.dstf[:, :]).then_inc(s_col, 1)
                dve.scalar_tensor_tensor(env.keyf[:, :], env.dstf[:, :], float(N), env.srcf[:, :], ALU.mult, ALU.add)\
                   .then_inc(s_col, 1)
                dve.memset(cont[:, 0:1], 0.0).then_inc(s_col, 1)
                dve.tensor_tensor(cont[:, 1:CH], env.dstf[:, 1:CH], endd[:, 0:CH - 1], ALU.is_equal).then_inc(s_col, 1)
                dve.tensor_tensor(own[:, :], own[:, :], env.dstf[:, :], ALU.subtract).then_inc(s_col, 1)
                dve.tensor_tensor(tmp[:, :], env.dstf[:, :], nextf[:, :], ALU.is_equal).then_inc(s_col, 1)
                dve.tensor_scalar(lastf[:, :], lastf[:, :], -float(4 * N), float(4 * N), ALU.mult, ALU.add).then_inc(s_col, 1)
                dve.wait_ge(s_col, 14)
                dve.tensor_tensor(own[:, :], own[:, :], cont[:, :], ALU.mult).then_inc(s_col, 1)
                dve.scalar_tensor_tensor(tmp[:, :], tmp[:, :], lastf[:, 0:1], env.dstf[:, :], ALU.mult, ALU.add).then_inc(s_col, 1)
                dve.wait_ge(s_col, 16)
                dve.tensor_tensor(env.scati[:, :], tmp[:, :], own[:, :], ALU.add).then_inc(s_col, 1)

            @block.tensor
            def _(pe):
                pe.wait_ge(s_rowf, 3)
                pe.wait_ge(s_sel, 9)
                for n in range(3):
                    for h in range(2):
                        pe.transpose(ps[n][0:P, sl(h, CR)], rowf[:, n, h, :], env.ident[0:CR, 0:CR])
                for h in range(2):
                    last = pe.transpose(ps[3][0:P, sl(h, CR)], endr[:, h, :], env.ident[0:CR, 0:CR])
                last.then_inc(s_tr, 1)


def layernorm(env, call):
    env.stage += 1
    nc, X, XN, xnT = env.nc, env.X, env.XN, env.xnT
    stats, aggr, var, std, rstd, xn, tr, out = (env.sem(n) for n in (
        "ln_stats", "ln_moments", "ln_var_eps", "ln_std", "ln_rstd", "xn_ready", "xn_transposed", "xnT_ready"))
    b = T * call
    with ExitStack() as ctx:
        st = env.sb(ctx, "ln_st", [P, T, 6])
        mv = env.sb(ctx, "ln_mv", [P, T, 2])
        sd = env.sb(ctx, "ln_sd", [P, T])
        rs = env.sb(ctx, "ln_rs", [P, T])
        ps = env.banks(ctx, "ln_ps", 2)
        with nc.Block() as block:
            @block.vector
            def _(dve):
                for t in range(T):
                    dve.bn_stats(st[:, t, :], X[:, t, :]).then_inc(stats, 1)
                for t in range(T):
                    dve.wait_ge(stats, b + t + 1)
                    dve.bn_aggr(mv[:, t, :], st[:, t, :]).then_inc(aggr, 1)
                dve.wait_ge(aggr, b + T)
                dve.tensor_scalar(sd[:, :], mv[:, :, 1], EPS, None, ALU.add).then_inc(var, 1)
                dve.wait_ge(std, call + 1)
                dve.reciprocal(rs[:, :], sd[:, :]).then_inc(rstd, 1)
                dve.wait_ge(rstd, call + 1)
                for t in range(T):
                    dve.tensor_scalar(XN[:, t, :], X[:, t, :], mv[:, t, 0:1], rs[:, t:t + 1], ALU.subtract, ALU.mult)\
                       .then_inc(xn, 1)

            @block.scalar
            def _(act):
                act.wait_ge(var, call + 1)
                act.activation(sd[:, :], sd[:, :], ACT.Sqrt).then_inc(std, 1)
                for t in range(T):
                    act.wait_ge(tr, b + t + 1)
                    act.activation(xnT[:, :, sl(t)], ps[t % 2][:, 0:KC * P].rearrange("p (k n) -> p k n", k=KC), ACT.Copy)\
                       .then_inc(out, 1)

            @block.tensor
            def _(pe):
                for t in range(T):
                    pe.wait_ge(xn, b + t + 1)
                    if t >= 2:
                        pe.wait_ge(out, b + t - 1)
                    for k in range(KC):
                        last = pe.transpose(ps[t % 2][:, sl(k)], XN[:, t, sl(k, 128)], env.ident[0:P, 0:P])
                    last.then_inc(tr, 1)


def linear_attention(env, call, wqkv, wout, bout, elu, counts=None):
    env.stage += 1
    nc, X, xnT = env.nc, env.X, env.xnT
    names = ("mix_weights", "mix_k_done", "mix_v_done", "mix_k_neg", "mix_k_exp", "mix_kf", "mix_v", "mix_kv", "mix_kvbd",
             "mix_ksb", "mix_kvT_ps", "mix_kvT", "mix_m_ps", "mix_m", "mix_q_ps", "mix_q_neg", "mix_q_exp", "mix_q",
             "mix_den_ps", "mix_den", "mix_rden", "mix_qs", "mix_y_ps", "mix_yb", "mix_x", "mix_ones")
    s = {n: env.sem(n) for n in names}
    SCALE = 64 ** -0.5
    U = KC * NN
    with ExitStack() as ctx:
        sb = lambda n, sh, d=F32: env.sb(ctx, n, sh, d)
        W = sb("mixW", [128, KC, 3 * D])
        WO = sb("mixWO", [128, KC, D])
        BO = sb("mixBO", [P, D])
        kf = sb("kf", [P, 2, D])
        kn = sb("kn", [P, 2, D])
        v = sb("v", [P, 2, KC, 130])
        qT = sb("qT", [128, KC, N])
        qn = sb("qn", [128, 2, NB])
        kvbd = sb("kvbd", [128, KC, 128])
        ksb = sb("ksb", [128, KC, 128])
        kvT = sb("kvT", [128, KC, 128])
        M = sb("M", [128, KC, D])
        dn = sb("dn", [128, 2, NB])
        yb = sb("yb", [P, 2, D])
        if counts:
            keyrow = sb("keyrow", [P, 2, GR * P])
            dr = sb("dr", [P, 2, GR * P], I32)
            sr = sb("sr", [P, 2, GR * P], I32)
            eq = sb("eq", [P, 2, P])
        ring = env.banks(ctx, "ring", 4)
        kvp = env.banks(ctx, "kvp", 4)
        src, dst, cnt = counts or (None, None, None)
        if counts:
            c_key, c_num, c_idx, c_fin = (env.sem(n) for n in ("count_keys", "count_compared", "count_step", "count_ready"))
            c_put = [env.sem(f"count_scattered{i}") for i in range(TABLES)]
            c_slot = [env.sem(f"count_rows_loaded{i}") for i in range(2)]

        with nc.Block() as block:
            @block.sync
            def _(sp):
                sp.dma_start(W[:, :, :], rows(wqkv)).then_inc(s["mix_weights"], 16)
                sp.dma_start(WO[:, :, :], rows(wout)).then_inc(s["mix_weights"], 16)
                sp.dma_start(BO[:, :], bcast(bout, P, D)).then_inc(s["mix_weights"], 16)
                if counts:
                    for g in range(CH // GR):
                        if g >= 2:
                            sp.wait_ge(c_key, g - 1)
                        for a, to in ((dst, dr), (src, sr)):
                            sp.dma_start(to[:, g % 2, :], bcast(a[g * GR * P:(g + 1) * GR * P], P, GR * P))\
                              .then_inc(c_slot[g % 2], 16)

            if counts:
                @block.gpsimd
                def _(g):
                    for c in range(CH):
                        if c % GR == 0:
                            g.wait_ge(c_fin, c // GR + 1)
                        if c >= TABLES:
                            g.wait_ge(c_put[c % TABLES], 16 * (c // TABLES))
                        g.indirect_dma_start(out=cnt[c % TABLES][:, :],
                                             out_offset=bass.IndirectOffsetOnAxis(ap=env.cidx[:, c:c + 1], axis=0),
                                             in_=env.cnum[:, c:c + 1], in_offset=None, compute_op=ALU.add)\
                         .then_inc(c_put[c % TABLES], 16)
                    for i in range(TABLES):
                        g.wait_ge(c_put[i], 16 * (CH // TABLES))

            @block.vector
            def _(dve):
                def count_group(g):
                    dve.wait_ge(c_slot[g % 2], 32 * (g // 2 + 1))
                    if g >= 2:
                        dve.wait_ge(c_num, 2 * GR * (g - 1))
                    dve.scalar_tensor_tensor(keyrow[:, g % 2, :], dr[:, g % 2, :], float(N), sr[:, g % 2, :], ALU.mult, ALU.add)\
                       .then_inc(c_key, 1)
                    dve.wait_ge(c_key, g + 1)
                    for i in range(GR):
                        c = g * GR + i
                        row = keyrow[:, g % 2, sl(i)]
                        if c:
                            dve.wait_ge(c_num, 2 * c)
                        dve.tensor_scalar(eq[:, 0, :], row, env.keyf[:, c:c + 1], 0.0, ALU.is_equal, ALU.add,
                                          accum_out=env.cnum[:, c:c + 1]).then_inc(c_num, 1)
                        dve.scalar_tensor_tensor(eq[:, 1, :], row, env.keyf[:, c:c + 1], env.later[:, :],
                                                 ALU.is_equal, ALU.mult, accum_out=env.clater[:, c:c + 1]).then_inc(c_num, 1)
                    cs = slice(g * GR, (g + 1) * GR)
                    k = 2 * g
                    dve.wait_ge(c_num, 2 * GR * (g + 1))
                    dve.tensor_scalar(env.clater[:, cs], env.clater[:, cs], 0.0, None, ALU.is_equal).then_inc(c_idx, 1)
                    dve.tensor_scalar(env.cdel[:, cs], env.keyf[:, cs], env.junk[:, 0:1], None, ALU.subtract).then_inc(c_idx, 1)
                    dve.wait_ge(c_idx, 3 * g + 2)
                    dve.tensor_tensor(env.cdel[:, cs], env.cdel[:, cs], env.clater[:, cs], ALU.mult).then_inc(c_idx, 1)
                    dve.wait_ge(c_idx, 3 * g + 3)
                    dve.tensor_scalar(env.cidx[:, cs], env.cdel[:, cs], env.junk[:, 0:1], None, ALU.add).then_inc(c_fin, 1)

                groups = list(range(CH // GR)) if counts else []
                if counts:
                    count_group(groups.pop(0))
                dve.memset(v[:, :, :, :], 1.0).then_inc(s["mix_ones"], 1)
                dve.wait_ge(s["mix_weights"], 48 * (call + 1))
                b = T * call
                for t in range(T):
                    u = t % 2
                    dve.wait_ge(s["mix_k_done"], b + t + 1)
                    if t >= 2:
                        dve.wait_ge(s["mix_kv"], b + t - 1)
                    if elu:
                        dve.tensor_scalar(kn[:, u, :], ring[u][0:P, :], 0.0, None, ALU.min).then_inc(s["mix_k_neg"], 1)
                        dve.wait_ge(s["mix_k_exp"], t + 1)
                        dve.scalar_tensor_tensor(kf[:, u, :], ring[u][0:P, :], 0.0, kn[:, u, :], ALU.max, ALU.add)\
                           .then_inc(s["mix_kf"], 1)
                    else:
                        dve.tensor_scalar(kf[:, u, :], ring[u][0:P, :], 0.0, SCALE, ALU.max, ALU.add).then_inc(s["mix_kf"], 1)
                    if groups:
                        count_group(groups.pop(0))
                dve.wait_ge(s["mix_kv"], b + T)
                for j in range(KC):
                    dve.tensor_tensor(kvbd[:, j, :], kvp[j][:, 0:128], env.bd[:, :], ALU.mult).then_inc(s["mix_kvbd"], 1)
                    dve.tensor_scalar(ksb[:, j, :], env.bd[:, :], kvp[j][:, 128:129], None, ALU.mult).then_inc(s["mix_ksb"], 1)
                for n in range(U):
                    j, m = n // NN, n % NN
                    q = qT[:, j, sl(m, NB)]
                    dve.wait_ge(s["mix_q_ps"], U * call + n + 1)
                    if elu:
                        dve.tensor_scalar(qn[:, n % 2, :], ring[n % 4][:, 0:NB], 0.0, None, ALU.min).then_inc(s["mix_q_neg"], 1)
                        dve.wait_ge(s["mix_q_exp"], n + 1)
                        dve.scalar_tensor_tensor(q, ring[n % 4][:, 0:NB], 0.0, qn[:, n % 2, :], ALU.max, ALU.add)\
                           .then_inc(s["mix_q"], 1)
                    else:
                        dve.tensor_scalar(q, ring[n % 4][:, 0:NB], 0.0, SCALE, ALU.max, ALU.add).then_inc(s["mix_q"], 1)
                    if groups and n % 3 == 2:
                        count_group(groups.pop(0))
                for n in range(U):
                    j, m = n // NN, n % NN
                    k = U * call + n
                    q = qT[:, j, sl(m, NB)]
                    dve.wait_ge(s["mix_den_ps"], k + 1)
                    dve.tensor_scalar(dn[:, n % 2, :], ring[n % 4][:, 0:NB], 1e-6, None, ALU.add).then_inc(s["mix_den"], 1)
                    dve.wait_ge(s["mix_den"], k + 1)
                    dve.reciprocal(dn[:, n % 2, :], dn[:, n % 2, :]).then_inc(s["mix_rden"], 1)
                    dve.wait_ge(s["mix_rden"], k + 1)
                    dve.tensor_tensor(q, q, dn[:, n % 2, :], ALU.mult).then_inc(s["mix_qs"], 1)
                    if groups and n % 2:
                        count_group(groups.pop(0))
                for t in range(T):
                    dve.wait_ge(s["mix_y_ps"], b + t + 1)
                    dve.tensor_tensor(yb[:, t % 2, :], ring[t % 4][0:P, :], BO[:, :], ALU.add).then_inc(s["mix_yb"], 1)
                    dve.wait_ge(s["mix_yb"], b + t + 1)
                    dve.tensor_tensor(X[:, t, :], X[:, t, :], yb[:, t % 2, :], ALU.add).then_inc(s["mix_x"], 1)

            @block.scalar
            def _(act):
                b = T * call
                act.wait_ge(s["mix_ones"], call + 1)
                for t in range(T):
                    u = t % 2
                    if elu:
                        act.wait_ge(s["mix_k_neg"], t + 1)
                        act.activation(kn[:, u, :], kn[:, u, :], ACT.Exp).then_inc(s["mix_k_exp"], 1)
                    act.wait_ge(s["mix_v_done"], b + t + 1)
                    if t >= 2:
                        act.wait_ge(s["mix_kv"], b + t - 1)
                    act.activation(v[:, u, :, 0:128], ring[2 + u][0:P, :].rearrange("p (j m) -> p j m", j=KC), ACT.Copy)\
                       .then_inc(s["mix_v"], 1)
                if elu:
                    for n in range(4):
                        act.wait_ge(s["mix_q_neg"], n + 1)
                        act.activation(qn[:, n % 2, :], qn[:, n % 2, :], ACT.Exp).then_inc(s["mix_q_exp"], 1)
                for j in range(KC):
                    act.wait_ge(s["mix_kvT_ps"], KC * call + j + 1)
                    act.activation(kvT[:, j, :], kvp[j][:, 0:128], ACT.Copy).then_inc(s["mix_kvT"], 1)
                for j in range(KC):
                    act.wait_ge(s["mix_m_ps"], KC * call + j + 1)
                    act.activation(M[:, j, :], kvp[j][:, :], ACT.Copy).then_inc(s["mix_m"], 1)
                if elu:
                    for n in range(4, U):
                        act.wait_ge(s["mix_q_neg"], n + 1)
                        act.activation(qn[:, n % 2, :], qn[:, n % 2, :], ACT.Exp).then_inc(s["mix_q_exp"], 1)

            @block.tensor
            def _(pe):
                b = T * call

                def product(ps, t, w, col):
                    for k in range(KC):
                        last = pe.matmul(ps, xnT[:, k, sl(t)], w[:, k, col:col + D], start=(k == 0), stop=(k == KC - 1))
                    return last

                def kv(t):
                    pe.wait_ge(s["mix_kf"], b + t + 1)
                    pe.wait_ge(s["mix_v"], b + t + 1)
                    for j in range(KC):
                        last = pe.matmul(kvp[j][:, 0:129], kf[:, t % 2, sl(j, 128)], v[:, t % 2, j, 0:129],
                                         start=(t == 0), stop=(t == T - 1))
                    last.then_inc(s["mix_kv"], 1)

                pe.wait_ge(s["mix_weights"], 48 * (call + 1))
                for t in range(T):
                    if t >= 2:
                        pe.wait_ge(s["mix_kf"], b + t - 1)
                        pe.wait_ge(s["mix_v"], b + t - 1)
                    product(ring[t % 2][0:P, :], t, W, D).then_inc(s["mix_k_done"], 1)
                    product(ring[2 + t % 2][0:P, :], t, W, 2 * D).then_inc(s["mix_v_done"], 1)
                    if t:
                        kv(t - 1)
                kv(T - 1)

                def q_product(n):
                    j, m = n // NN, n % NN
                    if n < 4:
                        pe.wait_ge(s["mix_kf"], b + T)
                        pe.wait_ge(s["mix_v"], b + T)
                    else:
                        pe.wait_ge(s["mix_q"], U * call + n - 3)
                    for k in range(KC):
                        last = pe.matmul(ring[n % 4][:, 0:NB], W[:, k, sl(j, 128)], xnT[:, k, sl(m, NB)],
                                         start=(k == 0), stop=(k == KC - 1))
                    last.then_inc(s["mix_q_ps"], 1)

                for n in range(4):
                    q_product(n)
                for j in range(KC):
                    pe.wait_ge(s["mix_kvbd"], KC * call + j + 1)
                    pe.wait_ge(s["mix_ksb"], KC * call + j + 1)
                    pe.transpose(kvp[j][:, 0:128], kvbd[:, j, :], env.ident[:, :]).then_inc(s["mix_kvT_ps"], 1)
                for j in range(KC):
                    pe.wait_ge(s["mix_kvT"], KC * call + j + 1)
                    pe.matmul(kvp[j][:, :], kvT[:, j, :], WO[:, j, :], start=True, stop=True).then_inc(s["mix_m_ps"], 1)
                for n in range(4, U):
                    q_product(n)
                for n in range(U):
                    j, m = n // NN, n % NN
                    pe.wait_ge(s["mix_q"], U * (call + 1))
                    if n >= 4:
                        pe.wait_ge(s["mix_qs"], U * call + n - 3)
                    pe.matmul(ring[n % 4][:, 0:NB], ksb[:, j, :], qT[:, j, sl(m, NB)], start=True, stop=True)\
                      .then_inc(s["mix_den_ps"], 1)
                pe.wait_ge(s["mix_m"], KC * (call + 1))
                pe.wait_ge(s["mix_qs"], U * (call + 1))
                for t in range(T):
                    if t >= 4:
                        pe.wait_ge(s["mix_x"], b + t - 3)
                    for j in range(KC):
                        last = pe.matmul(ring[t % 4][0:P, :], qT[:, j, sl(t)], M[:, j, :], start=(j == 0), stop=(j == KC - 1))
                    last.then_inc(s["mix_y_ps"], 1)


def graph_attention(env, W_, b_, a_, cnt, s_dram):
    env.stage += 1
    nc, X, xnT = env.nc, env.X, env.xnT
    g = {n: env.sem("gat_" + n) for n in ("weights", "emb_ps", "emb", "s", "t", "s_out", "s_row", "cnt0", "cnt1", "leak", "leak2", "leak3",
                                          "exp", "num", "at", "ps", "rec", "x", "num2")}
    with ExitStack() as ctx:
        sb = lambda n, sh, d=F32: env.sb(ctx, n, sh, d)
        W = sb("gatW", [128, KC, D])
        B = sb("gatB", [P, D])
        A = sb("gatA", [P, 2 * D])
        emb = sb("emb", [P, T, D])
        junk = sb("gjunk", [P, 2, D])
        sc = sb("gs", [P, T])
        tc = sb("gt", [P, T])
        srow = sb("srow", [P, N])
        ct = sb("ct", [P, 2, TABLES, N])
        z = sb("gz", [P, 2, N])
        z2 = sb("gz2", [P, 2, N])
        AT = sb("AT", [P, T, N])
        rec = sb("grec", [P, T])
        pe_ps = env.banks(ctx, "gp", 2)
        ysum = env.banks(ctx, "gy", 2)
        rsum = env.banks(ctx, "gr", 2)
        slots = (g["cnt0"], g["cnt1"])
        with nc.Block() as block:
            @block.sync
            def _(sp):
                sp.dma_start(W[:, :, :], rows(W_)).then_inc(g["weights"], 16)
                sp.dma_start(B[:, :], bcast(b_, P, D)).then_inc(g["weights"], 16)
                sp.dma_start(A[:, :], bcast(a_.rearrange("n o -> (n o)"), P, 2 * D)).then_inc(g["weights"], 16)
                for j in range(T):
                    if j >= 2:
                        sp.wait_ge(g["num"], j - 1)
                    if j == 2:
                        sp.wait_ge(g["s"], T)
                        with nc.allow_non_contiguous_dma("1250 values, turned from columns to a row"):
                            sp.dma_start(s_dram.rearrange("(t p) -> p t", p=P), sc[:, :]).then_inc(g["s_out"], 16)
                        sp.wait_ge(g["s_out"], 16)
                        sp.dma_start(srow[:, :], bcast(s_dram, P, N)).then_inc(g["s_row"], 16)
                    for i in range(TABLES):
                        sp.dma_start(ct[:, j % 2, i, :], cnt[i][0:N * N, :].rearrange("(j s) o -> j (s o)", s=N)[sl(j), :])\
                          .then_inc(slots[j % 2], 16)

            @block.vector
            def _(dve):
                dve.wait_ge(g["weights"], 48)
                for t in range(T):
                    dve.wait_ge(g["emb_ps"], t + 1)
                    dve.tensor_tensor(emb[:, t, :], pe_ps[t % 2][0:P, :], B[:, :], ALU.add).then_inc(g["emb"], 1)
                    dve.wait_ge(g["emb"], t + 1)
                    if t:
                        dve.wait_ge(g["s"], t)
                        dve.wait_ge(g["t"], t)
                    dve.scalar_tensor_tensor(junk[:, 0, :], emb[:, t, :], 1.0, A[:, 0:D], ALU.mult, ALU.mult,
                                             accum_out=sc[:, t:t + 1]).then_inc(g["s"], 1)
                    dve.scalar_tensor_tensor(junk[:, 1, :], emb[:, t, :], 1.0, A[:, D:2 * D], ALU.mult, ALU.mult,
                                             accum_out=tc[:, t:t + 1]).then_inc(g["t"], 1)
                for j in range(2):
                    dve.wait_ge(slots[j % 2], 16 * TABLES)
                    dve.tensor_tensor(AT[:, j, :], ct[:, j % 2, 0, :], ct[:, j % 2, 1, :], ALU.add).then_inc(g["num"], 1)
                dve.wait_ge(g["s_row"], 16)
                dve.wait_ge(g["t"], T)
                for j in range(T):
                    u = j % 2
                    if j >= 2:
                        dve.wait_ge(slots[u], 16 * TABLES * (j // 2 + 1))
                        dve.tensor_tensor(AT[:, j, :], ct[:, u, 0, :], ct[:, u, 1, :], ALU.add).then_inc(g["num"], 1)
                        dve.wait_ge(g["at"], j - 1)
                    dve.tensor_scalar(z[:, u, :], srow[:, :], tc[:, j:j + 1], None, ALU.add).then_inc(g["leak"], 1)
                    dve.wait_ge(g["leak"], j + 1)
                    dve.scalar_tensor_tensor(z2[:, u, :], z[:, u, :], 0.1, z[:, u, :], ALU.mult, ALU.max).then_inc(g["leak2"], 1)
                    dve.wait_ge(g["exp"], j + 1)
                    dve.wait_ge(g["num"], j + 1)
                    dve.tensor_tensor(AT[:, j, :], AT[:, j, :], z[:, u, :], ALU.mult).then_inc(g["at"], 1)
                for t in range(T):
                    dve.wait_ge(g["ps"], t + 1)
                    dve.reciprocal(rec[:, t:t + 1], rsum[t % 2][0:P, 0:1]).then_inc(g["rec"], 1)
                    dve.wait_ge(g["rec"], t + 1)
                    dve.scalar_tensor_tensor(X[:, t, :], ysum[t % 2][0:P, :], rec[:, t:t + 1], X[:, t, :], ALU.mult, ALU.add)\
                       .then_inc(g["x"], 1)

            @block.scalar
            def _(act):
                for j in range(T):
                    act.wait_ge(g["leak2"], j + 1)
                    act.activation(z[:, j % 2, :], z2[:, j % 2, :], ACT.Exp).then_inc(g["exp"], 1)

            @block.tensor
            def _(pe):
                pe.wait_ge(g["weights"], 48)
                for t in range(T):
                    if t >= 2:
                        pe.wait_ge(g["emb"], t - 1)
                    for k in range(KC):
                        last = pe.matmul(pe_ps[t % 2][0:P, :], xnT[:, k, sl(t)], W[:, k, :], start=(k == 0), stop=(k == KC - 1))
                    last.then_inc(g["emb_ps"], 1)
                pe.wait_ge(g["emb"], T)
                for t in range(T):
                    if t == 0:
                        pe.wait_ge(g["at"], T)
                    if t >= 2:
                        pe.wait_ge(g["x"], t - 1)
                    for j in range(T):
                        pe.matmul(ysum[t % 2][0:P, :], AT[:, j, sl(t)], emb[:, j, :], start=(j == 0), stop=(j == T - 1))
                    for j in range(T):
                        last = pe.matmul(rsum[t % 2][0:P, 0:2], AT[:, j, sl(t)], env.ones[0:P, 0:2], start=(j == 0), stop=(j == T - 1))
                    last.then_inc(g["ps"], 1)


def experts(env, call, wr, w1, wv, b1, w2, b2, out=None):
    env.stage += 1
    nc, X, xnT = env.nc, env.X, env.xnT
    f = {n: env.sem("ffn_" + n) for n in ("weights", "gate_ps", "gate", "gateT_ps", "gwT", "a_ps", "act", "h", "gb_ps", "hs", "y_ps", "x",
                                          "step", "exp", "out", "gb_free")}
    U = KC * NN
    nw = 4 if call == 0 else 5


    with ExitStack() as ctx:
        sb = lambda n, sh, d=F32: env.sb(ctx, n, sh, d)
        WR = sb("WR", [128, KC, NE])
        W1 = sb("W1", [128, KC, D])
        W2 = sb("W2", [128, KC, D])
        h = sb("h", [128, KC, N])
        gwT = sb("gwT", [NE, N])
        ab = sb("ab", [128, 2, NB])
        if call == 0:
            WV = sb("WV", [128, KC, D])
            L = sb("L", [P, T, NE])
            gt = sb("gt4", [P, T, NE, NE])
            ge = sb("ge4", [P, T, NE, NE])
            mx = sb("mx", [P, T])
            msk = sb("msk", [P, T, NE])
        else:
            B1 = sb("B1", [128, KC])
            B2 = sb("B2", [NE, D])
            LT = sb("LT", [NE, N])
            wk = sb("wk", [NE, N])
            m8 = sb("m8", [NE, 8])
            mx = sb("mx", [NE, 4])
        pa = env.banks(ctx, "pa", 2)
        pg = env.banks(ctx, "pg", 3)
        py = env.banks(ctx, "py", 2)
        with nc.Block() as block:
            @block.sync
            def _(sp):
                sp.dma_start(WR[:, :, :], rows(wr)).then_inc(f["weights"], 16)
                for k in range(KC):
                    sp.dma_start(W1[:, k, :].rearrange("p (e f) -> p e f", e=NE), w1[:, sl(k, 128), :].rearrange("e p f -> p e f"))\
                      .then_inc(f["weights"], 16)
                sp.dma_start(W2[:, :, :], rows(w2.rearrange("e f d -> (e f) d"))).then_inc(f["weights"], 16)
                if call == 0:
                    for k in range(KC):
                        sp.dma_start(WV[:, k, :].rearrange("p (e f) -> p e f", e=NE), wv[:, sl(k, 128), :].rearrange("e p f -> p e f"))\
                          .then_inc(f["weights"], 16)
                else:
                    with nc.allow_non_contiguous_dma("a bias of 512 values as columns"):
                        sp.dma_start(B1[:, :], b1.rearrange("e f -> (e f)").rearrange("(k p) -> p k", p=128)).then_inc(f["weights"], 16)
                    sp.dma_start(B2[:, :], b2).then_inc(f["weights"], 16)
                if out is not None:
                    for t in range(T):
                        sp.wait_ge(f["x"], T * call + t + 1)
                        sp.dma_start(out[sl(t), :], X[:, t, :]).then_inc(f["out"], 16)
                    sp.wait_ge(f["out"], 16 * T)
            W_READY = 16 * 10 if call == 0 else 16 * (10 + 8)

            @block.vector
            def _(dve):
                n0 = 0 if call == 0 else 9
                count = [n0]

                def step(ins):
                    ins.then_inc(f["step"], 1)
                    count[0] += 1
                    dve.wait_ge(f["step"], count[0])

                dve.wait_ge(f["gate_ps"], call + 1)
                if call == 0:
                    step(dve.tensor_copy(L[:, :, :], pg[2][0:P, 0:T * NE].rearrange("p (t e) -> p t e", e=NE)))
                    other = L[:, :, :].unsqueeze(2).to_broadcast([P, T, NE, NE])
                    own = L[:, :, :].unsqueeze(3).to_broadcast([P, T, NE, NE])
                    dve.tensor_tensor(gt[:, :, :, :], other, own, ALU.is_gt)
                    step(dve.tensor_tensor(ge[:, :, :, :], other, own, ALU.is_equal))
                    step(dve.tensor_tensor(ge[:, :, :, :], ge[:, :, :, :],
                                           env.tri[0:P, :, :].unsqueeze(1).to_broadcast([P, T, NE, NE]), ALU.mult))
                    step(dve.tensor_tensor(gt[:, :, :, :], gt[:, :, :, :], ge[:, :, :, :], ALU.add))
                    step(dve.tensor_reduce(msk[:, :, :], gt[:, :, :, :], AX.X, ALU.add))
                    dve.tensor_scalar(msk[:, :, :], msk[:, :, :], 2.0, None, ALU.is_lt)
                    step(dve.tensor_reduce(mx[:, :], L[:, :, :], AX.X, ALU.max))
                    dve.tensor_tensor(L[:, :, :], L[:, :, :], mx[:, :].unsqueeze(2).to_broadcast([P, T, NE]), ALU.subtract)\
                       .then_inc(f["gate"], 1)
                    dve.wait_ge(f["exp"], 1)
                    step(dve.tensor_tensor(L[:, :, :], L[:, :, :], msk[:, :, :], ALU.mult))
                    step(dve.tensor_reduce(mx[:, :], L[:, :, :], AX.X, ALU.add))
                    step(dve.reciprocal(mx[:, :], mx[:, :]))
                    dve.tensor_tensor(L[:, :, :], L[:, :, :], mx[:, :].unsqueeze(2).to_broadcast([P, T, NE]), ALU.mult)\
                       .then_inc(f["gate"], 1)
                else:
                    for m in range(3):
                        w = min(2 * NB, N - m * 2 * NB)
                        last = dve.tensor_copy(LT[:, m * 2 * NB:m * 2 * NB + w], pg[m][0:NE, 0:w])
                        step(last)
                    step(dve.tensor_reduce(mx[:, 0:1], LT[:, :], AX.X, ALU.max))
                    dve.tensor_scalar(mx[:, 1:2], mx[:, 0:1], -1.0, None, ALU.mult).then_inc(f["gate"], 1)
                    dve.wait_ge(f["exp"], 2)
                    step(dve.reciprocal(mx[:, 3:4], mx[:, 2:3]))
                    step(dve.tensor_scalar(LT[:, :], LT[:, :], mx[:, 3:4], None, ALU.mult))
                    for r in range(CAP // 8):
                        cur = LT if r == 0 else wk
                        step(dve.max(m8[:, :], cur[:, :]))
                        step(dve.match_replace(wk[:, :], m8[:, :], cur[:, :], -1.0))
                    step(dve.tensor_tensor(wk[:, :], wk[:, :], LT[:, :], ALU.not_equal))
                    dve.tensor_tensor(gwT[:, :], LT[:, :], wk[:, :], ALU.mult).then_inc(f["gwT"], 1)
                if call == 0:
                    for n in range(U):
                        j, m = n % KC, n // KC
                        dve.wait_ge(f["act"], n + 1)
                        dve.tensor_tensor(h[:, j, sl(m, NB)], pa[n % 2][:, NB:2 * NB], ab[:, n % 2, :], ALU.mult).then_inc(f["h"], 1)
                for n in range(U):
                    j, m = n % KC, n // KC
                    dve.wait_ge(f["gb_ps"], U * call + n + 1)
                    if call == 0:
                        dve.wait_ge(f["h"], n + 1)
                    else:
                        dve.wait_ge(f["act"], U + n + 1)
                    dve.tensor_tensor(h[:, j, sl(m, NB)], h[:, j, sl(m, NB)], pg[n % 2][:, 0:NB], ALU.mult).then_inc(f["hs"], 1)
                for t in range(T):
                    dve.wait_ge(f["y_ps"], T * call + t + 1)
                    dve.tensor_tensor(X[:, t, :], X[:, t, :], py[t % 2][0:P, :], ALU.add).then_inc(f["x"], 1)

            @block.scalar
            def _(act):
                act.wait_ge(f["gate"], 1 if call == 0 else 3)
                if call == 0:
                    act.activation(L[:, :, :], L[:, :, :], ACT.Exp).then_inc(f["exp"], 1)
                    for n in range(U):
                        act.wait_ge(f["a_ps"], n + 1)
                        if n >= 2:
                            act.wait_ge(f["h"], n - 1)
                        act.activation(ab[:, n % 2, :], pa[n % 2][:, 0:NB], ACT.Silu).then_inc(f["act"], 1)
                    for m in range(3):
                        w = min(4, T - 4 * m)
                        act.wait_ge(f["gateT_ps"], m + 1)
                        act.activation(gwT[:, m * 4 * P:(m * 4 + w) * P], pg[m][0:NE, 0:w * P], ACT.Copy).then_inc(f["gwT"], 1)
                else:
                    act.activation(LT[:, :], LT[:, :], ACT.Exp, bias=mx[:, 1:2], accum_out=mx[:, 2:3]).then_inc(f["exp"], 1)
                    act.wait_ge(f["weights"], W_READY)
                    for n in range(U):
                        j, m = n % KC, n // KC
                        act.wait_ge(f["a_ps"], U + n + 1)
                        act.activation(h[:, j, sl(m, NB)], pa[n % 2][:, 0:NB], ACT.Gelu, bias=B1[:, j:j + 1]).then_inc(f["act"], 1)

            @block.tensor
            def _(pe):
                pe.wait_ge(f["weights"], W_READY)
                if call == 0:
                    for t in range(T):
                        for k in range(KC):
                            last = pe.matmul(pg[2][0:P, t * NE:(t + 1) * NE], xnT[:, k, sl(t)], WR[:, k, :],
                                             start=(k == 0), stop=(k == KC - 1))
                    last.then_inc(f["gate_ps"], 1)
                else:
                    for m in range(NN):
                        for k in range(KC):
                            last = pe.matmul(pg[m // 2][0:NE, (m % 2) * NB:(m % 2 + 1) * NB], WR[:, k, :], xnT[:, k, sl(m, NB)],
                                             start=(k == 0), stop=(k == KC - 1))
                    last.then_inc(f["gate_ps"], 1)
                for n in range(U):
                    j, m = n % KC, n // KC
                    if n >= 2:
                        pe.wait_ge(f["act"], U * call + n - 1)
                        if call == 0:
                            pe.wait_ge(f["h"], n - 1)
                    for i, w in enumerate((W1, WV) if call == 0 else (W1,)):
                        for k in range(KC):
                            last = pe.matmul(pa[n % 2][:, sl(i, NB)], w[:, k, sl(j, 128)], xnT[:, k, sl(m, NB)],
                                             start=(k == 0), stop=(k == KC - 1))
                    last.then_inc(f["a_ps"], 1)
                if call == 0:
                    pe.wait_ge(f["gate"], 2)
                    for m in range(3):
                        for i in range(min(4, T - 4 * m)):
                            last = pe.transpose(pg[m][0:NE, sl(i)], L[:, 4 * m + i, :], env.ident[0:P, 0:P])
                        last.then_inc(f["gateT_ps"], 1)
                pe.wait_ge(f["gwT"], 3 if call == 0 else 4)
                for n in range(U):
                    j, m = n % KC, n // KC
                    if n >= 2:
                        pe.wait_ge(f["hs"], U * call + n - 1)
                    pe.matmul(pg[n % 2][:, 0:NB], env.sel[:, j, :], gwT[:, sl(m, NB)], start=True, stop=True).then_inc(f["gb_ps"], 1)
                pe.wait_ge(f["hs"], U * (call + 1))
                for t in range(T):
                    if t >= 2:
                        pe.wait_ge(f["x"], T * call + t - 1)
                    for j in range(KC):
                        last = pe.matmul(py[t % 2][0:P, :], h[:, j, sl(t)], W2[:, j, :], start=(j == 0),
                                         stop=(j == KC - 1 and call == 0))
                    if call == 1:
                        last = pe.matmul(py[t % 2][0:P, :], gwT[:, sl(t)], B2[:, :], start=False, stop=True)
                    last.then_inc(f["y_ps"], 1)



class NodeMlp:

    def __init__(self, env, ctx, call, tag, hs=None):
        self.env, self.call = env, call
        sb = lambda n, sh: env.sb(ctx, tag + n, sh)
        self.hs, self.hT = hs or sb("hs", [P, T, D]), sb("hT", [128, KC, N])
        self.ssq, self.sd, self.rs, self.junk = sb("ssq", [P, T]), sb("sd", [P, T]), sb("rs", [P, T]), sb("sq", [P, 2, D])
        self.G, self.BE, self.W2 = sb("G", [128, KC]), sb("BE", [128, KC]), sb("W2", [128, KC, D])
        self.pt, self.py = env.banks(ctx, tag + "pt", 2), env.banks(ctx, tag + "py", 2)
        self.s = {n: env.sem("mlp_" + n) for n in ("hs", "sq", "var", "std", "rstd", "xh", "tr", "relu", "y", "used")}
        self.b = T * call

    def act(self, act):
        s, b = self.s, self.b
        for t in range(T):
            act.wait_ge(s["hs"], b + t + 1)
            if t >= 2:
                act.wait_ge(s["sq"], b + t - 1)
            act.activation(self.junk[:, t % 2, :], self.hs[:, t, :], ACT.Square, accum_out=self.ssq[:, t:t + 1]).then_inc(s["sq"], 1)
        act.wait_ge(s["sq"], b + T)
        act.activation(self.sd[:, :], self.ssq[:, :], ACT.Sqrt, scale=1.0 / D, bias=self.env.eps[0:P, 0:1]).then_inc(s["std"], 1)
        for t in range(T):
            act.wait_ge(s["tr"], b + t + 1)
            for k in range(KC):
                last = act.activation(self.hT[:, k, sl(t)], self.pt[t % 2][:, sl(k)], ACT.Relu,
                                      scale=self.G[:, k:k + 1], bias=self.BE[:, k:k + 1])
            last.then_inc(s["relu"], 1)

    def dve(self, dve):
        s, b = self.s, self.b
        dve.wait_ge(s["std"], self.call + 1)
        dve.reciprocal(self.rs[:, :], self.sd[:, :]).then_inc(s["rstd"], 1)
        dve.wait_ge(s["rstd"], self.call + 1)
        for t in range(T):
            dve.tensor_scalar(self.hs[:, t, :], self.hs[:, t, :], self.rs[:, t:t + 1], None, ALU.mult).then_inc(s["xh"], 1)

    def pe(self, pe):
        s, b = self.s, self.b
        for t in range(T):
            pe.wait_ge(s["xh"], b + t + 1)
            if t >= 2:
                pe.wait_ge(s["relu"], b + t - 1)
            for k in range(KC):
                last = pe.transpose(self.pt[t % 2][:, sl(k)], self.hs[:, t, sl(k, 128)], self.env.ident[0:P, 0:P])
            last.then_inc(s["tr"], 1)
        for t in range(T):
            pe.wait_ge(s["relu"], b + t + 1)
            if t >= 2:
                pe.wait_ge(s["used"], b + t - 1)
            for k in range(KC):
                last = pe.matmul(self.py[t % 2][0:P, :], self.hT[:, k, sl(t)], self.W2[:, k, :], start=(k == 0), stop=(k == KC - 1))
            last.then_inc(s["y"], 1)


def centre(dve, step, w, nk, m, parts, scale=1.0):
    step(dve.tensor_reduce(m[0:parts, 0:nk], w, AX.X, ALU.add))
    step(dve.tensor_scalar(m[0:parts, 0:nk], m[0:parts, 0:nk], 1.0 / D, None, ALU.mult))
    for k in range(nk):
        last = dve.tensor_scalar(w[:, k, :], w[:, k, :], m[0:parts, k:k + 1], scale, ALU.subtract, ALU.mult)
    step(last)


def node_tables(env, w, tab):
    env.stage += 1
    nc, X, XN, xnT = env.nc, env.X, env.XN, env.xnT
    f = {n: env.sem("tab_" + n) for n in ("weights", "step", "xres", "ps", "row", "qrow", "qprod", "qb", "q")}
    slot = [env.sem(f"tab_stored{i}") for i in range(4)]
    with ExitStack() as ctx:
        sb = lambda n, sh, d=F32: env.sb(ctx, n, sh, d)
        WK, WV, WQ = sb("tWK", [128, 5, D]), sb("tWV", [128, 5, D]), sb("tWQ", [128, KC, D])
        BK, BV, BQ = sb("tBK", [P, 1, D]), sb("tBV", [P, 1, D]), sb("tBQ", [P, 1, D])
        B2Q, B2K = sb("tB2Q", [P, D]), sb("tB2K", [P, D])
        m = sb("tm", [128, 8])
        row = sb("trow", [P, 4, QW])
        prod = sb("tprod", [P, D])
        pp = env.banks(ctx, "pp", 4)
        E2 = {e: sb("tE2" + e, [128, KC, D]) for e in "kv"}
        mlp = NodeMlp(env, ctx, 0, "q", env.XN)
        with nc.Block() as block:
            @block.sync
            def _(sp):
                loads = [(WK[:, :, :], rows(w["hk_W1"])), (WV[:, :, :], rows(w["hv_W1"])), (WQ[:, :, :], rows(w["hq_W1"])),
                         (BK[:, 0, :], bcast(w["hk_b1"], P, D)), (BV[:, 0, :], bcast(w["hv_b1"], P, D)),
                         (BQ[:, 0, :], bcast(w["hq_b1"], P, D)), (B2Q[:, :], bcast(w["hq_b2"], P, D)),
                         (B2K[:, :], bcast(w["hk_b2"], P, D)), (mlp.W2[:, :, :], rows(w["hq_W2"])),
                         (E2["k"][:, :, :], rows(w["hk_W2"])), (E2["v"][:, :, :], rows(w["hv_W2"]))]
                for to, a in loads:
                    sp.dma_start(to, a).then_inc(f["weights"], 16)
                with nc.allow_non_contiguous_dma("512 values as columns"):
                    for to, a in ((mlp.G, "hq_g"), (mlp.BE, "hq_be"), (env.G["k"], "hk_g"), (env.BE["k"], "hk_be"),
                                  (env.G["v"], "hv_g"), (env.BE["v"], "hv_be")):
                        sp.dma_start(to[:, :], w[a].rearrange("(k p) -> p k", p=128)).then_inc(f["weights"], 16)
                for n in range(3 * T):
                    t = n % T
                    if n < 2 * T:
                        sp.wait_ge(f["row"], n + 1)
                        sp.dma_start(tab["k" if n < T else "v"][sl(t), :], row[:, n % 4, 0:D]).then_inc(slot[n % 4], 16)
                    else:
                        sp.wait_ge(f["q"], t + 1)
                        sp.dma_start(tab["q"][sl(t), :], row[:, n % 4, :]).then_inc(slot[n % 4], 16)
                for i in range(4):
                    sp.wait_ge(slot[i], 16 * len(range(i, 3 * T, 4)))

            @block.vector
            def _(dve):
                n_step = [0]

                def step(ins):
                    ins.then_inc(f["step"], 1)
                    n_step[0] += 1
                    dve.wait_ge(f["step"], n_step[0])

                def edge_weights():
                    for e, w1 in (("k", WK), ("v", WV)):
                        dve.tensor_scalar(env.W1E[e][:, 0, :], w1[:, KC, :], 1.0 / UP, None, ALU.mult)
                        step(dve.tensor_scalar(env.W2E[e][:, 0, :, :], E2[e][:, :, :], UP, None, ALU.mult))
                        dve.scalar_tensor_tensor(env.W1E[e][:, 1, :], w1[:, KC, :], 1.0 / UP, env.W1E[e][:, 0, :],
                                                 ALU.mult, ALU.subtract)
                        w2, hi, lo = (a.rearrange("p k m -> p (k m)") for a in (E2[e][:, :, :], env.W2E[e][:, 0, :, :],
                                                                                env.W2E[e][:, 1, :, :]))
                        dve.scalar_tensor_tensor(lo, w2, UP, hi, ALU.mult, ALU.subtract)
                        for a in (env.G[e], env.BE[e]):
                            dve.tensor_scalar(a[:, :], a[:, :], UP, None, ALU.mult)

                for t in range(T):
                    dve.tensor_tensor(X[:, t, :], X[:, t, :], XN[:, t, :], ALU.add).then_inc(f["xres"], 1)
                dve.wait_ge(f["xres"], T)
                dve.wait_ge(f["weights"], 16 * 17)
                centre(dve, step, WK[:, :, :], 5, m, 128, UP2)
                centre(dve, step, WV[:, :, :], 5, m, 128, UP2)
                centre(dve, step, WQ[:, :, :], KC, m, 128)
                for b, up in ((BK, UP2), (BV, UP2), (BQ, 1.0)):
                    centre(dve, step, b[:, :, :], 1, m, P, up)
                for n in range(3 * T):
                    dve.wait_ge(f["ps"], n + 1)
                    if n < 2 * T:
                        if n >= 4:
                            dve.wait_ge(slot[n % 4], 16 * (n // 4))
                        dve.tensor_tensor(row[:, n % 4, 0:D], pp[n % 4][0:P, :], (BK if n < T else BV)[:, 0, :], ALU.add)\
                           .then_inc(f["row"], 1)
                    else:
                        dve.tensor_tensor(mlp.hs[:, n - 2 * T, :], pp[n % 4][0:P, :], BQ[:, 0, :], ALU.add).then_inc(mlp.s["hs"], 1)
                mlp.dve(dve)
                for t in range(T):
                    n = 2 * T + t
                    r = row[:, n % 4, :]
                    dve.wait_ge(mlp.s["y"], t + 1)
                    dve.wait_ge(slot[n % 4], 16 * (n // 4))
                    dve.tensor_tensor(r[:, 0:D], mlp.py[t % 2][0:P, :], B2Q[:, :], ALU.add).then_inc(mlp.s["used"], 1)
                    dve.wait_ge(mlp.s["used"], t + 1)
                    dve.tensor_tensor(prod[:, :], r[:, 0:D], B2K[:, :], ALU.mult).then_inc(f["qprod"], 1)
                    dve.wait_ge(f["qprod"], t + 1)
                    dve.tensor_reduce(r[:, D:QW], prod[:, :].rearrange("p (h d) -> p h d", h=NH), AX.X, ALU.add).then_inc(f["qb"], 1)
                    dve.wait_ge(f["qb"], t + 1)
                    dve.tensor_scalar(r[:, 0:D], r[:, 0:D], float(HD) ** -0.5 / UP2, None, ALU.mult)
                    dve.tensor_scalar(r[:, D:QW], r[:, D:QW], float(HD) ** -0.5, None, ALU.mult).then_inc(f["q"], 1)
                    if t == 0:
                        edge_weights()

            @block.scalar
            def _(act):
                mlp.act(act)

            @block.tensor
            def _(pe):
                pe.wait_ge(f["step"], 6 * 3)
                for n in range(3 * T):
                    t, wt = n % T, (WK, WV, WQ)[n // T]
                    if n >= 4:
                        if n - 4 < 2 * T:
                            pe.wait_ge(f["row"], n - 3)
                        else:
                            pe.wait_ge(mlp.s["hs"], n - 3 - 2 * T)
                    for k in range(KC):
                        last = pe.matmul(pp[n % 4][0:P, :], xnT[:, k, sl(t)], wt[:, k, :], start=(k == 0), stop=(k == KC - 1))
                    last.then_inc(f["ps"], 1)
                mlp.pe(pe)


LAG = 11
LATE = 5
UN = 4
J0, J1 = 3, 42


def at(j, u, d):
    q, r = divmod(u + d, UN)
    return j + q, r


def chunks(eng, step, last):
    for c in range(UN * J0):
        step(*divmod(c, UN))
    with eng.Fori(J0, J1) as j:
        for u in range(UN):
            step(j, u)
    for c in range(UN * J1, last + 1):
        step(*divmod(c, UN))


def edge_pass(env, mode, edge_attr, tab, w, dst, agg):
    env.stage += 1
    nc = env.nc
    V = mode == "v"
    ci = 1 if V else 0
    b = CH * ci
    names = ("efT_ps", "efT_hi", "efT_lo", "h_ps", "hs", "sq", "std", "rstd", "xh", "tr", "relu", "r_hi", "r_lo", "y", "prod",
             "red", "logit", "wv", "wv_hi", "wv_lo", "sz", "tot_ps", "tot", "eps")
    f = {n: env.sem("edge_" + n) for n in names}
    ring = lambda n: [env.sem(f"edge_{n}{i}") for i in range(UN)]
    ef_in, g_in, q_in, d_in, sc_out = ring("attr_loaded"), ring("hidden_gathered"), ring("q_gathered"), ring("dst_loaded"), ring("scattered")
    uses = [len(range(u, CH, UN)) for u in range(UN)]
    W1, W2, G, BE = env.W1E[mode], env.W2E[mode], env.G[mode], env.BE[mode]

    def loaded(j, u, both=True):
        return 16 * (j + 1 + (uses[u] * ci if both else 0))

    with ExitStack() as ctx:
        sb = lambda n, sh, d=F32: env.sb(ctx, n, sh, d)
        ef = sb("ef", [P, UN, EF])
        efT = sb("efT", [128, 2, 2, P], F16)
        hg = sb("hg", [P, UN, D])
        hs = sb("ehs", [P, 2, D])
        sq = sb("esq", [P, D])
        ssq, sd, rs = sb("essq", [P, UN]), sb("esd", [P, UN]), sb("ers", [P, UN])
        eps = sb("eeps", [P, 1])
        xh = sb("exh", [P, 2, D])
        r32 = sb("er32", [128, UN, KC * P])
        rT = sb("erT", [128, UN, 2, KC * P], F16)
        if V:
            wv = sb("ewv", [P, D])
            wp = sb("ewp", [P, 2, 2, D], F16)
            dr = sb("edr", [P, UN, P], I32)
            S = sb("eS", [P, 2, P], F16)
            tot = sb("etot", [P, UN, QW])
        else:
            qg = sb("eqg", [P, UN, QW])
            prod, red = sb("eprod", [P, D]), sb("ered", [P, NH])
        pe_ef, pe_h = env.banks(ctx, "pef", 1)[0], env.banks(ctx, "peh", 1)[0]
        pt, py = env.banks(ctx, "pet", 2), env.banks(ctx, "pey", 2)
        if V:
            po, pd = env.banks(ctx, "peo", 1)[0], env.banks(ctx, "ped", 1)[0]
        with nc.Block() as block:
            @block.sync
            def _(sp):
                for c in range(CH + LATE):
                    if c < CH:
                        if c >= UN:
                            sp.wait_ge(f["efT_ps"], b + c - UN + 1)
                        sp.dma_start(ef[:, c % UN, :], edge_attr[sl(c), :]).then_inc(ef_in[c % UN], 16)
                    x = c - LATE
                    if V and x >= 0:
                        if x >= UN:
                            sp.wait_ge(f["sz"], x - UN + 1)
                        sp.dma_start(dr[:, x % UN, :], bcast(dst[sl(x)], P, P)).then_inc(d_in[x % UN], 16)

            @block.gpsimd
            def _(g):
                for c in range(CH + LAG):
                    if c < CH:
                        u = c % UN
                        if c >= UN:
                            g.wait_ge(f["hs"], b + c - UN + 1)
                        g.indirect_dma_start(out=hg[:, u, :], out_offset=None, in_=tab[mode][:, :],
                                             in_offset=bass.IndirectOffsetOnAxis(ap=env.srci[:, c:c + 1], axis=0))\
                         .then_inc(g_in[u], 16)
                    x = c - LATE
                    if not V and 0 <= x < CH:
                        if x >= UN:
                            g.wait_ge(f["logit"], x - UN + 1)
                        g.indirect_dma_start(out=qg[:, x % UN, :], out_offset=None, in_=tab["q"][:, :],
                                             in_offset=bass.IndirectOffsetOnAxis(ap=env.dsti[:, x:x + 1], axis=0))\
                         .then_inc(q_in[x % UN], 16)
                    if V and c >= LAG:
                        x = c - LAG
                        g.wait_ge(f["tot"], x + 1)
                        g.indirect_dma_start(out=agg[:, :], out_offset=bass.IndirectOffsetOnAxis(ap=env.scati[:, x:x + 1], axis=0),
                                             in_=tot[:, x % UN, :], in_offset=None, bounds_check=N + CH - 1, oob_is_err=False)\
                         .then_inc(sc_out[x % UN], 16)
                if V:
                    for u in range(UN):
                        g.wait_ge(sc_out[u], 16 * uses[u])

            @block.vector
            def _(dve):
                def add(j, u):
                    c = UN * j + u
                    dve.wait_ge(f["h_ps"], b + c + 1)
                    dve.wait_ge(g_in[u], loaded(j, u))
                    if not (isinstance(c, int) and c < 2):
                        dve.wait_ge(f["sq"], b + c - 1)
                        dve.wait_ge(f["xh"], b + c - 1)
                    dve.tensor_tensor(hs[:, u % 2, :], pe_h[0:P, :], hg[:, u, :], ALU.add).then_inc(f["hs"], 1)

                def ef_low(j, u):
                    c = UN * j + u
                    dve.wait_ge(f["efT_hi"], b + c + 1)
                    dve.scalar_tensor_tensor(efT[:, u % 2, 1, :], pe_ef[:, 0:P], UP, efT[:, u % 2, 0, :], ALU.mult, ALU.subtract)\
                       .then_inc(f["efT_lo"], 1)

                def r_low(j, u):
                    c = UN * j + u
                    dve.wait_ge(f["r_hi"], b + c + 1)
                    dve.tensor_tensor(rT[:, u, 1, :], r32[:, u, :], rT[:, u, 0, :], ALU.subtract).then_inc(f["r_lo"], 1)

                def invert(j, u):
                    c = UN * j + u
                    dve.wait_ge(f["std"], b + c + 1)
                    dve.reciprocal(rs[:, u:u + 1], sd[:, u:u + 1]).then_inc(f["rstd"], 1)

                def normalise(j, u):
                    c = UN * j + u
                    if not (isinstance(c, int) and c < 2):
                        dve.wait_ge(f["tr"], b + c - 1)
                    dve.wait_ge(f["rstd"], b + c + 1)
                    dve.tensor_scalar(xh[:, u % 2, :], hs[:, u % 2, :], rs[:, u:u + 1], None, ALU.mult).then_inc(f["xh"], 1)

                def times_q(j, u):
                    c = UN * j + u
                    dve.wait_ge(f["y"], c + 1)
                    dve.wait_ge(q_in[u], loaded(j, u, False))
                    if not (isinstance(c, int) and c < 1):
                        dve.wait_ge(f["red"], c)
                    dve.tensor_tensor(prod[:, :], py[u % 2][0:P, :], qg[:, u, 0:D], ALU.mult).then_inc(f["prod"], 1)

                def sum_heads(j, u):
                    c = UN * j + u
                    dve.wait_ge(f["prod"], c + 1)
                    if not (isinstance(c, int) and c < 1):
                        dve.wait_ge(f["logit"], c)
                    dve.tensor_reduce(red[:, :], prod[:, :].rearrange("p (h d) -> p h d", h=NH), AX.X, ALU.add).then_inc(f["red"], 1)

                def logits(j, u):
                    c = UN * j + u
                    dve.wait_ge(f["red"], c + 1)
                    dve.tensor_tensor(env.L[:, bass.ds(c * NH, NH)], red[:, :], qg[:, u, D:QW], ALU.add).then_inc(f["logit"], 1)

                def weigh(j, u):
                    c = UN * j + u
                    dve.wait_ge(f["y"], b + c + 1)
                    if not (isinstance(c, int) and c < 1):
                        dve.wait_ge(f["wv_lo"], c)
                    dve.scalar_tensor_tensor(wv[:, :].rearrange("p (h d) -> p h d", h=NH),
                                             py[u % 2][0:P, :].rearrange("p (h d) -> p h d", h=NH), 1.0 / UP,
                                             env.L[:, bass.ds(c * NH, NH)].unsqueeze(2).to_broadcast([P, NH, HD]),
                                             ALU.mult, ALU.mult).then_inc(f["wv"], 1)

                def compare(j, u):
                    c = UN * j + u
                    dve.wait_ge(d_in[u], loaded(j, u, False))
                    if not (isinstance(c, int) and c < 2):
                        dve.wait_ge(f["tot_ps"], c - 1)
                    dve.tensor_scalar(S[:, u % 2, :], dr[:, u, :], env.dstf[:, bass.ds(c, 1)], None, ALU.is_equal).then_inc(f["sz"], 1)

                def wv_high(j, u):
                    c = UN * j + u
                    dve.wait_ge(f["wv"], c + 1)
                    dve.tensor_copy(wp[:, u % 2, 0, :], wv[:, :]).then_inc(f["wv_hi"], 1)

                def wv_low(j, u):
                    c = UN * j + u
                    dve.wait_ge(f["wv_hi"], c + 1)
                    dve.tensor_tensor(wp[:, u % 2, 1, :], wv[:, :], wp[:, u % 2, 0, :], ALU.subtract).then_inc(f["wv_lo"], 1)

                dve.memset(eps[:, :], EPS * UP2 * UP2).then_inc(f["eps"], 1)
                ef_low(0, 0)

                def step(j, u):
                    c = UN * j + u
                    static = isinstance(c, int)
                    if not V and (not static or 0 <= c - 6 < CH):
                        logits(*at(j, u, -6))
                    if not static or c < CH:
                        add(j, u)
                    if not static or c + 1 < CH:
                        ef_low(*at(j, u, 1))
                    if not static or 0 <= c - 1 < CH:
                        invert(*at(j, u, -1))
                    if not static or 0 <= c - 5 < CH:
                        (weigh if V else times_q)(*at(j, u, -5))
                    if V and (not static or 0 <= c - 5 < CH):
                        compare(*at(j, u, -5))
                    if not static or 0 <= c - 1 < CH:
                        normalise(*at(j, u, -1))
                    if V and (not static or 0 <= c - 5 < CH):
                        wv_high(*at(j, u, -5))
                    if not static or 0 <= c - 3 < CH:
                        r_low(*at(j, u, -3))
                    if not static or 0 <= c - 5 < CH:
                        (wv_low if V else sum_heads)(*at(j, u, -5))
                chunks(dve, step, CH + 5)

            @block.scalar
            def _(act):
                def copy_ef(j, u):
                    c = UN * j + u
                    act.wait_ge(f["efT_ps"], b + c + 1)
                    if not (isinstance(c, int) and c < 2):
                        act.wait_ge(f["h_ps"], b + c - 1)
                    act.activation(efT[:, u % 2, 0, :], pe_ef[:, 0:P], ACT.Copy, scale=UP).then_inc(f["efT_hi"], 1)

                def deviation(j, u):
                    c = UN * j + u
                    act.wait_ge(f["hs"], b + c + 1)
                    act.activation(sq[:, :], hs[:, u % 2, :], ACT.Square, accum_out=ssq[:, u:u + 1]).then_inc(f["sq"], 1)
                    act.wait_ge(f["sq"], b + c + 1)
                    act.activation(sd[:, u:u + 1], ssq[:, u:u + 1], ACT.Sqrt, scale=1.0 / D, bias=eps[:, 0:1])\
                       .then_inc(f["std"], 1)

                def relu(j, u):
                    c = UN * j + u
                    act.wait_ge(f["tr"], b + c + 1)
                    if not (isinstance(c, int) and c < UN):
                        act.wait_ge(f["y"], b + c - UN + 1)
                    for k in range(KC):
                        last = act.activation(r32[:, u, sl(k)], pt[u % 2][:, sl(k)], ACT.Relu, scale=G[:, k:k + 1], bias=BE[:, k:k + 1])
                    last.then_inc(f["relu"], 1)

                def r_high(j, u):
                    c = UN * j + u
                    act.wait_ge(f["relu"], b + c + 1)
                    act.activation(rT[:, u, 0, :], r32[:, u, :], ACT.Copy).then_inc(f["r_hi"], 1)

                def total(j, u):
                    c = UN * j + u
                    act.wait_ge(f["tot_ps"], c + 1)
                    if not (isinstance(j, int) and j == 0):
                        act.wait_ge(sc_out[u], 16 * j)
                    act.activation(tot[:, u, 0:D], po[0:P, :], ACT.Copy)
                    act.activation(tot[:, u, D:QW], pd[0:P, 0:NH], ACT.Copy).then_inc(f["tot"], 1)

                act.wait_ge(f["eps"], ci + 1)
                copy_ef(0, 0)

                def step(j, u):
                    c = UN * j + u
                    static = isinstance(c, int)
                    if V and (not static or 0 <= c - 7 < CH):
                        total(*at(j, u, -7))
                    if not static or c + 1 < CH:
                        copy_ef(*at(j, u, 1))
                    if not static or c < CH:
                        deviation(j, u)
                    if not static or 0 <= c - 2 < CH:
                        relu(*at(j, u, -2))
                        r_high(*at(j, u, -2))
                chunks(act, step, CH + 6)

            @block.tensor
            def _(pe):
                def flip_ef(j, u):
                    c = UN * j + u
                    pe.wait_ge(ef_in[u], loaded(j, u))
                    if not (isinstance(c, int) and c < 1):
                        pe.wait_ge(f["efT_lo"], b + c)
                    pe.transpose(pe_ef[:, 0:P], ef[:, u, :], env.ident[0:P, 0:P]).then_inc(f["efT_ps"], 1)

                def hidden(j, u):
                    c = UN * j + u
                    pe.wait_ge(f["efT_lo"], b + c + 1)
                    if not (isinstance(c, int) and c < 1):
                        pe.wait_ge(f["hs"], b + c)
                    pe.matmul(pe_h[0:P, :], efT[:, u % 2, 0, :], W1[:, 0, :], start=True, stop=False)
                    pe.matmul(pe_h[0:P, :], efT[:, u % 2, 0, :], W1[:, 1, :], start=False, stop=False)
                    pe.matmul(pe_h[0:P, :], efT[:, u % 2, 1, :], W1[:, 0, :], start=False, stop=True).then_inc(f["h_ps"], 1)

                def flip_xh(j, u):
                    c = UN * j + u
                    pe.wait_ge(f["xh"], b + c + 1)
                    if not (isinstance(c, int) and c < 2):
                        pe.wait_ge(f["relu"], b + c - 1)
                    for k in range(KC):
                        last = pe.transpose(pt[u % 2][:, sl(k)], xh[:, u % 2, sl(k, 128)], env.ident[0:P, 0:P])
                    last.then_inc(f["tr"], 1)

                def product(j, u):
                    c = UN * j + u
                    pe.wait_ge(f["r_lo"], b + c + 1)
                    if not (isinstance(c, int) and c < 2):
                        pe.wait_ge(f["wv" if V else "prod"], c - 1)
                    for k in range(KC):
                        for r, w2 in ((0, 0), (0, 1), (1, 0)):
                            last = pe.matmul(py[u % 2][0:P, :], rT[:, u, r, sl(k)], W2[:, w2, k, :],
                                             start=(k == 0 and r == w2), stop=(k == KC - 1 and r == 1))
                    last.then_inc(f["y"], 1)

                def total(j, u):
                    c = UN * j + u
                    pe.wait_ge(f["wv_lo"], c + 1)
                    pe.wait_ge(f["sz"], c + 1)
                    if not (isinstance(c, int) and c < 1):
                        pe.wait_ge(f["tot"], c)
                    for part in range(2):
                        pe.matmul(po[0:P, :], S[:, u % 2, :], wp[:, u % 2, part, :], start=(part == 0), stop=(part == 1))
                    for part in range(2):
                        last = pe.matmul(pd[0:P, 0:NH], S[:, u % 2, :], env.LP[:, part, bass.ds(c * NH, NH)],
                                         start=(part == 0), stop=(part == 1))
                    last.then_inc(f["tot_ps"], 1)

                flip_ef(0, 0)

                def step(j, u):
                    c = UN * j + u
                    static = isinstance(c, int)
                    if not static or c < CH:
                        hidden(j, u)
                    if not static or c + 1 < CH:
                        flip_ef(*at(j, u, 1))
                    if not static or 0 <= c - 2 < CH:
                        flip_xh(*at(j, u, -2))
                    if not static or 0 <= c - 4 < CH:
                        product(*at(j, u, -4))
                    if V and (not static or 0 <= c - 6 < CH):
                        total(*at(j, u, -6))
                chunks(pe, step, CH + 5)


def segment_exp(env, dst):
    nc, L = env.nc, env.L
    R = SB_ * NH
    f = {n: env.sem("seg_" + n) for n in ("dst", "pad", "flag", "lt_ps", "lt", "step", "row_ps", "row", "col_ps", "col", "m", "m_ps", "sub", "exp", "hi")}
    Lb = L[:, :].rearrange("p (b i h) -> p i b h", b=SB_, h=NH)
    with ExitStack() as ctx:
        sb = lambda n, sh, d=F32: env.sb(ctx, n, sh, d)
        DD = sb("sDD", [R, BE + 2], I32)
        fl = sb("sfl", [R, BE + 1])
        LT = sb("sLT", [R, BE])
        F = sb("sF", [R, BE])
        B = sb("sB", [R, BE])
        Lc = sb("sLc", [P, 2, SB_, NH])
        fn = sb("sfn", [R, 4])
        row = sb("srow4", [1, 4, SB_, NH])
        ini = sb("sini", [1, 2, SB_, NH])
        col = sb("scol", [R, 2])
        tmp = sb("stmp", [1, 2, NH])
        pl = env.banks(ctx, "spl", 2)
        pr = env.banks(ctx, "spr", 2)
        pm = env.banks(ctx, "spm", 2)
        with nc.Block() as block:
            @block.sync
            def _(sp):
                sp.wait_ge(f["pad"], 1)
                for k in range(SB_):
                    lo, hi = max(0, k * BE - 1), min(E, (k + 1) * BE + 1)
                    at0 = 1 if k == 0 else 0
                    sp.dma_start(DD[k * NH:(k + 1) * NH, at0:at0 + hi - lo], bcast(dst[lo:hi], NH, hi - lo)).then_inc(f["dst"], 16)

            @block.tensor
            def _(pe):
                for i in range(BC):
                    q, r = divmod(i, 4)
                    pe.wait_ge(f["step"], i + 1)
                    if r == 0 and q >= 2:
                        pe.wait_ge(f["lt"], q - 1)
                    last = pe.transpose(pl[q % 2][0:R, sl(r)], Lc[:, i % 2, :, :].rearrange("p b h -> p (b h)"), env.ident[0:P, 0:P])
                    last.then_inc(f["lt_ps"], 1)
                pe.wait_ge(f["flag"], 6)
                for n, c in enumerate((F[:, BE - 1:BE], B[:, 0:1], fn[:, 0:1], fn[:, 1:2])):
                    last = pe.transpose(pr[0][0:1, n * R:(n + 1) * R], c, env.ident[0:R, 0:R])
                last.then_inc(f["row_ps"], 1)
                pe.wait_ge(f["row"], 1)
                for n in range(2):
                    last = pe.transpose(pr[1][0:R, n:n + 1], ini[0:1, n, :, :].rearrange("o b h -> o (b h)"), env.ident[0:1, 0:1])
                last.then_inc(f["col_ps"], 1)
                pe.wait_ge(f["m"], 1)
                for i in range(BC):
                    q, r = divmod(i, 6)
                    if r == 0 and q >= 2:
                        pe.wait_ge(f["sub"], q - 1)
                    last = pe.transpose(pm[q % 2][0:P, r * R:(r + 1) * R], F[:, sl(i)], env.ident[0:R, 0:R])
                    if r == 5 or i == BC - 1:
                        last.then_inc(f["m_ps"], 1)

            @block.scalar
            def _(act):
                for i in range(BC):
                    if i >= 2:
                        act.wait_ge(f["lt_ps"], i - 1)
                    act.activation(Lc[:, i % 2, :, :], Lb[:, i, :, :], ACT.Copy).then_inc(f["step"], 1)
                    q, r = divmod(i, 4)
                    if r == 3 or i == BC - 1:
                        act.wait_ge(f["lt_ps"], i + 1)
                        act.activation(LT[:, q * 4 * P:(q * 4 + r + 1) * P], pl[q % 2][0:R, 0:(r + 1) * P], ACT.Copy).then_inc(f["lt"], 1)
                act.wait_ge(f["sub"], (BC + 5) // 6)
                act.activation(L[:, :], L[:, :], ACT.Exp).then_inc(f["exp"], 1)
                act.wait_ge(f["exp"], 1)
                act.activation(env.LP[:, 0, :], L[:, :], ACT.Copy, scale=UP).then_inc(f["hi"], 1)

            @block.vector
            def _(dve):
                n = [0]
                chain = env.sem("seg_chain")

                def step(ins):
                    ins.then_inc(chain, 1)
                    n[0] += 1
                    dve.wait_ge(chain, n[0])

                dve.memset(DD[:, :], -1).then_inc(f["pad"], 1)
                dve.wait_ge(f["dst"], 16 * SB_)
                step(dve.tensor_tensor(fl[:, :], DD[:, 1:BE + 2], DD[:, 0:BE + 1], ALU.not_equal))
                step(dve.tensor_scalar(fl[:, :], fl[:, :], -BIG, None, ALU.mult))
                dve.tensor_reduce(fn[:, 0:1], fl[:, 0:BE], AX.X, ALU.min).then_inc(f["flag"], 1)
                dve.tensor_reduce(fn[:, 1:2], fl[:, 1:BE + 1], AX.X, ALU.min).then_inc(f["flag"], 1)
                dve.wait_ge(f["lt"], (BC + 3) // 4)
                dve.tensor_tensor_scan(F[:, :], fl[:, 0:BE], LT[:, :], -BIG, ALU.add, ALU.max).then_inc(f["flag"], 1)
                dve.tensor_tensor_scan(B[:, ::-1], fl[:, BE:0:-1], LT[:, ::-1], -BIG, ALU.add, ALU.max).then_inc(f["flag"], 1)
                dve.memset(ini[:, :, :, :], -BIG).then_inc(f["flag"], 1)
                dve.memset(tmp[:, :, :], 0.0).then_inc(f["flag"], 1)
                dve.wait_ge(f["row_ps"], 1)
                step(dve.tensor_copy(row[:, :, :, :].rearrange("o n b h -> o (n b h)"), pr[0][0:1, 0:4 * R]))
                for k in range(1, SB_):
                    m = SB_ - 1 - k
                    dve.tensor_tensor(tmp[:, 0, :], row[:, 0, k - 1, :], row[:, 2, k, :], ALU.add)
                    step(dve.tensor_tensor(tmp[:, 1, :], row[:, 1, m + 1, :], row[:, 3, m, :], ALU.add))
                    dve.tensor_tensor(row[:, 0, k, :], row[:, 0, k, :], tmp[:, 0, :], ALU.max)
                    step(dve.tensor_tensor(row[:, 1, m, :], row[:, 1, m, :], tmp[:, 1, :], ALU.max))
                step(dve.tensor_copy(ini[:, 0, 1:SB_, :], row[:, 0, 0:SB_ - 1, :]))
                dve.tensor_copy(ini[:, 1, 0:SB_ - 1, :], row[:, 1, 1:SB_, :]).then_inc(f["row"], 1)
                dve.wait_ge(f["col_ps"], 1)
                step(dve.tensor_copy(col[:, :], pr[1][0:R, 0:2]))
                dve.tensor_tensor_scan(F[:, :], fl[:, 0:BE], LT[:, :], col[:, 0:1], ALU.add, ALU.max)
                step(dve.tensor_tensor_scan(B[:, ::-1], fl[:, BE:0:-1], LT[:, ::-1], col[:, 1:2], ALU.add, ALU.max))
                dve.tensor_tensor(F[:, :], F[:, :], B[:, :], ALU.max).then_inc(f["m"], 1)
                for q in range((BC + 5) // 6):
                    k = min(6, BC - 6 * q)
                    dve.wait_ge(f["m_ps"], q + 1)
                    dve.tensor_tensor(Lb[:, 6 * q:6 * q + k, :, :], Lb[:, 6 * q:6 * q + k, :, :],
                                      pm[q % 2][0:P, 0:k * R].rearrange("p (i b h) -> p i b h", i=k, b=SB_), ALU.subtract)\
                       .then_inc(f["sub"], 1)
                dve.wait_ge(f["hi"], 1)
                dve.scalar_tensor_tensor(env.LP[:, 1, :], L[:, :], UP, env.LP[:, 0, :], ALU.mult, ALU.subtract)


def node_output(env, w, agg):
    env.stage += 1
    nc, X, xnT = env.nc, env.X, env.xnT
    f = {n: env.sem("out_" + n) for n in ("weights", "step", "agg", "tr", "aggT", "ps", "yb", "x", "iota", "head_ps", "head")}
    with ExitStack() as ctx:
        sb = lambda n, sh, d=F32: env.sb(ctx, n, sh, d)
        W1 = sb("oW1", [128, 2 * KC, D])
        B1, B2, BV = sb("oB1", [P, 1, D]), sb("oB2", [P, D]), sb("oBV", [P, D])
        A = sb("oA", [P, T, QW])
        H = sb("oH", [CR, 2, QW])
        ni, nf, OH = sb("oni", [CR, N], I32), sb("onf", [CR, N]), sb("oOH", [CR, T, 2, P])
        den, one = sb("oden", [P, T, NH]), sb("oone", [P, T, NH])
        bv = sb("obv", [P, 2, D])
        m = sb("om", [128, 8])
        aT = sb("oaT", [128, KC, N])
        yb = sb("oyb", [P, 2, D])
        pa, pp = env.banks(ctx, "opa", 2), env.banks(ctx, "opp", 2)
        mlp = NodeMlp(env, ctx, 1, "o", env.XN)
        with nc.Block() as block:
            @block.sync
            def _(sp):
                for to, a in ((W1[:, :, :], rows(w["no_W1"])), (B1[:, 0, :], bcast(w["no_b1"], P, D)), (B2[:, :], bcast(w["no_b2"], P, D)),
                              (BV[:, :], bcast(w["hv_b2"], P, D)), (mlp.W2[:, :, :], rows(w["no_W2"])),
                              (A[:, :, :], agg[0:N, :].rearrange("(t p) d -> p t d", p=P)),
                              (H[:, :, :], agg[N:N + CH, :].rearrange("(p h) d -> p h d", h=2))):
                    sp.dma_start(to, a).then_inc(f["weights"], 16)
                with nc.allow_non_contiguous_dma("512 values as columns"):
                    for to, a in ((mlp.G, "no_g"), (mlp.BE, "no_be")):
                        sp.dma_start(to[:, :], w[a].rearrange("(k p) -> p k", p=128)).then_inc(f["weights"], 16)

            @block.vector
            def _(dve):
                n = [0]

                def step(ins):
                    ins.then_inc(f["step"], 1)
                    n[0] += 1
                    dve.wait_ge(f["step"], n[0])

                def heads_of_chunks():
                    dve.wait_ge(f["iota"], 1)
                    step(dve.tensor_copy(nf[:, :], ni[:, :]))
                    for t in range(T):
                        for h in range(2):
                            last = dve.tensor_scalar(OH[:, t, h, :], nf[:, sl(t)], env.headf[:, h:h + 1], None, ALU.is_equal)
                        last.then_inc(f["head"], 1)
                    for t in range(T):
                        dve.wait_ge(f["head_ps"], t + 1)
                        dve.tensor_tensor(A[:, t, 0:D], A[:, t, 0:D], pp[t % 2][0:P, :], ALU.add)
                        step(dve.tensor_tensor(A[:, t, D:QW], A[:, t, D:QW], pa[t % 2][0:P, 0:NH], ALU.add))

                dve.wait_ge(f["weights"], 16 * 9)
                heads_of_chunks()
                centre(dve, step, W1[:, :, :], 2 * KC, m, 128)
                centre(dve, step, B1[:, :, :], 1, m, P)
                step(dve.tensor_scalar(one[:, :, :], A[:, :, D:QW], 0.0, None, ALU.is_equal))
                step(dve.tensor_tensor(den[:, :, :], A[:, :, D:QW], one[:, :, :], ALU.add))
                dve.reciprocal(den[:, :, :], den[:, :, :])
                step(dve.tensor_scalar(one[:, :, :], one[:, :, :], -1.0, 1.0, ALU.mult, ALU.add))
                heads = lambda a: a.rearrange("p (h d) -> p h d", h=NH)
                wide = lambda a: a.unsqueeze(2).to_broadcast([P, NH, HD])
                for t in range(T):
                    a = A[:, t, 0:D]
                    dve.tensor_tensor(heads(bv[:, t % 2, :]), heads(BV[:, :]), wide(one[:, t, :]), ALU.mult)
                    step(dve.tensor_tensor(heads(a), heads(a), wide(den[:, t, :]), ALU.mult))
                    dve.tensor_tensor(a, a, bv[:, t % 2, :], ALU.add).then_inc(f["agg"], 1)
                for t in range(T):
                    dve.wait_ge(f["ps"], t + 1)
                    dve.tensor_tensor(mlp.hs[:, t, :], pp[t % 2][0:P, :], B1[:, 0, :], ALU.add).then_inc(mlp.s["hs"], 1)
                mlp.dve(dve)
                for t in range(T):
                    dve.wait_ge(mlp.s["y"], T + t + 1)
                    dve.tensor_tensor(yb[:, t % 2, :], mlp.py[t % 2][0:P, :], B2[:, :], ALU.add).then_inc(mlp.s["used"], 1)
                    dve.wait_ge(mlp.s["used"], T + t + 1)
                    dve.tensor_tensor(X[:, t, :], X[:, t, :], yb[:, t % 2, :], ALU.add).then_inc(f["x"], 1)

            @block.gpsimd
            def _(g):
                g.iota(ni[:, :], pattern=[[1, N]], base=0, channel_multiplier=0).then_inc(f["iota"], 1)

            @block.scalar
            def _(act):
                for t in range(T):
                    act.wait_ge(f["tr"], t + 1)
                    act.activation(aT[:, :, sl(t)], pa[t % 2][:, 0:KC * P].rearrange("p (k n) -> p k n", k=KC), ACT.Copy)\
                       .then_inc(f["aggT"], 1)
                mlp.act(act)

            @block.tensor
            def _(pe):
                pe.wait_ge(f["weights"], 16 * 9)
                for t in range(T):
                    pe.wait_ge(f["head"], t + 1)
                    if t >= 2:
                        pe.wait_ge(f["step"], t)
                    for h in range(2):
                        pe.matmul(pp[t % 2][0:P, :], OH[:, t, h, :], H[:, h, 0:D], start=(h == 0), stop=(h == 1))
                    for h in range(2):
                        last = pe.matmul(pa[t % 2][0:P, 0:NH], OH[:, t, h, :], H[:, h, D:QW], start=(h == 0), stop=(h == 1))
                    last.then_inc(f["head_ps"], 1)
                for t in range(T):
                    pe.wait_ge(f["agg"], t + 1)
                    if t >= 2:
                        pe.wait_ge(f["aggT"], t - 1)
                    for k in range(KC):
                        last = pe.transpose(pa[t % 2][:, sl(k)], A[:, t, sl(k, 128)], env.ident[0:P, 0:P])
                    last.then_inc(f["tr"], 1)
                for t in range(T):
                    pe.wait_ge(f["aggT"], t + 1)
                    if t >= 2:
                        pe.wait_ge(mlp.s["hs"], T + t - 1)
                    for k in range(2 * KC):
                        part = aT[:, k, sl(t)] if k < KC else xnT[:, k - KC, sl(t)]
                        last = pe.matmul(pp[t % 2][0:P, :], part, W1[:, k, :], start=(k == 0), stop=(k == 2 * KC - 1))
                    last.then_inc(f["ps"], 1)
                mlp.pe(pe)


STAGES = 99


def build(nc, a, out):
    with ExitStack() as ctx:
        env = Env(nc, ctx)
        sb = lambda n, s, d=F32: env.sb(ctx, n, s, d)
        env.X, env.XN, env.xnT = sb("X", [P, T, D]), sb("XN", [P, T, D]), sb("xnT", [128, KC, N])
        env.ident, env.bd = sb("ident", [128, 128]), sb("bd", [128, 128])
        env.later, env.tri, env.sel = sb("later", [P, P]), sb("tri", [P, NE, NE]), sb("sel", [NE, KC, 128])
        env.ones, env.eps, env.junk = sb("ones", [128, 2]), sb("eps", [128, 1]), sb("junk", [P, 1])
        env.srcf, env.dstf, env.keyf = (sb(n, [P, CH]) for n in ("srcf", "dstf", "keyf"))
        env.headf = sb("headf", [CR, 2])
        env.cnum, env.clater, env.cdel = (sb(n, [P, CH]) for n in ("cnum", "clater", "cdel"))
        env.srci, env.dsti, env.scati, env.cidx = (sb(n, [P, CH], I32) for n in ("srci", "dsti", "scati", "cidx"))
        dram = lambda n, shape: nc.dram_tensor(n, shape, F32, kind="Internal").ap()
        cnt = [dram(f"counts{i}", (N * N + P, 1)) for i in range(TABLES)]
        tab = {"k": dram("hidden_k", (N, D)), "v": dram("hidden_v", (N, D)), "q": dram("queries", (N, QW))}
        agg = dram("aggregate", (N + CH, QW))
        s_dram = dram("s_row", (N,))
        L1 = {k[7:]: v for k, v in a.items() if k.startswith("L1_gnn_")}
        setup(env, a["src"], a["dst"], cnt, agg, a["x"])
        layernorm(env, 0)
        linear_attention(env, 0, a["L0_mix_w_qkv"], a["L0_mix_w_out"], a["L0_mix_b_out"], True, (a["src"], a["dst"], cnt))
        graph_attention(env, a["L0_gnn_W"], a["L0_gnn_b"], a["L0_gnn_a"], cnt, s_dram)
        env.retire("const", "zero", "tables", "index", "x_loaded", "count", "gat_")
        if STAGES > 1:
            layernorm(env, 1)
            experts(env, 0, a["L0_ffn_Wg"], a["L0_ffn_W"], a["L0_ffn_V"], None, a["L0_ffn_W2"], None)
        if STAGES > 2:
            layernorm(env, 2)
            with ExitStack() as edges:
                keep = lambda n, s, d=F32: env.sb(edges, n, s, d)
                env.L = keep("L", [P, CH * NH])
                env.LP = keep("LP", [P, 2, CH * NH], F16)
                env.W1E = {e: keep("W1E" + e, [128, 2, D], F16) for e in "kv"}
                env.W2E = {e: keep("W2E" + e, [128, 2, KC, D], F16) for e in "kv"}
                env.G, env.BE = ({e: keep(n + e, [128, KC]) for e in "kv"} for n in ("edge_g", "edge_be"))
                node_tables(env, L1, tab)
                edge_pass(env, "k", a["edge_attr_128"], tab, L1, a["dst"], agg)
                env.retire("tab_")
                segment_exp(env, a["dst"])
                edge_pass(env, "v", a["edge_attr_128"], tab, L1, a["dst"], agg)
            env.retire("edge_", "seg_")
            node_output(env, L1, agg)
            linear_attention(env, 1, a["L1_mix_W_qkv"], a["L1_mix_W_proj"], a["L1_mix_b_proj"], False)
        if STAGES > 3:
            layernorm(env, 3)
            experts(env, 1, a["L1_ffn_Wr"], a["L1_ffn_W1"], None, a["L1_ffn_b1"], a["L1_ffn_W2"], a["L1_ffn_b2"], out)
        else:
            with nc.Block() as block:
                @block.sync
                def _(sp):
                    sp.dma_start(out.rearrange("(t p) d -> p t d", p=P), env.X[:, :, :]).then_inc(env.sem("dbg"), 16)
                    sp.wait_ge(env.sem("dbg"), 16)


def kernel(**inputs):
    import numpy as np
    import concourse.bacc as bacc
    from concourse.bass_utils import run_bass_kernel_spmd

    nc = bacc.Bacc("TRN2", target_bir_lowering=False, num_devices=1)
    arrays, args = {}, {}
    for name, value in inputs.items():
        value = np.asarray(value)
        if name in ("L1_mix_W_qkv", "L1_mix_W_proj"):
            value = value.T
        value = np.ascontiguousarray(value)
        arrays["in_" + name] = value
        args[name] = nc.dram_tensor("in_" + name, value.shape, mybir.dt.from_np(value.dtype), kind="ExternalInput").ap()
    out = nc.dram_tensor("out", (N, D), F32, kind="ExternalOutput").ap()
    build(nc, args, out)
    return run_bass_kernel_spmd(nc, [arrays], core_ids=[0]).results[0]["out"]
```

```python
from contextlib import ExitStack

import concourse.bass as bass
import concourse.mybir as mybir
from concourse.alu_op_type import AluOpType as ALU

ACT = mybir.ActivationFunctionType
AX = mybir.AxisListType
F32 = mybir.dt.float32
I32 = mybir.dt.int32
F16 = mybir.dt.float16

P = 125
N = 1250
T = N // P
D = 512
KC = D // 128
NB = 250
NN = N // NB
E = 21250
CH = E // P
EF = 128
NE = 8
CAP = 128
NH = 16
HD = D // NH
QW = D + NH
EPS = 1e-5
BIG = 1e30
TABLES = 3
GR = 10
CLEARED = 16 * TABLES * (T + 1)
SCATTERED = [16 * len(range(i, CH, TABLES)) for i in range(TABLES)]
CUT = 130
SB_ = 5
BC = CH // SB_
BE = BC * P
CR = CH // 2

UP = 64.0
UP2 = UP * UP


def sl(t, n=P):
    return slice(t * n, (t + 1) * n)


class Env:

    def __init__(self, nc, ctx):
        self.nc, self.ctx, self.sems, self.stage = nc, ctx, {}, 0

    def sem(self, name):
        if name not in self.sems:
            self.sems[name] = self.nc.alloc_semaphore(name=name)
        return self.sems[name]

    def retire(self, *prefixes):
        old = [n for n in self.sems if n.startswith(prefixes)]
        self.nc.clear_and_free_semaphores([self.sems.pop(n) for n in old])
        self.nc.all_engine_barrier()

    def sb(self, ctx, name, shape, dt=F32):
        return ctx.enter_context(self.nc.sbuf_tensor(f"{name}_{self.stage}", shape, dt))

    def banks(self, ctx, name, n):
        return [ctx.enter_context(self.nc.psum_tensor(f"{name}{i}_{self.stage}", [128, 512], F32)) for i in range(n)]


class Weights:

    def __init__(self, env, ctx, ready, side="right"):
        self.env, self.ctx, self.ready, self.side, self.loads = env, ctx, env.sem(ready), side, []

    def tensor(self, name, shape, *loads):
        to = self.ctx.enter_context(self.env.nc.sbuf_tensor(f"{name}_w{self.env.stage}", shape, F32, side=self.side))
        for place, array in loads:
            self.loads.append((place(to), array))
        return to

    def start(self, sp, first=0, last=None):
        with self.env.nc.allow_non_contiguous_dma("some are 512 values as columns"):
            for to, array in self.loads[first:last]:
                sp.dma_start(to, array).then_inc(self.ready, 16)


def whole(t):
    return t[:, :, :] if len(t.shape) == 3 else t[:, :]


def rows(w):
    return w.rearrange("(k p) m -> p k m", p=128)


def bcast(row, parts, n):
    return row.rearrange("(o n) -> o n", o=1).to_broadcast([parts, n])


def setup(env, src, dst, x, weights, count_rows):
    nc = env.nc
    with ExitStack() as ctx:
        sb = lambda n, s, d=F32: env.sb(ctx, n, s, d)
        rowi = sb("rowi", [CR, 3, 2, P], I32)
        rowf = sb("rowf", [CR, 3, 2, P])
        nextf = sb("nextf", [P, CH])
        lastf = sb("lastf", [P, 1])
        junki = sb("junki", [P, 1], I32)
        tmp, cont, own = sb("tmp", [P, CH]), sb("cont", [P, CH]), sb("own", [P, CH])
        owni = sb("owni", [P, CH], I32)
        endd = sb("endd", [P, CH])
        endr = sb("endr", [CR, 2, P])
        ps = env.banks(ctx, "ps", 4)
        s_mem, s_sel, s_zero = env.sem("const_cleared"), env.sem("const_ready"), env.sem("zero_ready")
        s_row, s_rowf, s_tr, s_col, s_pad, s_x = (env.sem("index_rows_loaded"), env.sem("index_rows_float"),
                                             env.sem("index_columns"), env.sem("index_step"), env.sem("index_padded"),
                                             env.sem("x_loaded"))
        with nc.Block() as block:
            @block.sync
            def _(sp):
                sp.wait_ge(s_pad, 1)
                for n, a in enumerate((src, dst)):
                    sp.dma_start(rowi[:, n, :, :], a.rearrange("(p h e) -> p h e", h=2, e=P)).then_inc(s_row, 16)
                m = 84 * 2 * P
                sp.dma_start(rowi[0:84, 2, :, :], dst[1:1 + m].rearrange("(p h e) -> p h e", h=2, e=P)).then_inc(s_row, 16)
                sp.dma_start(rowi[84:85, 2, 0, :], dst[1 + m:1 + m + P].rearrange("(p e) -> p e", e=P)).then_inc(s_row, 16)
                sp.dma_start(rowi[84:85, 2, 1, 0:P - 1], dst[1 + m + P:E].rearrange("(p e) -> p e", e=P - 1)).then_inc(s_row, 16)
                sp.dma_start(env.X[:, :, :], x.rearrange("(t p) d -> p t d", p=P)).then_inc(s_x, 16)
                weights.start(sp)
                for g in range(2):
                    load_count_rows(env, sp, src, dst, count_rows, g)

            @block.gpsimd
            def _(g):
                for n, (m, v) in enumerate(((env.ident, 0.0), (env.bd, 0.0), (env.later, 1.0), (env.tri, 1.0),
                                            (env.sel, 0.0), (lastf, 0.0))):
                    if n:
                        g.wait_ge(s_mem, n)
                    g.memset(m[:], v).then_inc(s_mem, 1)
                g.wait_ge(s_mem, 6)
                g.affine_select(out=env.ident[:, :], in_=env.ident[:, :], compare_op=ALU.not_equal, fill=1.0,
                                base=0, pattern=[[-1, 128]], channel_multiplier=1).then_inc(s_sel, 1)
                g.wait_ge(s_sel, 1)
                g.memset(env.bd[0:64, 0:64], 1.0).then_inc(s_sel, 1)
                g.wait_ge(s_sel, 2)
                g.memset(env.bd[64:128, 64:128], 1.0).then_inc(s_sel, 1)
                g.wait_ge(s_sel, 3)
                g.affine_select(out=env.later[:, :], in_=env.later[:, :], compare_op=ALU.is_gt, fill=0.0,
                                base=0, pattern=[[1, P]], channel_multiplier=-1).then_inc(s_sel, 1)
                g.wait_ge(s_sel, 4)
                g.affine_select(out=env.tri[:, :, :], in_=env.tri[:, :, :], compare_op=ALU.is_gt, fill=0.0,
                                base=0, pattern=[[1, NE], [-1, NE]], channel_multiplier=0).then_inc(s_sel, 1)
                g.wait_ge(s_sel, 5)
                g.affine_select(out=env.sel[:, :, :].rearrange("e b (h f) -> e (b h) f", h=2),
                                in_=env.sel[:, :, :].rearrange("e b (h f) -> e (b h) f", h=2),
                                compare_op=ALU.not_equal, fill=1.0, base=0, pattern=[[-1, NE], [0, 64]],
                                channel_multiplier=1).then_inc(s_sel, 1)
                g.wait_ge(s_sel, 6)
                g.affine_select(out=lastf[:, :], in_=lastf[:, :], compare_op=ALU.not_equal, fill=1.0,
                                base=-(P - 1), pattern=[[0, 1]], channel_multiplier=1).then_inc(s_sel, 1)
                g.wait_ge(s_sel, 7)
                g.iota(junki[:, :], pattern=[[0, 1]], base=N * N, channel_multiplier=1).then_inc(s_sel, 1)
                g.wait_ge(s_sel, 8)
                g.iota(owni[:, :], pattern=[[1, CH]], base=N, channel_multiplier=0).then_inc(s_sel, 1)

            @block.vector
            def _(dve):
                dve.memset(rowi[:, :, :, :], -1).then_inc(s_pad, 1)
                dve.memset(env.zero[:, :], 0.0).then_inc(s_zero, 1)
                dve.memset(env.ones[:, :], 1.0).then_inc(s_zero, 1)
                dve.memset(env.eps[:, :], EPS).then_inc(s_zero, 1)
                dve.wait_ge(s_row, 80)
                dve.tensor_copy(rowf[:, :, :, :], rowi[:, :, :, :]).then_inc(s_rowf, 1)
                dve.wait_ge(s_rowf, 1)
                dve.tensor_copy(endr[:, :, :], rowf[:, 1, :, P - 1:P].to_broadcast([CR, 2, P])).then_inc(s_rowf, 1)
                dve.tensor_copy(env.headf[:, :], rowf[:, 1, :, 0]).then_inc(s_rowf, 1)
                dve.wait_ge(s_sel, 9)
                dve.tensor_copy(env.junk[:, :], junki[:, :]).then_inc(s_col, 1)
                dve.tensor_copy(own[:, :], owni[:, :]).then_inc(s_col, 1)
                dve.wait_ge(s_tr, 1)
                for n, to in enumerate((env.srcf, env.dstf, nextf, endd)):
                    dve.tensor_copy(to[:, :].rearrange("p (c h) -> p h c", h=2),
                                    ps[n][0:P, 0:CH].rearrange("p (h c) -> p h c", h=2)).then_inc(s_col, 1)
                dve.wait_ge(s_col, 6)
                dve.tensor_copy(env.srci[:, :], env.srcf[:, :]).then_inc(s_col, 1)
                dve.tensor_copy(env.dsti[:, :], env.dstf[:, :]).then_inc(s_col, 1)
                dve.scalar_tensor_tensor(env.keyf[:, :], env.dstf[:, :], float(N), env.srcf[:, :], ALU.mult, ALU.add)\
                   .then_inc(s_col, 1)
                dve.memset(cont[:, 0:1], 0.0).then_inc(s_col, 1)
                dve.tensor_tensor(cont[:, 1:CH], env.dstf[:, 1:CH], endd[:, 0:CH - 1], ALU.is_equal).then_inc(s_col, 1)
                dve.tensor_tensor(own[:, :], own[:, :], env.dstf[:, :], ALU.subtract).then_inc(s_col, 1)
                dve.tensor_tensor(tmp[:, :], env.dstf[:, :], nextf[:, :], ALU.is_equal).then_inc(s_col, 1)
                dve.tensor_scalar(lastf[:, :], lastf[:, :], -float(4 * N), float(4 * N), ALU.mult, ALU.add).then_inc(s_col, 1)
                dve.wait_ge(s_col, 14)
                dve.tensor_tensor(own[:, :], own[:, :], cont[:, :], ALU.mult).then_inc(s_col, 1)
                dve.scalar_tensor_tensor(tmp[:, :], tmp[:, :], lastf[:, 0:1], env.dstf[:, :], ALU.mult, ALU.add).then_inc(s_col, 1)
                dve.wait_ge(s_col, 16)
                dve.tensor_tensor(env.scati[:, :], tmp[:, :], own[:, :], ALU.add).then_inc(s_col, 1)

            @block.tensor
            def _(pe):
                pe.wait_ge(s_rowf, 3)
                pe.wait_ge(s_sel, 9)
                for n in range(3):
                    for h in range(2):
                        pe.transpose(ps[n][0:P, sl(h, CR)], rowf[:, n, h, :], env.ident[0:CR, 0:CR])
                for h in range(2):
                    last = pe.transpose(ps[3][0:P, sl(h, CR)], endr[:, h, :], env.ident[0:CR, 0:CR])
                last.then_inc(s_tr, 1)


def load_count_rows(env, sp, src, dst, count_rows, g):
    for a, to in zip((dst, src), count_rows):
        sp.dma_start(to[:, g % 2, :], bcast(a[g * GR * P:(g + 1) * GR * P], P, GR * P))\
          .then_inc(env.sem(f"count_rows_loaded{g % 2}"), 16)


def clear_counts(env, sp, cnt):
    cleared = env.sem("tables_cleared")
    sp.wait_ge(env.sem("zero_ready"), 3)
    for table in cnt:
        for k in range(T):
            sp.dma_start(table[k * P * N:(k + 1) * P * N, :].rearrange("(p a) o -> p (a o)", p=P), env.zero[:, 0:N])\
              .then_inc(cleared, 16)
        sp.dma_start(table[N * N:N * N + P, :], env.zero[:, 0:1]).then_inc(cleared, 16)


def clear_aggregate(env, sp, agg):
    for k in range(0, N + CH, P):
        m = min(P, N + CH - k)
        sp.dma_start(agg[k:k + m, :], env.zero[0:m, 0:QW]).then_inc(env.sem("aggregate_cleared"), 16)
    sp.wait_ge(env.sem("aggregate_cleared"), 16 * ((N + CH + P - 1) // P))


class Layernorm:

    def __init__(self, env, ctx, call, banks):
        self.env, self.b, self.ps = env, T * call, banks
        self.st, self.mv = env.sb(ctx, "ln_st", [P, T, 6]), env.sb(ctx, "ln_mv", [P, T, 2])
        self.sd, self.rs = env.sb(ctx, "ln_sd", [P, T]), env.sb(ctx, "ln_rs", [P, T])
        self.s = {n: env.sem("ln_" + n) for n in ("stats", "moments", "var", "std", "rstd", "xn", "transposed", "xnT")}

    def moments(self, dve, t, made=None):
        s, b, t1 = self.s, self.b, slice(t, t + 1)
        if made:
            dve.wait_ge(*made)
        dve.bn_stats(self.st[:, t, :], self.env.X[:, t, :]).then_inc(s["stats"], 1)
        dve.wait_ge(s["stats"], b + t + 1)
        dve.bn_aggr(self.mv[:, t, :], self.st[:, t, :]).then_inc(s["moments"], 1)
        dve.wait_ge(s["moments"], b + t + 1)
        dve.tensor_scalar(self.sd[:, t1], self.mv[:, t, 1:2], EPS, None, ALU.add).then_inc(s["var"], 1)

    def normalise(self, dve, t):
        s, b, t1 = self.s, self.b, slice(t, t + 1)
        dve.wait_ge(s["std"], b + t + 1)
        dve.reciprocal(self.rs[:, t1], self.sd[:, t1]).then_inc(s["rstd"], 1)
        dve.wait_ge(s["rstd"], b + t + 1)
        dve.tensor_scalar(self.env.XN[:, t, :], self.env.X[:, t, :], self.mv[:, t, 0:1], self.rs[:, t1], ALU.subtract, ALU.mult)\
           .then_inc(s["xn"], 1)

    def root(self, act, t):
        act.wait_ge(self.s["var"], self.b + t + 1)
        act.activation(self.sd[:, t:t + 1], self.sd[:, t:t + 1], ACT.Sqrt).then_inc(self.s["std"], 1)

    def copy(self, act, t):
        act.wait_ge(self.s["transposed"], self.b + t + 1)
        act.activation(self.env.xnT[:, :, sl(t)], self.ps[t % len(self.ps)][:, 0:KC * P].rearrange("p (k n) -> p k n", k=KC), ACT.Copy)\
           .then_inc(self.s["xnT"], 1)

    def act(self, act):
        for t in range(T + 2):
            if t < T:
                self.root(act, t)
            if t >= 2:
                self.copy(act, t - 2)

    def flip(self, pe, t):
        s, b, n = self.s, self.b, len(self.ps)
        pe.wait_ge(s["xn"], b + t + 1)
        if t >= n:
            pe.wait_ge(s["xnT"], b + t - n + 1)
        for k in range(KC):
            last = pe.transpose(self.ps[t % n][:, sl(k)], self.env.XN[:, t, sl(k, 128)], self.env.ident[0:P, 0:P])
        last.then_inc(s["transposed"], 1)


def first_layernorm(env, cnt):
    env.stage += 1
    nc = env.nc
    with ExitStack() as ctx:
        ln = Layernorm(env, ctx, 0, env.banks(ctx, "ln_ps", 2))
        with nc.Block() as block:
            @block.sync
            def _(sp):
                clear_counts(env, sp, cnt)

            @block.vector
            def _(dve):
                dve.wait_ge(env.sem("x_loaded"), 16)
                for t in range(T + 1):
                    if t < T:
                        ln.moments(dve, t)
                    if t:
                        ln.normalise(dve, t - 1)

            @block.scalar
            def _(act):
                ln.act(act)

            @block.tensor
            def _(pe):
                for t in range(T):
                    ln.flip(pe, t)


def mix_weights(env, ctx, wqkv, wout, bout, side="right"):
    w = Weights(env, ctx, "mix_weights", side)
    w.qkv = w.tensor("mixW", [128, KC, 3 * D], (whole, rows(wqkv)))
    w.out = w.tensor("mixWO", [128, KC, D], (whole, rows(wout)))
    w.bias = w.tensor("mixBO", [P, D], (whole, bcast(bout, P, D)))
    return w


def scatter_counts(env, g, cnt, first, last):
    c_fin = env.sem("count_ready")
    c_put = [env.sem(f"count_scattered{i}") for i in range(TABLES)]
    for c in range(first, last):
        if c % GR == 0:
            g.wait_ge(c_fin, c // GR + 1)
        if c >= TABLES:
            g.wait_ge(c_put[c % TABLES], 16 * (c // TABLES))
        g.indirect_dma_start(out=cnt[c % TABLES][:, :],
                             out_offset=bass.IndirectOffsetOnAxis(ap=env.cidx[:, c:c + 1], axis=0),
                             in_=env.cnum[:, c:c + 1], in_offset=None, compute_op=ALU.add)\
         .then_inc(c_put[c % TABLES], 16)


def linear_attention(env, call, w, elu, counts=None, ahead=None):
    env.stage += 1
    nc, X, xnT = env.nc, env.X, env.xnT
    names = ("mix_weights", "mix_k_done", "mix_v_done", "mix_k_neg", "mix_k_exp", "mix_kf", "mix_v", "mix_kv", "mix_kvbd",
             "mix_ksb", "mix_kvT_ps", "mix_kvT", "mix_m_ps", "mix_m", "mix_q_ps", "mix_q_neg", "mix_q_exp", "mix_q",
             "mix_den_ps", "mix_den", "mix_rden", "mix_z_ps", "mix_qs", "mix_y_ps", "mix_yb", "mix_x", "mix_ones")
    s = {n: env.sem(n) for n in names}
    SCALE = 64 ** -0.5
    U = KC * NN
    with ExitStack() as ctx:
        sb = lambda n, sh, d=F32: env.sb(ctx, n, sh, d)
        W, WO, BO = w.qkv, w.out, w.bias
        kf = sb("kf", [P, 2, D])
        kn = sb("kn", [P, 2, D])
        v = sb("v", [P, 2, KC, 130])
        qT = sb("qT", [128, KC, N])
        qn = sb("qn", [128, 2, NB])
        kvbd = sb("kvbd", [128, KC, 128])
        ks = sb("ks", [128, KC, NE])
        kvT = sb("kvT", [128, KC, 128])
        M = sb("M", [128, KC, D])
        dn = sb("dn", [NE, N])
        yb = sb("yb", [P, 2, D])
        if counts:
            keyrow = sb("keyrow", [P, GR * P])
            eq = env.eq
        ring = env.banks(ctx, "ring", 4)
        kvp = env.banks(ctx, "kvp", 4)
        src, dst, cnt, agg, count_rows = counts or (None, None, None, None, (None, None))
        dr, sr = count_rows
        if counts:
            c_key, c_num, c_idx, c_fin = (env.sem(n) for n in ("count_keys", "count_compared", "count_step", "count_ready"))
            c_slot = [env.sem(f"count_rows_loaded{i}") for i in range(2)]

        with nc.Block() as block:
            @block.sync
            def _(sp):
                if ahead:
                    ahead.start(sp)
                if counts:
                    for g in range(2, CH // GR):
                        sp.wait_ge(c_key, g - 1)
                        load_count_rows(env, sp, src, dst, count_rows, g)
                        if g == 2:
                            clear_counts(env, sp, cnt[2:])
                    clear_aggregate(env, sp, agg)

            if counts:
                @block.gpsimd
                def _(g):
                    g.wait_ge(env.sem("tables_cleared"), CLEARED)
                    scatter_counts(env, g, cnt, 0, CUT)

            @block.vector
            def _(dve):
                def count_keys(g):
                    dve.wait_ge(c_slot[g % 2], 32 * (g // 2 + 1))
                    if g:
                        dve.wait_ge(c_num, 2 * GR * g)
                    dve.scalar_tensor_tensor(keyrow[:, :], dr[:, g % 2, :], float(N), sr[:, g % 2, :], ALU.mult, ALU.add)\
                       .then_inc(c_key, 1)
                    dve.wait_ge(c_key, g + 1)

                def count_chunk(c):
                    row = keyrow[:, sl(c % GR)]
                    u = c % 2
                    if c >= 2:
                        dve.wait_ge(c_num, 2 * (c - 1))
                    dve.tensor_scalar(eq[:, u, 0, :], row, env.keyf[:, c:c + 1], 0.0, ALU.is_equal, ALU.add,
                                      accum_out=env.cnum[:, c:c + 1]).then_inc(c_num, 1)
                    dve.scalar_tensor_tensor(eq[:, u, 1, :], row, env.keyf[:, c:c + 1], env.later[:, :],
                                             ALU.is_equal, ALU.mult, accum_out=env.clater[:, c:c + 1]).then_inc(c_num, 1)

                def count_rows_of(g):
                    cs = slice(g * GR, (g + 1) * GR)
                    dve.wait_ge(c_num, 2 * GR * (g + 1))
                    dve.tensor_scalar(env.clater[:, cs], env.clater[:, cs], 0.0, None, ALU.is_equal).then_inc(c_idx, 1)
                    dve.tensor_scalar(env.cdel[:, cs], env.keyf[:, cs], env.junk[:, 0:1], None, ALU.subtract).then_inc(c_idx, 1)
                    dve.wait_ge(c_idx, 3 * g + 2)
                    dve.tensor_tensor(env.cdel[:, cs], env.cdel[:, cs], env.clater[:, cs], ALU.mult).then_inc(c_idx, 1)
                    dve.wait_ge(c_idx, 3 * g + 3)
                    dve.tensor_scalar(env.cidx[:, cs], env.cdel[:, cs], env.junk[:, 0:1], None, ALU.add).then_inc(c_fin, 1)

                counted = [0]

                def count(n):
                    for c in range(counted[0], min(CH, counted[0] + n) if counts else 0):
                        if c % GR == 0:
                            count_keys(c // GR)
                        count_chunk(c)
                        if c % GR == GR - 1:
                            count_rows_of(c // GR)
                        counted[0] = c + 1

                count(GR)
                dve.memset(v[:, :, :, :], 1.0).then_inc(s["mix_ones"], 1)
                dve.memset(ks[:, :, :], 0.0).then_inc(s["mix_ones"], 1)
                dve.wait_ge(s["mix_weights"], 48 * (call + 1))
                b = T * call
                for t in range(T):
                    u = t % 2
                    dve.wait_ge(s["mix_k_done"], b + t + 1)
                    if t >= 2:
                        dve.wait_ge(s["mix_kv"], b + t - 1)
                    if elu:
                        dve.tensor_scalar(kn[:, u, :], ring[u][0:P, :], 0.0, None, ALU.min).then_inc(s["mix_k_neg"], 1)
                        dve.wait_ge(s["mix_k_exp"], t + 1)
                        dve.scalar_tensor_tensor(kf[:, u, :], ring[u][0:P, :], 0.0, kn[:, u, :], ALU.max, ALU.add)\
                           .then_inc(s["mix_kf"], 1)
                    else:
                        dve.tensor_scalar(kf[:, u, :], ring[u][0:P, :], 0.0, SCALE, ALU.max, ALU.add).then_inc(s["mix_kf"], 1)
                    count((2, 2, 3, 3, 5, 5)[t] if t < 6 else 8)
                dve.wait_ge(s["mix_kv"], b + T)
                dve.wait_ge(s["mix_ones"], 2 * (call + 1))
                for j in range(KC):
                    dve.tensor_tensor(kvbd[:, j, :], kvp[j][:, 0:128], env.bd[:, :], ALU.mult).then_inc(s["mix_kvbd"], 1)
                    dve.tensor_scalar(ks[:, j, 2 * j:2 * j + 2], env.bd[:, 0:128:64], kvp[j][:, 128:129], None, ALU.mult)\
                       .then_inc(s["mix_ksb"], 1)
                for n in range(U):
                    j, m = n // NN, n % NN
                    q = qT[:, j, sl(m, NB)]
                    dve.wait_ge(s["mix_q_ps"], U * call + n + 1)
                    if elu:
                        dve.tensor_scalar(qn[:, n % 2, :], ring[n % 4][:, 0:NB], 0.0, None, ALU.min).then_inc(s["mix_q_neg"], 1)
                        dve.wait_ge(s["mix_q_exp"], n + 1)
                        dve.scalar_tensor_tensor(q, ring[n % 4][:, 0:NB], 0.0, qn[:, n % 2, :], ALU.max, ALU.add)\
                           .then_inc(s["mix_q"], 1)
                    else:
                        dve.tensor_scalar(q, ring[n % 4][:, 0:NB], 0.0, SCALE, ALU.max, ALU.add).then_inc(s["mix_q"], 1)
                    count(2)
                for m in range(NN):
                    k = NN * call + m + 1
                    z = dn[:, sl(m, NB)]
                    dve.wait_ge(s["mix_den_ps"], k)
                    dve.tensor_scalar(z, kvp[m % 4][0:NE, 0:NB], 1e-6, None, ALU.add).then_inc(s["mix_den"], 1)
                    dve.wait_ge(s["mix_den"], k)
                    dve.reciprocal(z, z).then_inc(s["mix_rden"], 1)
                for n in range(U):
                    m, j = n // KC, n % KC
                    q = qT[:, j, sl(m, NB)]
                    dve.wait_ge(s["mix_z_ps"], U * call + n + 1)
                    dve.tensor_tensor(q, q, ring[n % 4][:, 0:NB], ALU.mult).then_inc(s["mix_qs"], 1)
                    count(1)
                for t in range(T):
                    dve.wait_ge(s["mix_y_ps"], b + t + 1)
                    dve.tensor_tensor(yb[:, t % 2, :], ring[t % 4][0:P, :], BO[:, :], ALU.add).then_inc(s["mix_yb"], 1)
                    dve.wait_ge(s["mix_yb"], b + t + 1)
                    dve.tensor_tensor(X[:, t, :], X[:, t, :], yb[:, t % 2, :], ALU.add).then_inc(s["mix_x"], 1)
                    count(5)

            @block.scalar
            def _(act):
                b = T * call
                act.wait_ge(s["mix_ones"], 2 * call + 1)
                for t in range(T):
                    u = t % 2
                    if elu:
                        act.wait_ge(s["mix_k_neg"], t + 1)
                        act.activation(kn[:, u, :], kn[:, u, :], ACT.Exp).then_inc(s["mix_k_exp"], 1)
                    act.wait_ge(s["mix_v_done"], b + t + 1)
                    if t >= 2:
                        act.wait_ge(s["mix_kv"], b + t - 1)
                    act.activation(v[:, u, :, 0:128], ring[2 + u][0:P, :].rearrange("p (j m) -> p j m", j=KC), ACT.Copy)\
                       .then_inc(s["mix_v"], 1)
                if elu:
                    for n in range(4):
                        act.wait_ge(s["mix_q_neg"], n + 1)
                        act.activation(qn[:, n % 2, :], qn[:, n % 2, :], ACT.Exp).then_inc(s["mix_q_exp"], 1)
                for j in range(KC):
                    act.wait_ge(s["mix_kvT_ps"], KC * call + j + 1)
                    act.activation(kvT[:, j, :], kvp[j][:, 0:128], ACT.Copy).then_inc(s["mix_kvT"], 1)
                for j in range(KC):
                    act.wait_ge(s["mix_m_ps"], KC * call + j + 1)
                    act.activation(M[:, j, :], kvp[j][:, :], ACT.Copy).then_inc(s["mix_m"], 1)
                if elu:
                    for n in range(4, U):
                        act.wait_ge(s["mix_q_neg"], n + 1)
                        act.activation(qn[:, n % 2, :], qn[:, n % 2, :], ACT.Exp).then_inc(s["mix_q_exp"], 1)

            @block.tensor
            def _(pe):
                b = T * call

                def product(ps, t, w, col):
                    for k in range(KC):
                        last = pe.matmul(ps, xnT[:, k, sl(t)], w[:, k, col:col + D], start=(k == 0), stop=(k == KC - 1))
                    return last

                def kv(t):
                    pe.wait_ge(s["mix_kf"], b + t + 1)
                    pe.wait_ge(s["mix_v"], b + t + 1)
                    for j in range(KC):
                        last = pe.matmul(kvp[j][:, 0:129], kf[:, t % 2, sl(j, 128)], v[:, t % 2, j, 0:129],
                                         start=(t == 0), stop=(t == T - 1))
                    last.then_inc(s["mix_kv"], 1)

                pe.wait_ge(s["mix_weights"], 48 * (call + 1))
                for t in range(T):
                    if t >= 2:
                        pe.wait_ge(s["mix_kf"], b + t - 1)
                        pe.wait_ge(s["mix_v"], b + t - 1)
                    product(ring[t % 2][0:P, :], t, W, D).then_inc(s["mix_k_done"], 1)
                    product(ring[2 + t % 2][0:P, :], t, W, 2 * D).then_inc(s["mix_v_done"], 1)
                    if t:
                        kv(t - 1)
                kv(T - 1)

                def q_product(n):
                    j, m = n // NN, n % NN
                    if n < 4:
                        pe.wait_ge(s["mix_kf"], b + T)
                        pe.wait_ge(s["mix_v"], b + T)
                    else:
                        pe.wait_ge(s["mix_q"], U * call + n - 3)
                    for k in range(KC):
                        last = pe.matmul(ring[n % 4][:, 0:NB], W[:, k, sl(j, 128)], xnT[:, k, sl(m, NB)],
                                         start=(k == 0), stop=(k == KC - 1))
                    last.then_inc(s["mix_q_ps"], 1)

                for n in range(4):
                    q_product(n)
                for j in range(KC):
                    pe.wait_ge(s["mix_kvbd"], KC * call + j + 1)
                    pe.wait_ge(s["mix_ksb"], KC * call + j + 1)
                    pe.transpose(kvp[j][:, 0:128], kvbd[:, j, :], env.ident[:, :]).then_inc(s["mix_kvT_ps"], 1)
                for j in range(KC):
                    pe.wait_ge(s["mix_kvT"], KC * call + j + 1)
                    pe.matmul(kvp[j][:, :], kvT[:, j, :], WO[:, j, :], start=True, stop=True).then_inc(s["mix_m_ps"], 1)
                for n in range(4, U):
                    q_product(n)
                pe.wait_ge(s["mix_q"], U * (call + 1))
                pe.wait_ge(s["mix_m"], KC * (call + 1))
                for m in range(NN):
                    if m >= 4:
                        pe.wait_ge(s["mix_den"], NN * call + m - 3)
                    for j in range(KC):
                        last = pe.matmul(kvp[m % 4][0:NE, 0:NB], ks[:, j, :], qT[:, j, sl(m, NB)],
                                         start=(j == 0), stop=(j == KC - 1))
                    last.then_inc(s["mix_den_ps"], 1)
                for n in range(U):
                    m, j = n // KC, n % KC
                    pe.wait_ge(s["mix_rden"], NN * call + m + 1)
                    if n >= 4:
                        pe.wait_ge(s["mix_qs"], U * call + n - 3)
                    pe.matmul(ring[n % 4][:, 0:NB], env.sel[:, j, :], dn[:, sl(m, NB)], start=True, stop=True)\
                      .then_inc(s["mix_z_ps"], 1)
                pe.wait_ge(s["mix_qs"], U * (call + 1))
                for t in range(T):
                    if t >= 4:
                        pe.wait_ge(s["mix_x"], b + t - 3)
                    for j in range(KC):
                        last = pe.matmul(ring[t % 4][0:P, :], qT[:, j, sl(t)], M[:, j, :], start=(j == 0), stop=(j == KC - 1))
                    last.then_inc(s["mix_y_ps"], 1)


def gat_weights(env, ctx, W_, b_, a_):
    w = Weights(env, ctx, "gat_weights")
    w.W = w.tensor("gatW", [128, KC, D], (whole, rows(W_)))
    w.B = w.tensor("gatB", [P, D], (whole, bcast(b_, P, D)))
    w.A = w.tensor("gatA", [P, 2 * D], (whole, bcast(a_.rearrange("n o -> (n o)"), P, 2 * D)))
    return w


def graph_attention(env, w, cnt, s_dram, ct, ahead):
    env.stage += 1
    nc, X, xnT = env.nc, env.X, env.xnT
    g = {n: env.sem("gat_" + n) for n in ("weights", "emb_ps", "emb", "s", "t", "s_out", "s_row", "cnt0", "cnt1", "leak", "leak2", "leak3",
                                          "exp", "num", "at", "ps", "rec", "x", "num2")}
    YB = T // 2
    with ExitStack() as ctx:
        sb = lambda n, sh, d=F32: env.sb(ctx, n, sh, d)
        W, B, A = w.W, w.B, w.A
        emb = sb("emb", [P, T, D])
        junk = sb("gjunk", [P, 2, D])
        sc = sb("gs", [P, T])
        tc = sb("gt", [P, T])
        srow = sb("srow", [P, N])
        ct = ct[0:P, :].rearrange("p (u i n) -> p u i n", u=2, i=TABLES)
        z = sb("gz", [P, 2, N])
        AT = sb("AT", [P, T, N])
        rec = sb("grec", [P, T])
        pe_ps = env.banks(ctx, "gp", 2)
        ysum = env.banks(ctx, "gy", YB)
        rsum = pe_ps
        ln = Layernorm(env, ctx, 1, env.banks(ctx, "gln", 1))
        slots = (g["cnt0"], g["cnt1"])
        with nc.Block() as block:
            @block.sync
            def _(sp):
                sp.wait_ge(g["s"], T)
                with nc.allow_non_contiguous_dma("1250 values, turned from columns to a row"):
                    sp.dma_start(s_dram.rearrange("(t p) -> p t", p=P), sc[:, :]).then_inc(g["s_out"], 16)
                sp.wait_ge(g["s_out"], 16)
                sp.dma_start(srow[:, :], bcast(s_dram, P, N)).then_inc(g["s_row"], 16)
                for i in range(TABLES):
                    sp.wait_ge(env.sem(f"count_scattered{i}"), SCATTERED[i])
                for j in range(T):
                    if j >= 2:
                        sp.wait_ge(g["at"], j - 1)
                    for i in range(TABLES):
                        sp.dma_start(ct[:, j % 2, i, :], cnt[i][0:N * N, :].rearrange("(j s) o -> j (s o)", s=N)[sl(j), :])\
                          .then_inc(slots[j % 2], 16)
                sp.wait_ge(g["at"], T)
                ahead.start(sp)

            @block.gpsimd
            def _(pool):
                scatter_counts(env, pool, cnt, CUT, CH)
                for i in range(TABLES):
                    pool.wait_ge(env.sem(f"count_scattered{i}"), SCATTERED[i])

            @block.vector
            def _(dve):
                dve.wait_ge(g["weights"], 48)
                for t in range(T):
                    dve.wait_ge(g["emb_ps"], t + 1)
                    dve.tensor_tensor(emb[:, t, :], pe_ps[t % 2][0:P, :], B[:, :], ALU.add).then_inc(g["emb"], 1)
                    dve.wait_ge(g["emb"], t + 1)
                    if t:
                        dve.wait_ge(g["s"], t)
                        dve.wait_ge(g["t"], t)
                    dve.scalar_tensor_tensor(junk[:, 0, :], emb[:, t, :], 1.0, A[:, 0:D], ALU.mult, ALU.mult,
                                             accum_out=sc[:, t:t + 1]).then_inc(g["s"], 1)
                    dve.scalar_tensor_tensor(junk[:, 1, :], emb[:, t, :], 1.0, A[:, D:2 * D], ALU.mult, ALU.mult,
                                             accum_out=tc[:, t:t + 1]).then_inc(g["t"], 1)
                dve.wait_ge(g["s_row"], 16)
                dve.wait_ge(g["t"], T)
                def leaky(j):
                    if j >= 2:
                        dve.wait_ge(g["leak2"], j - 1)
                    dve.tensor_scalar(z[:, j % 2, :], srow[:, :], tc[:, j:j + 1], None, ALU.add).then_inc(g["leak"], 1)
                    dve.wait_ge(g["leak"], j + 1)
                    dve.scalar_tensor_tensor(AT[:, j, :], z[:, j % 2, :], 0.1, z[:, j % 2, :], ALU.mult, ALU.max).then_inc(g["leak2"], 1)

                def times_counts(j):
                    u = j % 2
                    dve.wait_ge(slots[u], 16 * TABLES * (j // 2 + 1))
                    num = ct[:, u, 0, :]
                    dve.tensor_tensor(num, num, ct[:, u, 1, :], ALU.add).then_inc(g["num2"], 1)
                    dve.wait_ge(g["num2"], j + 1)
                    dve.tensor_tensor(num, num, ct[:, u, 2, :], ALU.add).then_inc(g["num"], 1)
                    dve.wait_ge(g["exp"], j + 1)
                    dve.wait_ge(g["num"], j + 1)
                    dve.tensor_tensor(AT[:, j, :], AT[:, j, :], num, ALU.mult).then_inc(g["at"], 1)

                leaky(0)
                for j in range(T):
                    if j + 1 < T:
                        leaky(j + 1)
                    times_counts(j)
                for t in range(T):
                    dve.wait_ge(g["ps"], t + 1)
                    dve.reciprocal(rec[:, t:t + 1], rsum[t % 2][0:P, 0:1]).then_inc(g["rec"], 1)
                    dve.wait_ge(g["rec"], t + 1)
                    dve.scalar_tensor_tensor(X[:, t, :], ysum[t % YB][0:P, :], rec[:, t:t + 1], X[:, t, :], ALU.mult, ALU.add)\
                       .then_inc(g["x"], 1)
                    ln.moments(dve, t, (g["x"], t + 1))
                    if t:
                        ln.normalise(dve, t - 1)
                ln.normalise(dve, T - 1)

            @block.scalar
            def _(act):
                for j in range(T):
                    act.wait_ge(g["leak2"], j + 1)
                    act.activation(AT[:, j, :], AT[:, j, :], ACT.Exp).then_inc(g["exp"], 1)
                ln.act(act)

            @block.tensor
            def _(pe):
                pe.wait_ge(g["weights"], 48)
                for t in range(T):
                    if t >= 2:
                        pe.wait_ge(g["emb"], t - 1)
                    for k in range(KC):
                        last = pe.matmul(pe_ps[t % 2][0:P, :], xnT[:, k, sl(t)], W[:, k, :], start=(k == 0), stop=(k == KC - 1))
                    last.then_inc(g["emb_ps"], 1)
                pe.wait_ge(g["emb"], T)
                for j in range(T):
                    pe.wait_ge(g["at"], j + 1)
                    for t in range(YB):
                        pe.matmul(ysum[t][0:P, :], AT[:, j, sl(t)], emb[:, j, :], start=(j == 0), stop=(j == T - 1))
                for t in range(T):
                    if t >= 2:
                        pe.wait_ge(g["x"], t - 1)
                    if t >= YB:
                        pe.wait_ge(g["x"], t - YB + 1)
                        for j in range(T):
                            pe.matmul(ysum[t % YB][0:P, :], AT[:, j, sl(t)], emb[:, j, :], start=(j == 0), stop=(j == T - 1))
                    for j in range(T):
                        last = pe.matmul(rsum[t % 2][0:P, 0:2], AT[:, j, sl(t)], env.ones[0:P, 0:2], start=(j == 0), stop=(j == T - 1))
                    last.then_inc(g["ps"], 1)
                    if t >= 2:
                        ln.flip(pe, t - 2)
                ln.flip(pe, T - 2)
                ln.flip(pe, T - 1)


def expert_weights(env, ctx, wr, w1, wv, b1, w2, b2, side="right", place=None):
    w = Weights(env, ctx, "ffn_weights", side)
    used = [0]

    def large(name, *loads):
        if place is None:
            return w.tensor(name, [128, KC, D], *loads)
        i, used[0] = used[0], used[0] + 1
        view = place[:, sl(i, KC * D)].rearrange("p (k m) -> p k m", k=KC)
        w.loads += [(part(view), array) for part, array in loads]
        return view

    beside = lambda a: [(lambda t, k=k: t[:, k, :].rearrange("p (e f) -> p e f", e=NE), a[:, sl(k, 128), :].rearrange("e p f -> p e f"))
                        for k in range(KC)]
    w.WR = w.tensor("WR", [128, KC, NE], (whole, rows(wr)))
    w.W1 = large("W1", *beside(w1))
    w.WV = large("WV", *beside(wv)) if wv is not None else None
    w.W2 = large("W2", (whole, rows(w2.rearrange("e f d -> (e f) d"))))
    if b1 is not None:
        w.B1 = w.tensor("B1", [128, KC], (whole, b1.rearrange("e f -> (e f)").rearrange("(k p) -> p k", p=128)))
        w.B2 = w.tensor("B2", [NE, D], (whole, b2))
    return w


def experts(env, call, w, out=None, ahead=None):
    env.stage += 1
    nc, X, xnT = env.nc, env.X, env.xnT
    f = {n: env.sem("ffn_" + n) for n in ("weights", "gate_ps", "gate", "gateT_ps", "gwT", "a_ps", "act", "h", "gb_ps", "hs", "y_ps", "x",
                                          "step", "exp", "out", "gb_free")}
    U = KC * NN
    with ExitStack() as ctx:
        sb = lambda n, sh, d=F32: env.sb(ctx, n, sh, d)
        WR, W1, W2 = w.WR, w.W1, w.W2
        h = sb("h", [128, KC, N])
        gwT = sb("gwT", [NE, N])
        ab = sb("ab", [128, 2, NB])
        if call == 0:
            WV = w.WV
            L = sb("L", [P, T, NE])
            gt = sb("gt4", [P, T, NE, NE])
            ge = sb("ge4", [P, T, NE, NE])
            mx = sb("mx", [P, T])
            msk = sb("msk", [P, T, NE])
        else:
            B1, B2 = w.B1, w.B2
            LT = sb("LT", [NE, N])
            wk = sb("wk", [NE, N])
            m8 = sb("m8", [NE, 8])
            mx = sb("mx", [NE, 4])
        pa = env.banks(ctx, "pa", 2)
        pg = env.banks(ctx, "pg", 3)
        py = env.banks(ctx, "py", 2)
        if call == 0:
            ln = Layernorm(env, ctx, 2, env.banks(ctx, "fln", 1))
        with nc.Block() as block:
            @block.sync
            def _(sp):
                if ahead:
                    ahead.start(sp)
                if out is not None:
                    for t in range(T):
                        sp.wait_ge(f["x"], T * call + t + 1)
                        sp.dma_start(out[sl(t), :], X[:, t, :]).then_inc(f["out"], 16)
                    sp.wait_ge(f["out"], 16 * T)
            W_READY = 16 * 10 if call == 0 else 16 * (10 + 8)

            @block.vector
            def _(dve):
                n0 = 0 if call == 0 else 9
                count = [n0]

                def step(ins):
                    ins.then_inc(f["step"], 1)
                    count[0] += 1
                    dve.wait_ge(f["step"], count[0])

                dve.wait_ge(f["gate_ps"], call + 1)
                if call == 0:
                    step(dve.tensor_copy(L[:, :, :], pg[2][0:P, 0:T * NE].rearrange("p (t e) -> p t e", e=NE)))
                    other = L[:, :, :].unsqueeze(2).to_broadcast([P, T, NE, NE])
                    own = L[:, :, :].unsqueeze(3).to_broadcast([P, T, NE, NE])
                    dve.tensor_tensor(gt[:, :, :, :], other, own, ALU.is_gt)
                    step(dve.tensor_tensor(ge[:, :, :, :], other, own, ALU.is_equal))
                    step(dve.tensor_tensor(ge[:, :, :, :], ge[:, :, :, :],
                                           env.tri[0:P, :, :].unsqueeze(1).to_broadcast([P, T, NE, NE]), ALU.mult))
                    step(dve.tensor_tensor(gt[:, :, :, :], gt[:, :, :, :], ge[:, :, :, :], ALU.add))
                    step(dve.tensor_reduce(msk[:, :, :], gt[:, :, :, :], AX.X, ALU.add))
                    dve.tensor_scalar(msk[:, :, :], msk[:, :, :], 2.0, None, ALU.is_lt)
                    step(dve.tensor_reduce(mx[:, :], L[:, :, :], AX.X, ALU.max))
                    dve.tensor_tensor(L[:, :, :], L[:, :, :], mx[:, :].unsqueeze(2).to_broadcast([P, T, NE]), ALU.subtract)\
                       .then_inc(f["gate"], 1)
                    dve.wait_ge(f["exp"], 1)
                    step(dve.tensor_tensor(L[:, :, :], L[:, :, :], msk[:, :, :], ALU.mult))
                    step(dve.tensor_reduce(mx[:, :], L[:, :, :], AX.X, ALU.add))
                    step(dve.reciprocal(mx[:, :], mx[:, :]))
                    dve.tensor_tensor(L[:, :, :], L[:, :, :], mx[:, :].unsqueeze(2).to_broadcast([P, T, NE]), ALU.mult)\
                       .then_inc(f["gate"], 1)
                else:
                    for m in range(3):
                        w = min(2 * NB, N - m * 2 * NB)
                        last = dve.tensor_copy(LT[:, m * 2 * NB:m * 2 * NB + w], pg[m][0:NE, 0:w])
                        step(last)
                    step(dve.tensor_reduce(mx[:, 0:1], LT[:, :], AX.X, ALU.max))
                    dve.tensor_scalar(mx[:, 1:2], mx[:, 0:1], -1.0, None, ALU.mult).then_inc(f["gate"], 1)
                    dve.wait_ge(f["exp"], 2)
                    step(dve.reciprocal(mx[:, 3:4], mx[:, 2:3]))
                    step(dve.tensor_scalar(LT[:, :], LT[:, :], mx[:, 3:4], None, ALU.mult))
                    for r in range(CAP // 8):
                        cur = LT if r == 0 else wk
                        step(dve.max(m8[:, :], cur[:, :]))
                        step(dve.match_replace(wk[:, :], m8[:, :], cur[:, :], -1.0))
                    step(dve.tensor_tensor(wk[:, :], wk[:, :], LT[:, :], ALU.not_equal))
                    dve.tensor_tensor(gwT[:, :], LT[:, :], wk[:, :], ALU.mult).then_inc(f["gwT"], 1)
                if call == 0:
                    for n in range(U):
                        if n % 3 == 2 and n // 3 < len(ahead.to_centre):
                            centre_table_weight(env, dve, ahead, n // 3)
                        j, m = n % KC, n // KC
                        dve.wait_ge(f["act"], n + 1)
                        dve.tensor_tensor(h[:, j, sl(m, NB)], pa[n % 2][:, NB:2 * NB], ab[:, n % 2, :], ALU.mult).then_inc(f["h"], 1)
                for n in range(U):
                    j, m = n % KC, n // KC
                    dve.wait_ge(f["gb_ps"], U * call + n + 1)
                    if call == 0:
                        dve.wait_ge(f["h"], n + 1)
                    else:
                        dve.wait_ge(f["act"], U + n + 1)
                    dve.tensor_tensor(h[:, j, sl(m, NB)], h[:, j, sl(m, NB)], pg[n % 2][:, 0:NB], ALU.mult).then_inc(f["hs"], 1)
                for t in range(T):
                    dve.wait_ge(f["y_ps"], T * call + t + 1)
                    dve.tensor_tensor(X[:, t, :], X[:, t, :], py[t % 2][0:P, :], ALU.add).then_inc(f["x"], 1)
                    if call == 0:
                        ln.moments(dve, t, (f["x"], t + 1))
                        if t:
                            ln.normalise(dve, t - 1)
                if call == 0:
                    ln.normalise(dve, T - 1)

            @block.scalar
            def _(act):
                act.wait_ge(f["gate"], 1 if call == 0 else 3)
                if call == 0:
                    act.activation(L[:, :, :], L[:, :, :], ACT.Exp).then_inc(f["exp"], 1)
                    for n in range(U):
                        act.wait_ge(f["a_ps"], n + 1)
                        if n >= 2:
                            act.wait_ge(f["h"], n - 1)
                        act.activation(ab[:, n % 2, :], pa[n % 2][:, 0:NB], ACT.Silu).then_inc(f["act"], 1)
                    for m in range(3):
                        w = min(4, T - 4 * m)
                        act.wait_ge(f["gateT_ps"], m + 1)
                        act.activation(gwT[:, m * 4 * P:(m * 4 + w) * P], pg[m][0:NE, 0:w * P], ACT.Copy).then_inc(f["gwT"], 1)
                    ln.act(act)
                else:
                    act.activation(LT[:, :], LT[:, :], ACT.Exp, bias=mx[:, 1:2], accum_out=mx[:, 2:3]).then_inc(f["exp"], 1)
                    act.wait_ge(f["weights"], W_READY)
                    for n in range(U):
                        j, m = n % KC, n // KC
                        act.wait_ge(f["a_ps"], U + n + 1)
                        act.activation(h[:, j, sl(m, NB)], pa[n % 2][:, 0:NB], ACT.Gelu, bias=B1[:, j:j + 1]).then_inc(f["act"], 1)

            @block.tensor
            def _(pe):
                pe.wait_ge(f["weights"], W_READY)
                if call == 0:
                    for t in range(T):
                        for k in range(KC):
                            last = pe.matmul(pg[2][0:P, t * NE:(t + 1) * NE], xnT[:, k, sl(t)], WR[:, k, :],
                                             start=(k == 0), stop=(k == KC - 1))
                    last.then_inc(f["gate_ps"], 1)
                else:
                    for m in range(NN):
                        for k in range(KC):
                            last = pe.matmul(pg[m // 2][0:NE, (m % 2) * NB:(m % 2 + 1) * NB], WR[:, k, :], xnT[:, k, sl(m, NB)],
                                             start=(k == 0), stop=(k == KC - 1))
                    last.then_inc(f["gate_ps"], 1)
                for n in range(U):
                    j, m = n % KC, n // KC
                    if n >= 2:
                        pe.wait_ge(f["act"], U * call + n - 1)
                        if call == 0:
                            pe.wait_ge(f["h"], n - 1)
                    for i, w in enumerate((W1, WV) if call == 0 else (W1,)):
                        for k in range(KC):
                            last = pe.matmul(pa[n % 2][:, sl(i, NB)], w[:, k, sl(j, 128)], xnT[:, k, sl(m, NB)],
                                             start=(k == 0), stop=(k == KC - 1))
                    last.then_inc(f["a_ps"], 1)
                if call == 0:
                    pe.wait_ge(f["gate"], 2)
                    for m in range(3):
                        for i in range(min(4, T - 4 * m)):
                            last = pe.transpose(pg[m][0:NE, sl(i)], L[:, 4 * m + i, :], env.ident[0:P, 0:P])
                        last.then_inc(f["gateT_ps"], 1)
                pe.wait_ge(f["gwT"], 3 if call == 0 else 4)
                for n in range(U):
                    j, m = n % KC, n // KC
                    if n >= 2:
                        pe.wait_ge(f["hs"], U * call + n - 1)
                    pe.matmul(pg[n % 2][:, 0:NB], env.sel[:, j, :], gwT[:, sl(m, NB)], start=True, stop=True).then_inc(f["gb_ps"], 1)
                pe.wait_ge(f["hs"], U * (call + 1))
                for t in range(T):
                    if t >= 2:
                        pe.wait_ge(f["x"], T * call + t - 1)
                    for j in range(KC):
                        last = pe.matmul(py[t % 2][0:P, :], h[:, j, sl(t)], W2[:, j, :], start=(j == 0),
                                         stop=(j == KC - 1 and call == 0))
                    if call == 1:
                        last = pe.matmul(py[t % 2][0:P, :], gwT[:, sl(t)], B2[:, :], start=False, stop=True)
                    last.then_inc(f["y_ps"], 1)
                    if call == 0 and t >= 2:
                        ln.flip(pe, t - 2)
                if call == 0:
                    ln.flip(pe, T - 2)
                    ln.flip(pe, T - 1)



class NodeMlp:

    def __init__(self, env, ctx, call, tag, hs, w=None, hT=None):
        self.env, self.call = env, call
        sb = lambda n, sh: env.sb(ctx, tag + n, sh)
        self.hs, self.hT = hs, hT or sb("hT", [128, KC, N])
        self.ssq, self.sd, self.rs, self.junk = sb("ssq", [P, T]), sb("sd", [P, T]), sb("rs", [P, T]), sb("sq", [P, 2, D])
        self.G, self.BE, self.W2 = (w.G, w.BE, w.W2) if w else (sb("G", [128, KC]), sb("BE", [128, KC]), sb("W2", [128, KC, D]))
        self.pt, self.py = env.banks(ctx, tag + "pt", 2), env.banks(ctx, tag + "py", 2)
        self.s = {n: env.sem("mlp_" + n) for n in ("hs", "sq", "var", "std", "rstd", "xh", "tr", "relu", "y", "used")}
        self.b = T * call

    def act(self, act):
        s, b = self.s, self.b
        for t in range(T):
            act.wait_ge(s["hs"], b + t + 1)
            if t >= 2:
                act.wait_ge(s["sq"], b + t - 1)
            act.activation(self.junk[:, t % 2, :], self.hs[:, t, :], ACT.Square, accum_out=self.ssq[:, t:t + 1]).then_inc(s["sq"], 1)
        act.wait_ge(s["sq"], b + T)
        act.activation(self.sd[:, :], self.ssq[:, :], ACT.Sqrt, scale=1.0 / D, bias=self.env.eps[0:P, 0:1]).then_inc(s["std"], 1)
        for t in range(T):
            act.wait_ge(s["tr"], b + t + 1)
            for k in range(KC):
                last = act.activation(self.hT[:, k, sl(t)], self.pt[t % 2][:, sl(k)], ACT.Relu,
                                      scale=self.G[:, k:k + 1], bias=self.BE[:, k:k + 1])
            last.then_inc(s["relu"], 1)

    def dve(self, dve):
        s, b = self.s, self.b
        dve.wait_ge(s["std"], self.call + 1)
        dve.reciprocal(self.rs[:, :], self.sd[:, :]).then_inc(s["rstd"], 1)
        dve.wait_ge(s["rstd"], self.call + 1)
        for t in range(T):
            dve.tensor_scalar(self.hs[:, t, :], self.hs[:, t, :], self.rs[:, t:t + 1], None, ALU.mult).then_inc(s["xh"], 1)

    def pe(self, pe, ln=None):
        s, b = self.s, self.b
        for t in range(T):
            pe.wait_ge(s["xh"], b + t + 1)
            if t >= 2:
                pe.wait_ge(s["relu"], b + t - 1)
            for k in range(KC):
                last = pe.transpose(self.pt[t % 2][:, sl(k)], self.hs[:, t, sl(k, 128)], self.env.ident[0:P, 0:P])
            last.then_inc(s["tr"], 1)
        for t in range(T):
            pe.wait_ge(s["relu"], b + t + 1)
            if t >= 2:
                pe.wait_ge(s["used"], b + t - 1)
            for k in range(KC):
                last = pe.matmul(self.py[t % 2][0:P, :], self.hT[:, k, sl(t)], self.W2[:, k, :], start=(k == 0), stop=(k == KC - 1))
            last.then_inc(s["y"], 1)
            if ln and t >= 2:
                ln.flip(pe, t - 2)
        if ln:
            ln.flip(pe, T - 2)
            ln.flip(pe, T - 1)


def centre(dve, step, w, nk, m, parts, scale=1.0):
    step(dve.tensor_reduce(m[0:parts, 0:nk], w, AX.X, ALU.add))
    step(dve.tensor_scalar(m[0:parts, 0:nk], m[0:parts, 0:nk], 1.0 / D, None, ALU.mult))
    for k in range(nk):
        last = dve.tensor_scalar(w[:, k, :], w[:, k, :], m[0:parts, k:k + 1], scale, ALU.subtract, ALU.mult)
    step(last)


def table_weights(env, ctx, a):
    w = Weights(env, ctx, "tab_weights", "left")
    w.W1 = {e: w.tensor("tW" + e, [128, 5 if e != "q" else KC, D], (whole, rows(a[f"h{e}_W1"]))) for e in "kvq"}
    w.B1 = {e: w.tensor("tB" + e, [P, 1, D], (lambda t: t[:, 0, :], bcast(a[f"h{e}_b1"], P, D))) for e in "kvq"}
    w.b2 = {e: w.tensor("tB2" + e, [P, D], (whole, bcast(a[f"h{e}_b2"], P, D))) for e in "qk"}
    w.m = w.tensor("tm", [128, 8])
    up = {"k": UP2, "v": UP2, "q": 1.0}
    w.to_centre = ([(w.W1[e], 5 if e != "q" else KC, 128, up[e]) for e in "kvq"] + [(w.B1[e], 1, P, up[e]) for e in "kvq"])
    return w


def centre_table_weight(env, dve, w, i):
    done = [3 * i]

    def step(ins):
        ins.then_inc(env.sem("tab_step"), 1)
        done[0] += 1
        dve.wait_ge(env.sem("tab_step"), done[0])

    dve.wait_ge(w.ready, 16 * len(w.loads))
    a, blocks, parts, scale = w.to_centre[i]
    centre(dve, step, a[:, :, :], blocks, w.m, parts, scale)


def node_tables(env, weights, w, tab):
    env.stage += 1
    nc, X, XN, xnT = env.nc, env.X, env.XN, env.xnT
    f = {n: env.sem("tab_" + n) for n in ("weights", "weights2", "step", "xres", "ps", "row", "qrow", "qprod", "qb", "q")}
    slot = [env.sem(f"tab_stored{i}") for i in range(4)]
    with ExitStack() as ctx:
        sb = lambda n, sh, d=F32: env.sb(ctx, n, sh, d)
        (WK, WV, WQ), (BK, BV, BQ), (B2Q, B2K) = ([d[e] for e in d] for d in (weights.W1, weights.B1, weights.b2))
        row = sb("trow", [P, 4, QW])
        prod = sb("tprod", [P, D])
        pp = env.banks(ctx, "pp", 4)
        E2 = {e: sb("tE2" + e, [128, KC, D]) for e in "kv"}
        mlp = NodeMlp(env, ctx, 0, "q", env.XN)
        with nc.Block() as block:
            @block.sync
            def _(sp):
                loads = [(mlp.W2[:, :, :], rows(w["hq_W2"])), (E2["k"][:, :, :], rows(w["hk_W2"])), (E2["v"][:, :, :], rows(w["hv_W2"]))]
                for to, a in loads:
                    sp.dma_start(to, a).then_inc(f["weights2"], 16)
                with nc.allow_non_contiguous_dma("512 values as columns"):
                    for to, a in ((mlp.G, "hq_g"), (mlp.BE, "hq_be"), (env.G["k"], "hk_g"), (env.BE["k"], "hk_be"),
                                  (env.G["v"], "hv_g"), (env.BE["v"], "hv_be")):
                        sp.dma_start(to[:, :], w[a].rearrange("(k p) -> p k", p=128)).then_inc(f["weights2"], 16)
                for n in range(3 * T):
                    t = n % T
                    if n < 2 * T:
                        sp.wait_ge(f["row"], n + 1)
                        sp.dma_start(tab["k" if n < T else "v"][sl(t), :], row[:, n % 4, 0:D]).then_inc(slot[n % 4], 16)
                    else:
                        sp.wait_ge(f["q"], t + 1)
                        sp.dma_start(tab["q"][sl(t), :], row[:, n % 4, :]).then_inc(slot[n % 4], 16)
                for i in range(4):
                    sp.wait_ge(slot[i], 16 * len(range(i, 3 * T, 4)))

            @block.vector
            def _(dve):
                n_step = [3 * len(weights.to_centre)]

                def step(ins):
                    ins.then_inc(f["step"], 1)
                    n_step[0] += 1
                    dve.wait_ge(f["step"], n_step[0])

                def edge_weights():
                    dve.wait_ge(f["weights2"], 16 * 9)
                    for e, w1 in (("k", WK), ("v", WV)):
                        dve.tensor_scalar(env.W1E[e][:, 0, :], w1[:, KC, :], 1.0 / UP, None, ALU.mult)
                        step(dve.tensor_scalar(env.W2E[e][:, 0, :, :], E2[e][:, :, :], UP, None, ALU.mult))
                        dve.scalar_tensor_tensor(env.W1E[e][:, 1, :], w1[:, KC, :], 1.0 / UP, env.W1E[e][:, 0, :],
                                                 ALU.mult, ALU.subtract)
                        w2, hi, lo = (a.rearrange("p k m -> p (k m)") for a in (E2[e][:, :, :], env.W2E[e][:, 0, :, :],
                                                                                env.W2E[e][:, 1, :, :]))
                        dve.scalar_tensor_tensor(lo, w2, UP, hi, ALU.mult, ALU.subtract)
                        for a in (env.G[e], env.BE[e]):
                            dve.tensor_scalar(a[:, :], a[:, :], UP, None, ALU.mult)

                for t in range(T):
                    dve.tensor_tensor(X[:, t, :], X[:, t, :], XN[:, t, :], ALU.add).then_inc(f["xres"], 1)
                dve.wait_ge(f["xres"], T)
                for n in range(3 * T):
                    dve.wait_ge(f["ps"], n + 1)
                    if n < 2 * T:
                        if n >= 4:
                            dve.wait_ge(slot[n % 4], 16 * (n // 4))
                        dve.tensor_tensor(row[:, n % 4, 0:D], pp[n % 4][0:P, :], (BK if n < T else BV)[:, 0, :], ALU.add)\
                           .then_inc(f["row"], 1)
                    else:
                        dve.tensor_tensor(mlp.hs[:, n - 2 * T, :], pp[n % 4][0:P, :], BQ[:, 0, :], ALU.add).then_inc(mlp.s["hs"], 1)
                mlp.dve(dve)
                for t in range(T):
                    n = 2 * T + t
                    r = row[:, n % 4, :]
                    dve.wait_ge(mlp.s["y"], t + 1)
                    dve.wait_ge(slot[n % 4], 16 * (n // 4))
                    dve.tensor_tensor(r[:, 0:D], mlp.py[t % 2][0:P, :], B2Q[:, :], ALU.add).then_inc(mlp.s["used"], 1)
                    dve.wait_ge(mlp.s["used"], t + 1)
                    dve.tensor_tensor(prod[:, :], r[:, 0:D], B2K[:, :], ALU.mult).then_inc(f["qprod"], 1)
                    dve.wait_ge(f["qprod"], t + 1)
                    dve.tensor_reduce(r[:, D:QW], prod[:, :].rearrange("p (h d) -> p h d", h=NH), AX.X, ALU.add).then_inc(f["qb"], 1)
                    dve.wait_ge(f["qb"], t + 1)
                    dve.tensor_scalar(r[:, 0:D], r[:, 0:D], float(HD) ** -0.5 / UP2, None, ALU.mult)
                    dve.tensor_scalar(r[:, D:QW], r[:, D:QW], float(HD) ** -0.5, None, ALU.mult).then_inc(f["q"], 1)
                    if t == 0:
                        edge_weights()

            @block.scalar
            def _(act):
                act.wait_ge(f["weights2"], 16 * 9)
                mlp.act(act)

            @block.tensor
            def _(pe):
                pe.wait_ge(f["step"], 6 * 3)
                for n in range(3 * T):
                    t, wt = n % T, (WK, WV, WQ)[n // T]
                    if n >= 4:
                        if n - 4 < 2 * T:
                            pe.wait_ge(f["row"], n - 3)
                        else:
                            pe.wait_ge(mlp.s["hs"], n - 3 - 2 * T)
                    for k in range(KC):
                        last = pe.matmul(pp[n % 4][0:P, :], xnT[:, k, sl(t)], wt[:, k, :], start=(k == 0), stop=(k == KC - 1))
                    last.then_inc(f["ps"], 1)
                pe.wait_ge(f["weights2"], 16 * 9)
                mlp.pe(pe)


LAG = 11
LATE = 5
UN = 4
J0, J1 = 3, 42


def at(j, u, d):
    q, r = divmod(u + d, UN)
    return j + q, r


def chunks(eng, step, last):
    for c in range(UN * J0):
        step(*divmod(c, UN))
    with eng.Fori(J0, J1) as j:
        for u in range(UN):
            step(j, u)
    for c in range(UN * J1, last + 1):
        step(*divmod(c, UN))


def edge_pass(env, mode, edge_attr, tab, dst, agg, ahead=None):
    env.stage += 1
    nc = env.nc
    V = mode == "v"
    ci = 1 if V else 0
    b = CH * ci
    names = ("efT_ps", "efT_hi", "efT_lo", "h_ps", "hs", "sq", "std", "rstd", "xh", "tr", "relu", "r_hi", "r_lo", "y", "prod",
             "red", "logit", "wv", "wv_hi", "wv_lo", "sz", "tot_ps", "tot", "eps")
    f = {n: env.sem("edge_" + n) for n in names}
    ring = lambda n: [env.sem(f"edge_{n}{i}") for i in range(UN)]
    ef_in, g_in, q_in, d_in, sc_out = ring("attr_loaded"), ring("hidden_gathered"), ring("q_gathered"), ring("dst_loaded"), ring("scattered")
    uses = [len(range(u, CH, UN)) for u in range(UN)]
    W1, W2, G, BE = env.W1E[mode], env.W2E[mode], env.G[mode], env.BE[mode]

    def loaded(j, u, both=True):
        return 16 * (j + 1 + (uses[u] * ci if both else 0))

    with ExitStack() as ctx:
        sb = lambda n, sh, d=F32: env.sb(ctx, n, sh, d)
        ef = sb("ef", [P, UN, EF])
        efT = sb("efT", [128, 2, 2, P], F16)
        hg = sb("hg", [P, UN, D])
        hs = sb("ehs", [P, 2, D])
        sq = sb("esq", [P, D])
        ssq, sd, rs = sb("essq", [P, UN]), sb("esd", [P, UN]), sb("ers", [P, UN])
        eps = sb("eeps", [P, 1])
        xh = sb("exh", [P, 2, D])
        r32 = sb("er32", [128, UN, KC * P])
        rT = sb("erT", [128, UN, 2, KC * P], F16)
        if V:
            wv = sb("ewv", [P, D])
            wp = sb("ewp", [P, 2, 2, D], F16)
            dr = sb("edr", [P, UN, P], I32)
            S = sb("eS", [P, 2, P], F16)
            tot = sb("etot", [P, UN, QW])
        else:
            qg = sb("eqg", [P, UN, QW])
            prod, red = sb("eprod", [P, D]), sb("ered", [P, NH])
        pe_ef, pe_h = env.banks(ctx, "pef", 1)[0], env.banks(ctx, "peh", 1)[0]
        pt, py = env.banks(ctx, "pet", 2), env.banks(ctx, "pey", 2)
        if V:
            po, pd = env.banks(ctx, "peo", 1)[0], env.banks(ctx, "ped", 1)[0]
        with nc.Block() as block:
            @block.sync
            def _(sp):
                for c in range(CH + LATE):
                    if ahead and c % 16 == 8:
                        ahead.start(sp, c // 16, c // 16 + 1)
                    if c < CH:
                        if c >= UN:
                            sp.wait_ge(f["efT_ps"], b + c - UN + 1)
                        sp.dma_start(ef[:, c % UN, :], edge_attr[sl(c), :]).then_inc(ef_in[c % UN], 16)
                    x = c - LATE
                    if V and x >= 0:
                        if x >= UN:
                            sp.wait_ge(f["sz"], x - UN + 1)
                        sp.dma_start(dr[:, x % UN, :], bcast(dst[sl(x)], P, P)).then_inc(d_in[x % UN], 16)

            @block.gpsimd
            def _(g):
                for c in range(CH + LAG):
                    if c < CH:
                        u = c % UN
                        if c >= UN:
                            g.wait_ge(f["hs"], b + c - UN + 1)
                        g.indirect_dma_start(out=hg[:, u, :], out_offset=None, in_=tab[mode][:, :],
                                             in_offset=bass.IndirectOffsetOnAxis(ap=env.srci[:, c:c + 1], axis=0))\
                         .then_inc(g_in[u], 16)
                    x = c - LATE
                    if not V and 0 <= x < CH:
                        if x >= UN:
                            g.wait_ge(f["logit"], x - UN + 1)
                        g.indirect_dma_start(out=qg[:, x % UN, :], out_offset=None, in_=tab["q"][:, :],
                                             in_offset=bass.IndirectOffsetOnAxis(ap=env.dsti[:, x:x + 1], axis=0))\
                         .then_inc(q_in[x % UN], 16)
                    if V and c >= LAG:
                        x = c - LAG
                        g.wait_ge(f["tot"], x + 1)
                        g.indirect_dma_start(out=agg[:, :], out_offset=bass.IndirectOffsetOnAxis(ap=env.scati[:, x:x + 1], axis=0),
                                             in_=tot[:, x % UN, :], in_offset=None, bounds_check=N + CH - 1, oob_is_err=False)\
                         .then_inc(sc_out[x % UN], 16)
                if V:
                    for u in range(UN):
                        g.wait_ge(sc_out[u], 16 * uses[u])

            @block.vector
            def _(dve):
                def add(j, u):
                    c = UN * j + u
                    dve.wait_ge(f["h_ps"], b + c + 1)
                    dve.wait_ge(g_in[u], loaded(j, u))
                    if not (isinstance(c, int) and c < 2):
                        dve.wait_ge(f["sq"], b + c - 1)
                        dve.wait_ge(f["xh"], b + c - 1)
                    dve.tensor_tensor(hs[:, u % 2, :], pe_h[0:P, :], hg[:, u, :], ALU.add).then_inc(f["hs"], 1)

                def ef_low(j, u):
                    c = UN * j + u
                    dve.wait_ge(f["efT_hi"], b + c + 1)
                    dve.scalar_tensor_tensor(efT[:, u % 2, 1, :], pe_ef[:, 0:P], UP, efT[:, u % 2, 0, :], ALU.mult, ALU.subtract)\
                       .then_inc(f["efT_lo"], 1)

                def r_low(j, u):
                    c = UN * j + u
                    dve.wait_ge(f["r_hi"], b + c + 1)
                    dve.tensor_tensor(rT[:, u, 1, :], r32[:, u, :], rT[:, u, 0, :], ALU.subtract).then_inc(f["r_lo"], 1)

                def invert(j, u):
                    c = UN * j + u
                    dve.wait_ge(f["std"], b + c + 1)
                    dve.reciprocal(rs[:, u:u + 1], sd[:, u:u + 1]).then_inc(f["rstd"], 1)

                def normalise(j, u):
                    c = UN * j + u
                    if not (isinstance(c, int) and c < 2):
                        dve.wait_ge(f["tr"], b + c - 1)
                    dve.wait_ge(f["rstd"], b + c + 1)
                    dve.tensor_scalar(xh[:, u % 2, :], hs[:, u % 2, :], rs[:, u:u + 1], None, ALU.mult).then_inc(f["xh"], 1)

                def times_q(j, u):
                    c = UN * j + u
                    dve.wait_ge(f["y"], c + 1)
                    dve.wait_ge(q_in[u], loaded(j, u, False))
                    if not (isinstance(c, int) and c < 1):
                        dve.wait_ge(f["red"], c)
                    dve.tensor_tensor(prod[:, :], py[u % 2][0:P, :], qg[:, u, 0:D], ALU.mult).then_inc(f["prod"], 1)

                def sum_heads(j, u):
                    c = UN * j + u
                    dve.wait_ge(f["prod"], c + 1)
                    if not (isinstance(c, int) and c < 1):
                        dve.wait_ge(f["logit"], c)
                    dve.tensor_reduce(red[:, :], prod[:, :].rearrange("p (h d) -> p h d", h=NH), AX.X, ALU.add).then_inc(f["red"], 1)

                def logits(j, u):
                    c = UN * j + u
                    dve.wait_ge(f["red"], c + 1)
                    dve.tensor_tensor(env.L[:, bass.ds(c * NH, NH)], red[:, :], qg[:, u, D:QW], ALU.add).then_inc(f["logit"], 1)

                def weigh(j, u):
                    c = UN * j + u
                    dve.wait_ge(f["y"], b + c + 1)
                    if not (isinstance(c, int) and c < 1):
                        dve.wait_ge(f["wv_lo"], c)
                    dve.scalar_tensor_tensor(wv[:, :].rearrange("p (h d) -> p h d", h=NH),
                                             py[u % 2][0:P, :].rearrange("p (h d) -> p h d", h=NH), 1.0 / UP,
                                             env.L[:, bass.ds(c * NH, NH)].unsqueeze(2).to_broadcast([P, NH, HD]),
                                             ALU.mult, ALU.mult).then_inc(f["wv"], 1)

                def compare(j, u):
                    c = UN * j + u
                    dve.wait_ge(d_in[u], loaded(j, u, False))
                    if not (isinstance(c, int) and c < 2):
                        dve.wait_ge(f["tot_ps"], c - 1)
                    dve.tensor_scalar(S[:, u % 2, :], dr[:, u, :], env.dstf[:, bass.ds(c, 1)], None, ALU.is_equal).then_inc(f["sz"], 1)

                def wv_high(j, u):
                    c = UN * j + u
                    dve.wait_ge(f["wv"], c + 1)
                    dve.tensor_copy(wp[:, u % 2, 0, :], wv[:, :]).then_inc(f["wv_hi"], 1)

                def wv_low(j, u):
                    c = UN * j + u
                    dve.wait_ge(f["wv_hi"], c + 1)
                    dve.tensor_tensor(wp[:, u % 2, 1, :], wv[:, :], wp[:, u % 2, 0, :], ALU.subtract).then_inc(f["wv_lo"], 1)

                dve.memset(eps[:, :], EPS * UP2 * UP2).then_inc(f["eps"], 1)
                ef_low(0, 0)

                def step(j, u):
                    c = UN * j + u
                    static = isinstance(c, int)
                    if not V and (not static or 0 <= c - 6 < CH):
                        logits(*at(j, u, -6))
                    if not static or c < CH:
                        add(j, u)
                    if not static or c + 1 < CH:
                        ef_low(*at(j, u, 1))
                    if not static or 0 <= c - 1 < CH:
                        invert(*at(j, u, -1))
                    if not static or 0 <= c - 5 < CH:
                        (weigh if V else times_q)(*at(j, u, -5))
                    if V and (not static or 0 <= c - 5 < CH):
                        compare(*at(j, u, -5))
                    if not static or 0 <= c - 1 < CH:
                        normalise(*at(j, u, -1))
                    if V and (not static or 0 <= c - 5 < CH):
                        wv_high(*at(j, u, -5))
                    if not static or 0 <= c - 3 < CH:
                        r_low(*at(j, u, -3))
                    if not static or 0 <= c - 5 < CH:
                        (wv_low if V else sum_heads)(*at(j, u, -5))
                chunks(dve, step, CH + 5)

            @block.scalar
            def _(act):
                def copy_ef(j, u):
                    c = UN * j + u
                    act.wait_ge(f["efT_ps"], b + c + 1)
                    if not (isinstance(c, int) and c < 2):
                        act.wait_ge(f["h_ps"], b + c - 1)
                    act.activation(efT[:, u % 2, 0, :], pe_ef[:, 0:P], ACT.Copy, scale=UP).then_inc(f["efT_hi"], 1)

                def deviation(j, u):
                    c = UN * j + u
                    act.wait_ge(f["hs"], b + c + 1)
                    act.activation(sq[:, :], hs[:, u % 2, :], ACT.Square, accum_out=ssq[:, u:u + 1]).then_inc(f["sq"], 1)
                    act.wait_ge(f["sq"], b + c + 1)
                    act.activation(sd[:, u:u + 1], ssq[:, u:u + 1], ACT.Sqrt, scale=1.0 / D, bias=eps[:, 0:1])\
                       .then_inc(f["std"], 1)

                def relu(j, u):
                    c = UN * j + u
                    act.wait_ge(f["tr"], b + c + 1)
                    if not (isinstance(c, int) and c < UN):
                        act.wait_ge(f["y"], b + c - UN + 1)
                    for k in range(KC):
                        last = act.activation(r32[:, u, sl(k)], pt[u % 2][:, sl(k)], ACT.Relu, scale=G[:, k:k + 1], bias=BE[:, k:k + 1])
                    last.then_inc(f["relu"], 1)

                def r_high(j, u):
                    c = UN * j + u
                    act.wait_ge(f["relu"], b + c + 1)
                    act.activation(rT[:, u, 0, :], r32[:, u, :], ACT.Copy).then_inc(f["r_hi"], 1)

                def total(j, u):
                    c = UN * j + u
                    act.wait_ge(f["tot_ps"], c + 1)
                    if not (isinstance(j, int) and j == 0):
                        act.wait_ge(sc_out[u], 16 * j)
                    act.activation(tot[:, u, 0:D], po[0:P, :], ACT.Copy)
                    act.activation(tot[:, u, D:QW], pd[0:P, 0:NH], ACT.Copy).then_inc(f["tot"], 1)

                act.wait_ge(f["eps"], ci + 1)
                copy_ef(0, 0)

                def step(j, u):
                    c = UN * j + u
                    static = isinstance(c, int)
                    if V and (not static or 0 <= c - 7 < CH):
                        total(*at(j, u, -7))
                    if not static or c + 1 < CH:
                        copy_ef(*at(j, u, 1))
                    if not static or c < CH:
                        deviation(j, u)
                    if not static or 0 <= c - 2 < CH:
                        relu(*at(j, u, -2))
                        r_high(*at(j, u, -2))
                chunks(act, step, CH + 6)

            @block.tensor
            def _(pe):
                def flip_ef(j, u):
                    c = UN * j + u
                    pe.wait_ge(ef_in[u], loaded(j, u))
                    if not (isinstance(c, int) and c < 1):
                        pe.wait_ge(f["efT_lo"], b + c)
                    pe.transpose(pe_ef[:, 0:P], ef[:, u, :], env.ident[0:P, 0:P]).then_inc(f["efT_ps"], 1)

                def hidden(j, u):
                    c = UN * j + u
                    pe.wait_ge(f["efT_lo"], b + c + 1)
                    if not (isinstance(c, int) and c < 1):
                        pe.wait_ge(f["hs"], b + c)
                    pe.matmul(pe_h[0:P, :], efT[:, u % 2, 0, :], W1[:, 0, :], start=True, stop=False)
                    pe.matmul(pe_h[0:P, :], efT[:, u % 2, 0, :], W1[:, 1, :], start=False, stop=False)
                    pe.matmul(pe_h[0:P, :], efT[:, u % 2, 1, :], W1[:, 0, :], start=False, stop=True).then_inc(f["h_ps"], 1)

                def flip_xh(j, u):
                    c = UN * j + u
                    pe.wait_ge(f["xh"], b + c + 1)
                    if not (isinstance(c, int) and c < 2):
                        pe.wait_ge(f["relu"], b + c - 1)
                    for k in range(KC):
                        last = pe.transpose(pt[u % 2][:, sl(k)], xh[:, u % 2, sl(k, 128)], env.ident[0:P, 0:P])
                    last.then_inc(f["tr"], 1)

                def product(j, u):
                    c = UN * j + u
                    pe.wait_ge(f["r_lo"], b + c + 1)
                    if not (isinstance(c, int) and c < 2):
                        pe.wait_ge(f["wv" if V else "prod"], c - 1)
                    for k in range(KC):
                        for r, w2 in ((0, 0), (0, 1), (1, 0)):
                            last = pe.matmul(py[u % 2][0:P, :], rT[:, u, r, sl(k)], W2[:, w2, k, :],
                                             start=(k == 0 and r == w2), stop=(k == KC - 1 and r == 1))
                    last.then_inc(f["y"], 1)

                def total(j, u):
                    c = UN * j + u
                    pe.wait_ge(f["wv_lo"], c + 1)
                    pe.wait_ge(f["sz"], c + 1)
                    if not (isinstance(c, int) and c < 1):
                        pe.wait_ge(f["tot"], c)
                    for part in range(2):
                        pe.matmul(po[0:P, :], S[:, u % 2, :], wp[:, u % 2, part, :], start=(part == 0), stop=(part == 1))
                    for part in range(2):
                        last = pe.matmul(pd[0:P, 0:NH], S[:, u % 2, :], env.LP[:, part, bass.ds(c * NH, NH)],
                                         start=(part == 0), stop=(part == 1))
                    last.then_inc(f["tot_ps"], 1)

                flip_ef(0, 0)

                def step(j, u):
                    c = UN * j + u
                    static = isinstance(c, int)
                    if not static or c < CH:
                        hidden(j, u)
                    if not static or c + 1 < CH:
                        flip_ef(*at(j, u, 1))
                    if not static or 0 <= c - 2 < CH:
                        flip_xh(*at(j, u, -2))
                    if not static or 0 <= c - 4 < CH:
                        product(*at(j, u, -4))
                    if V and (not static or 0 <= c - 6 < CH):
                        total(*at(j, u, -6))
                chunks(pe, step, CH + 5)


def segment_exp(env, dst):
    nc, L = env.nc, env.L
    R = SB_ * NH
    f = {n: env.sem("seg_" + n) for n in ("dst", "pad", "flag", "lt_ps", "lt", "step", "row_ps", "row", "col_ps", "col", "m", "m_ps", "sub", "exp", "hi")}
    Lb = L[:, :].rearrange("p (b i h) -> p i b h", b=SB_, h=NH)
    with ExitStack() as ctx:
        sb = lambda n, sh, d=F32: env.sb(ctx, n, sh, d)
        DD = sb("sDD", [R, BE + 2], I32)
        fl = sb("sfl", [R, BE + 1])
        LT = sb("sLT", [R, BE])
        F = sb("sF", [R, BE])
        B = sb("sB", [R, BE])
        Lc = sb("sLc", [P, 2, SB_, NH])
        fn = sb("sfn", [R, 4])
        row = sb("srow4", [1, 4, SB_, NH])
        ini = sb("sini", [1, 2, SB_, NH])
        col = sb("scol", [R, 2])
        tmp = sb("stmp", [1, 2, NH])
        pl = env.banks(ctx, "spl", 2)
        pr = env.banks(ctx, "spr", 2)
        pm = env.banks(ctx, "spm", 2)
        with nc.Block() as block:
            @block.sync
            def _(sp):
                sp.wait_ge(f["pad"], 2)
                for k in range(SB_):
                    lo, hi = max(0, k * BE - 1), min(E, (k + 1) * BE + 1)
                    at0 = 1 if k == 0 else 0
                    sp.dma_start(DD[k * NH:(k + 1) * NH, at0:at0 + hi - lo], bcast(dst[lo:hi], NH, hi - lo)).then_inc(f["dst"], 16)

            @block.tensor
            def _(pe):
                for i in range(BC):
                    q, r = divmod(i, 4)
                    pe.wait_ge(f["step"], i + 1)
                    if r == 0 and q >= 2:
                        pe.wait_ge(f["lt"], q - 1)
                    last = pe.transpose(pl[q % 2][0:R, sl(r)], Lc[:, i % 2, :, :].rearrange("p b h -> p (b h)"), env.ident[0:P, 0:P])
                    last.then_inc(f["lt_ps"], 1)
                pe.wait_ge(f["flag"], 6)
                for n, c in enumerate((F[:, BE - 1:BE], B[:, 0:1], fn[:, 0:1], fn[:, 1:2])):
                    last = pe.transpose(pr[0][0:1, n * R:(n + 1) * R], c, env.ident[0:R, 0:R])
                last.then_inc(f["row_ps"], 1)
                pe.wait_ge(f["row"], 1)
                for n in range(2):
                    last = pe.transpose(pr[1][0:R, n:n + 1], ini[0:1, n, :, :].rearrange("o b h -> o (b h)"), env.ident[0:1, 0:1])
                last.then_inc(f["col_ps"], 1)
                pe.wait_ge(f["m"], 1)
                for i in range(BC):
                    q, r = divmod(i, 6)
                    if r == 0 and q >= 2:
                        pe.wait_ge(f["sub"], q - 1)
                    last = pe.transpose(pm[q % 2][0:P, r * R:(r + 1) * R], F[:, sl(i)], env.ident[0:R, 0:R])
                    if r == 5 or i == BC - 1:
                        last.then_inc(f["m_ps"], 1)

            @block.scalar
            def _(act):
                for i in range(BC):
                    if i >= 2:
                        act.wait_ge(f["lt_ps"], i - 1)
                    act.activation(Lc[:, i % 2, :, :], Lb[:, i, :, :], ACT.Copy).then_inc(f["step"], 1)
                    q, r = divmod(i, 4)
                    if r == 3 or i == BC - 1:
                        act.wait_ge(f["lt_ps"], i + 1)
                        act.activation(LT[:, q * 4 * P:(q * 4 + r + 1) * P], pl[q % 2][0:R, 0:(r + 1) * P], ACT.Copy).then_inc(f["lt"], 1)
                act.wait_ge(f["sub"], (BC + 5) // 6)
                act.activation(L[:, :], L[:, :], ACT.Exp).then_inc(f["exp"], 1)
                act.wait_ge(f["exp"], 1)
                act.activation(env.LP[:, 0, :], L[:, :], ACT.Copy, scale=UP).then_inc(f["hi"], 1)

            @block.vector
            def _(dve):
                n = [0]
                chain = env.sem("seg_chain")

                def step(ins):
                    ins.then_inc(chain, 1)
                    n[0] += 1
                    dve.wait_ge(chain, n[0])

                dve.memset(DD[:, 0:1], -1).then_inc(f["pad"], 1)
                dve.memset(DD[:, BE + 1:BE + 2], -1).then_inc(f["pad"], 1)
                dve.wait_ge(f["dst"], 16 * SB_)
                step(dve.tensor_tensor(fl[:, :], DD[:, 1:BE + 2], DD[:, 0:BE + 1], ALU.not_equal))
                step(dve.tensor_scalar(fl[:, 0:BE], fl[:, 0:BE], 1.0, 0.0, ALU.mult, ALU.add, accum_out=fn[:, 0:1]))
                step(dve.tensor_tensor(fn[:, 1:2], fn[:, 0:1], fl[:, 0:1], ALU.subtract))
                step(dve.tensor_tensor(fn[:, 1:2], fn[:, 1:2], fl[:, BE:BE + 1], ALU.add))
                dve.tensor_scalar(fn[:, 0:2], fn[:, 0:2], -BIG, None, ALU.mult).then_inc(f["flag"], 2)
                step(dve.tensor_scalar(fl[:, :], fl[:, :], -BIG, None, ALU.mult))
                dve.wait_ge(f["lt"], (BC + 3) // 4)
                dve.tensor_tensor_scan(F[:, :], fl[:, 0:BE], LT[:, :], -BIG, ALU.add, ALU.max).then_inc(f["flag"], 1)
                dve.tensor_tensor_scan(B[:, ::-1], fl[:, BE:0:-1], LT[:, ::-1], -BIG, ALU.add, ALU.max).then_inc(f["flag"], 1)
                dve.memset(ini[:, :, :, :], -BIG).then_inc(f["flag"], 1)
                dve.memset(tmp[:, :, :], 0.0).then_inc(f["flag"], 1)
                dve.wait_ge(f["row_ps"], 1)
                step(dve.tensor_copy(row[:, :, :, :].rearrange("o n b h -> o (n b h)"), pr[0][0:1, 0:4 * R]))
                for k in range(1, SB_):
                    m = SB_ - 1 - k
                    dve.tensor_tensor(tmp[:, 0, :], row[:, 0, k - 1, :], row[:, 2, k, :], ALU.add)
                    step(dve.tensor_tensor(tmp[:, 1, :], row[:, 1, m + 1, :], row[:, 3, m, :], ALU.add))
                    dve.tensor_tensor(row[:, 0, k, :], row[:, 0, k, :], tmp[:, 0, :], ALU.max)
                    step(dve.tensor_tensor(row[:, 1, m, :], row[:, 1, m, :], tmp[:, 1, :], ALU.max))
                step(dve.tensor_copy(ini[:, 0, 1:SB_, :], row[:, 0, 0:SB_ - 1, :]))
                dve.tensor_copy(ini[:, 1, 0:SB_ - 1, :], row[:, 1, 1:SB_, :]).then_inc(f["row"], 1)
                dve.wait_ge(f["col_ps"], 1)
                step(dve.tensor_copy(col[:, :], pr[1][0:R, 0:2]))
                dve.tensor_tensor_scan(F[:, :], fl[:, 0:BE], LT[:, :], col[:, 0:1], ALU.add, ALU.max)
                step(dve.tensor_tensor_scan(B[:, ::-1], fl[:, BE:0:-1], LT[:, ::-1], col[:, 1:2], ALU.add, ALU.max))
                dve.tensor_tensor(F[:, :], F[:, :], B[:, :], ALU.max).then_inc(f["m"], 1)
                for q in range((BC + 5) // 6):
                    k = min(6, BC - 6 * q)
                    dve.wait_ge(f["m_ps"], q + 1)
                    dve.tensor_tensor(Lb[:, 6 * q:6 * q + k, :, :], Lb[:, 6 * q:6 * q + k, :, :],
                                      pm[q % 2][0:P, 0:k * R].rearrange("p (i b h) -> p i b h", i=k, b=SB_), ALU.subtract)\
                       .then_inc(f["sub"], 1)
                dve.wait_ge(f["hi"], 1)
                dve.scalar_tensor_tensor(env.LP[:, 1, :], L[:, :], UP, env.LP[:, 0, :], ALU.mult, ALU.subtract)


def out_weights(env, ctx, a):
    w = Weights(env, ctx, "out_weights")
    column = lambda n: (whole, a[n].rearrange("(k p) -> p k", p=128))
    w.W1 = w.tensor("oW1", [128, 2 * KC, D], (whole, rows(a["no_W1"])))
    w.B1 = w.tensor("oB1", [P, 1, D], (lambda t: t[:, 0, :], bcast(a["no_b1"], P, D)))
    w.B2 = w.tensor("oB2", [P, D], (whole, bcast(a["no_b2"], P, D)))
    w.BV = w.tensor("oBV", [P, D], (whole, bcast(a["hv_b2"], P, D)))
    w.W2 = w.tensor("oW2", [128, KC, D], (whole, rows(a["no_W2"])))
    w.G, w.BE = w.tensor("oG", [128, KC], column("no_g")), w.tensor("oBE", [128, KC], column("no_be"))
    return w


def node_output(env, w, agg, ahead):
    env.stage += 1
    nc, X, xnT = env.nc, env.X, env.xnT
    f = {n: env.sem("out_" + n) for n in ("weights", "rows", "step", "sums_ps", "agg", "tr", "aggT", "xn_ps", "xn_h", "ps", "x", "iota",
                                          "head_ps", "head")}
    with ExitStack() as ctx:
        sb = lambda n, sh, d=F32: env.sb(ctx, n, sh, d)
        W1, B1, B2, BV = w.W1, w.B1, w.B2, w.BV
        A = sb("oA", [P, T, QW])
        H = sb("oH", [CR, 2, QW])
        ni, nf, OH = sb("oni", [CR, N], I32), sb("onf", [CR, N]), sb("oOH", [CR, T, 2, P])
        den, one = sb("oden", [P, T, NH]), sb("oone", [P, T, NH])
        bv = sb("obv", [P, 2, D])
        m = sb("om", [128, 8])
        aT = sb("oaT", [128, KC, N])
        yb = sb("oyb", [P, 2, D])
        pa, pp = env.banks(ctx, "opa", 2), env.banks(ctx, "opp", 2)
        mlp = NodeMlp(env, ctx, 1, "o", env.XN, w, aT)
        px = mlp.py
        ln = Layernorm(env, ctx, 3, pa)
        with nc.Block() as block:
            @block.sync
            def _(sp):
                for to, a in ((H[:, :, :], agg[N:N + CH, :].rearrange("(p h) d -> p h d", h=2)),
                              (A[:, :, :], agg[0:N, :].rearrange("(t p) d -> p t d", p=P))):
                    sp.dma_start(to, a).then_inc(f["rows"], 16)
                ahead.start(sp)

            @block.vector
            def _(dve):
                n = [0]

                def step(ins):
                    ins.then_inc(f["step"], 1)
                    n[0] += 1
                    dve.wait_ge(f["step"], n[0])

                dve.wait_ge(f["weights"], 16 * len(w.loads))
                centre(dve, step, W1[:, :, :], 2 * KC, m, 128)
                centre(dve, step, B1[:, :, :], 1, m, P)
                dve.wait_ge(f["iota"], 1)
                step(dve.tensor_copy(nf[:, :], ni[:, :]))
                for t in range(T):
                    for h in range(2):
                        last = dve.tensor_scalar(OH[:, t, h, :], nf[:, sl(t)], env.headf[:, h:h + 1], None, ALU.is_equal)
                    last.then_inc(f["head"], 1)
                dve.wait_ge(f["rows"], 32)
                dve.wait_ge(f["sums_ps"], 1)
                step(dve.tensor_tensor(A[:, :, D:QW], A[:, :, D:QW], pa[0][0:P, 0:T * NH].rearrange("p (t h) -> p t h", h=NH), ALU.add))
                step(dve.tensor_scalar(one[:, :, :], A[:, :, D:QW], 0.0, None, ALU.is_equal))
                step(dve.tensor_tensor(den[:, :, :], A[:, :, D:QW], one[:, :, :], ALU.add))
                dve.reciprocal(den[:, :, :], den[:, :, :])
                step(dve.tensor_scalar(one[:, :, :], one[:, :, :], -1.0, 1.0, ALU.mult, ALU.add))
                heads = lambda a: a.rearrange("p (h d) -> p h d", h=NH)
                wide = lambda a: a.unsqueeze(2).to_broadcast([P, NH, HD])
                for t in range(T):
                    a = A[:, t, 0:D]
                    if t >= 2:
                        dve.wait_ge(f["agg"], t - 1)
                    dve.tensor_tensor(heads(bv[:, t % 2, :]), heads(BV[:, :]), wide(one[:, t, :]), ALU.mult)
                    dve.wait_ge(f["head_ps"], t + 1)
                    step(dve.tensor_tensor(a, a, pp[t % 2][0:P, :], ALU.add))
                    dve.wait_ge(f["xn_ps"], t + 1)
                    dve.tensor_tensor(mlp.hs[:, t, :], px[t % 2][0:P, :], B1[:, 0, :], ALU.add).then_inc(f["xn_h"], 1)
                    step(dve.tensor_tensor(heads(a), heads(a), wide(den[:, t, :]), ALU.mult))
                    dve.tensor_tensor(a, a, bv[:, t % 2, :], ALU.add).then_inc(f["agg"], 1)
                for t in range(T):
                    dve.wait_ge(f["ps"], t + 1)
                    dve.wait_ge(f["xn_h"], t + 1)
                    dve.tensor_tensor(mlp.hs[:, t, :], mlp.hs[:, t, :], pp[t % 2][0:P, :], ALU.add).then_inc(mlp.s["hs"], 1)
                mlp.dve(dve)
                for t in range(T):
                    dve.wait_ge(mlp.s["y"], T + t + 1)
                    dve.tensor_tensor(yb[:, t % 2, :], mlp.py[t % 2][0:P, :], B2[:, :], ALU.add).then_inc(mlp.s["used"], 1)
                    dve.wait_ge(mlp.s["used"], T + t + 1)
                    dve.tensor_tensor(X[:, t, :], X[:, t, :], yb[:, t % 2, :], ALU.add).then_inc(f["x"], 1)
                    if t == 0:
                        dve.wait_ge(mlp.s["tr"], 2 * T)
                    ln.moments(dve, t, (f["x"], t + 1))
                    if t:
                        ln.normalise(dve, t - 1)
                ln.normalise(dve, T - 1)

            @block.gpsimd
            def _(g):
                g.iota(ni[:, :], pattern=[[1, N]], base=0, channel_multiplier=0).then_inc(f["iota"], 1)

            @block.scalar
            def _(act):
                for t in range(T):
                    act.wait_ge(f["tr"], t + 1)
                    act.activation(aT[:, :, sl(t)], pa[t % 2][:, 0:KC * P].rearrange("p (k n) -> p k n", k=KC), ACT.Copy)\
                       .then_inc(f["aggT"], 1)
                mlp.act(act)
                ln.act(act)

            @block.tensor
            def _(pe):
                def flip(t):
                    pe.wait_ge(f["agg"], t + 1)
                    if t >= 2:
                        pe.wait_ge(f["aggT"], t - 1)
                    for k in range(KC):
                        last = pe.transpose(pa[t % 2][:, sl(k)], A[:, t, sl(k, 128)], env.ident[0:P, 0:P])
                    last.then_inc(f["tr"], 1)

                pe.wait_ge(f["rows"], 32)
                pe.wait_ge(f["head"], T)
                for t in range(T):
                    for h in range(2):
                        last = pe.matmul(pa[0][0:P, t * NH:(t + 1) * NH], OH[:, t, h, :], H[:, h, D:QW], start=(h == 0), stop=(h == 1))
                last.then_inc(f["sums_ps"], 1)
                for t in range(T):
                    if t >= 2:
                        pe.wait_ge(f["agg"], t - 1)
                        pe.wait_ge(f["xn_h"], t - 1)
                    for h in range(2):
                        last = pe.matmul(pp[t % 2][0:P, :], OH[:, t, h, :], H[:, h, 0:D], start=(h == 0), stop=(h == 1))
                    last.then_inc(f["head_ps"], 1)
                    for k in range(KC):
                        last = pe.matmul(px[t % 2][0:P, :], xnT[:, k, sl(t)], W1[:, KC + k, :], start=(k == 0), stop=(k == KC - 1))
                    last.then_inc(f["xn_ps"], 1)
                    if t >= 2:
                        flip(t - 2)
                flip(T - 2)
                flip(T - 1)
                for t in range(T):
                    pe.wait_ge(f["aggT"], t + 1)
                    if t >= 2:
                        pe.wait_ge(mlp.s["hs"], T + t - 1)
                    for k in range(KC):
                        last = pe.matmul(pp[t % 2][0:P, :], aT[:, k, sl(t)], W1[:, k, :], start=(k == 0), stop=(k == KC - 1))
                    last.then_inc(f["ps"], 1)
                mlp.pe(pe, ln)


def build(nc, a, out):
    with ExitStack() as ctx:
        env = Env(nc, ctx)
        sb = lambda n, s, d=F32: env.sb(ctx, n, s, d)
        env.X, env.XN, env.xnT = sb("X", [P, T, D]), sb("XN", [P, T, D]), sb("xnT", [128, KC, N])
        env.ident, env.bd = sb("ident", [128, 128]), sb("bd", [128, 128])
        env.later, env.tri, env.sel = sb("later", [P, P]), sb("tri", [P, NE, NE]), sb("sel", [NE, KC, 128])
        env.ones, env.eps, env.junk = sb("ones", [128, 2]), sb("eps", [128, 1]), sb("junk", [P, 1])
        env.srcf, env.dstf, env.keyf = (sb(n, [P, CH]) for n in ("srcf", "dstf", "keyf"))
        env.headf = sb("headf", [CR, 2])
        env.cnum, env.clater, env.cdel = (sb(n, [P, CH]) for n in ("cnum", "clater", "cdel"))
        env.srci, env.dsti, env.scati, env.cidx = (sb(n, [P, CH], I32) for n in ("srci", "dsti", "scati", "cidx"))
        dram = lambda n, shape: nc.dram_tensor(n, shape, F32, kind="Internal").ap()
        cnt = [dram(f"counts{i}", (N * N + P, 1)) for i in range(TABLES)]
        tab = {"k": dram("hidden_k", (N, D)), "v": dram("hidden_v", (N, D)), "q": dram("queries", (N, QW))}
        agg = dram("aggregate", (N + CH, QW))
        s_dram = dram("s_row", (N,))
        L1 = {k[7:]: v for k, v in a.items() if k.startswith("L1_gnn_")}
        with ExitStack() as left:
            with ExitStack() as right:
                shared = right.enter_context(nc.sbuf_tensor("shared", [128, 2 * TABLES * N], F32, side="right"))
                rows_of = lambda i: shared[0:P, sl(i, 2 * GR * P)].bitcast(I32).rearrange("p (s n) -> p s n", s=2)
                count_rows = (rows_of(0), rows_of(1))
                z = 4 * GR * P
                env.zero = shared[0:P, z:z + N + 1]
                env.eq = shared[0:P, z + N + 1:z + N + 1 + 4 * P].rearrange("p (s n e) -> p s n e", s=2, n=2)
                ffn_w = expert_weights(env, right, a["L0_ffn_Wg"], a["L0_ffn_W"], a["L0_ffn_V"], None, a["L0_ffn_W2"], None, place=shared)
                with ExitStack() as far:
                    gat_w = gat_weights(env, far, a["L0_gnn_W"], a["L0_gnn_b"], a["L0_gnn_a"])
                    with ExitStack() as early:
                        mix_w = mix_weights(env, early, a["L0_mix_w_qkv"], a["L0_mix_w_out"], a["L0_mix_b_out"])
                        setup(env, a["src"], a["dst"], a["x"], mix_w, count_rows)
                        first_layernorm(env, cnt[0:2])
                        linear_attention(env, 0, mix_w, True, (a["src"], a["dst"], cnt, agg, count_rows), gat_w)
                    graph_attention(env, gat_w, cnt, s_dram, shared, ffn_w)
                env.retire("const", "zero", "tables", "index", "x_loaded", "count", "gat_")
                tab_w = table_weights(env, left, L1)
                experts(env, 0, ffn_w, ahead=tab_w)
            with ExitStack() as right:
                keep = lambda n, shape, d=F32: right.enter_context(nc.sbuf_tensor(n, shape, d, side="right"))
                env.L = keep("logits", [P, CH * NH])
                env.LP = keep("weights_of_edges", [P, 2, CH * NH], F16)
                env.W1E = {e: keep("W1E" + e, [128, 2, D], F16) for e in "kv"}
                env.W2E = {e: keep("W2E" + e, [128, 2, KC, D], F16) for e in "kv"}
                env.G, env.BE = ({e: keep(n + e, [128, KC]) for e in "kv"} for n in ("edge_g", "edge_be"))
                node_tables(env, tab_w, L1, tab)
                left.close()
                edge_pass(env, "k", a["edge_attr_128"], tab, a["dst"], agg)
                env.retire("tab_")
                segment_exp(env, a["dst"])
                mix_w = mix_weights(env, left, a["L1_mix_W_qkv"], a["L1_mix_W_proj"], a["L1_mix_b_proj"], "left")
                edge_pass(env, "v", a["edge_attr_128"], tab, a["dst"], agg, mix_w)
            env.retire("edge_", "seg_")
            with ExitStack() as right:
                out_w = out_weights(env, right, L1)
                linear_attention(env, 1, mix_w, False, ahead=out_w)
                left.close()
                ffn_w = expert_weights(env, left, a["L1_ffn_Wr"], a["L1_ffn_W1"], None, a["L1_ffn_b1"], a["L1_ffn_W2"], a["L1_ffn_b2"],
                                       "left")
                node_output(env, out_w, agg, ffn_w)
            experts(env, 1, ffn_w, out)


def kernel(**inputs):
    import numpy as np
    import concourse.bacc as bacc
    from concourse.bass_utils import run_bass_kernel_spmd

    nc = bacc.Bacc("TRN2", target_bir_lowering=False, num_devices=1)
    arrays, args = {}, {}
    for name, value in inputs.items():
        value = np.asarray(value)
        if name in ("L1_mix_W_qkv", "L1_mix_W_proj"):
            value = value.T
        value = np.ascontiguousarray(value)
        arrays["in_" + name] = value
        args[name] = nc.dram_tensor("in_" + name, value.shape, mybir.dt.from_np(value.dtype), kind="ExternalInput").ap()
    out = nc.dram_tensor("out", (N, D), F32, kind="ExternalOutput").ap()
    build(nc, args, out)
    return run_bass_kernel_spmd(nc, [arrays], core_ids=[0]).results[0]["out"]
```
